# Optimizing a Trainium2 kernel written in Bass

```python
import numpy as np
import jax
import jax.numpy as jnp

def _softmax(x, axis=-1):
    return jax.nn.softmax(x, axis=axis)

def _gelu(x):
    return jax.nn.gelu(x, approximate=True)

def _silu(x):
    return jax.nn.silu(x)

def _sigmoid(x):
    return jax.nn.sigmoid(x)

def _layernorm(x, axis=-1, eps=1e-05):
    m = jnp.mean(x, axis=axis, keepdims=True)
    v = jnp.var(x, axis=axis, keepdims=True)
    return (x - m) / jnp.sqrt(v + eps)

def _scatter_add(tgt, idx, src, axis=0):
    return tgt.at[idx].add(src)

def _segment_sum(src, seg, n):
    return jax.ops.segment_sum(src, seg, n)
kernel_name = 'mk_lm_tower_d2_tok_ids512_r4_0073d5'

def setup_inputs(seed: int=0):
    np.random.seed(seed)
    _w = jnp.asarray

    def _rec_inputs():
        import jax
        import jax.numpy as jnp
        _rk = jax.random.key(seed)
        x = jax.random.randint(jax.random.fold_in(_rk, 1), (2, 2048), 0, 8000, jnp.int32)
        return x
    x = _rec_inputs()

    def _L0_tok_setup():
        import jax, jax.numpy as jnp
        import numpy as np
        VOCAB = 8000
        DIM = 128
        PAD_IDX = 0
        key = jax.random.key(seed)
        k_tok, k_w = jax.random.split(key)
        tensor = jax.random.randint(k_tok, (16, 512), 0, VOCAB, dtype=jnp.int64)
        weight = jax.random.normal(k_w, (VOCAB, DIM), dtype=jnp.float32)
        weight = weight.at[PAD_IDX].set(0.0)
        return {'tensor': tensor, 'weight': weight}
    _L0_tok_all = _L0_tok_setup()
    _L0_tok_in = {k: v for k, v in _L0_tok_all.items() if k in ('weight',)}
    del _L0_tok_all

    def _L0_attn_setup():
        import jax, jax.numpy as jnp
        import numpy as np
        import math
        EMB = 128
        HEADS = 8
        key = jax.random.key(seed)
        ks = jax.random.split(key, 9)
        s = 1.0 / math.sqrt(EMB)
        x = jax.random.normal(ks[0], (4, 512, EMB), dtype=jnp.float32)
        Wq = jax.random.uniform(ks[1], (EMB, EMB), jnp.float32, -s, s)
        bq = jax.random.uniform(ks[2], (EMB,), jnp.float32, -s, s)
        Wk = jax.random.uniform(ks[3], (EMB, EMB), jnp.float32, -s, s)
        bk = jax.random.uniform(ks[4], (EMB,), jnp.float32, -s, s)
        Wv = jax.random.uniform(ks[5], (EMB, EMB), jnp.float32, -s, s)
        bv = jax.random.uniform(ks[6], (EMB,), jnp.float32, -s, s)
        Wo = jax.random.uniform(ks[7], (EMB, EMB), jnp.float32, -s, s)
        bo = jax.random.uniform(ks[8], (EMB,), jnp.float32, -s, s)
        return {'x': x, 'Wq': Wq, 'bq': bq, 'Wk': Wk, 'bk': bk, 'Wv': Wv, 'bv': bv, 'Wo': Wo, 'bo': bo}
    _L0_attn_all = _L0_attn_setup()
    _L0_attn_in = {k: v for k, v in _L0_attn_all.items() if k in ('Wq', 'bq', 'Wk', 'bk', 'Wv', 'bv', 'Wo', 'bo')}
    del _L0_attn_all

    def _L0_ffn_setup():
        import jax, jax.numpy as jnp
        import numpy as np
        B, C, IN_LEN, OUT_LEN, E, TOP_K, N_I = (1, 2048, 128, 128, 8, 2, 16)
        key = jax.random.key(seed)
        ks = jax.random.split(key, 8)
        w = lambda k, shape, sc=0.02: jax.random.normal(k, shape, dtype=jnp.float32) * sc
        return {'x': jax.random.normal(ks[0], (B, C, IN_LEN), dtype=jnp.float32), 'Ins_tk': jax.random.normal(ks[1], (B, N_I, OUT_LEN), dtype=jnp.float32), 'gate_w': w(ks[2], (IN_LEN, E)), 'expert_w': w(ks[3], (E, IN_LEN, OUT_LEN)), 'expert_b': jnp.zeros((E, OUT_LEN), dtype=jnp.float32), 'gamma_w': w(ks[4], (E, OUT_LEN)), 'beta_w': w(ks[5], (E, OUT_LEN, OUT_LEN)), 'rmod_w': w(ks[6], (OUT_LEN, E))}
    _L0_ffn_all = _L0_ffn_setup()
    _L0_ffn_in = {k: v for k, v in _L0_ffn_all.items() if k in ('Ins_tk', 'gate_w', 'expert_w', 'expert_b', 'gamma_w', 'beta_w', 'rmod_w')}
    del _L0_ffn_all

    def _L1_attn_setup():
        import jax, jax.numpy as jnp
        import numpy as np
        N_HEADS = 8
        key = jax.random.key(seed)
        ks = jax.random.split(key, 5)
        b, s, d = (2, 1024, 128)
        return {'x': jax.random.normal(ks[0], (b, s, d), dtype=jnp.float32), 'qkv_w': jax.random.normal(ks[1], (3 * d, d), dtype=jnp.float32) * 0.02, 'qkv_b': jax.random.normal(ks[2], (3 * d,), dtype=jnp.float32) * 0.02, 'out_w': jax.random.normal(ks[3], (d, d), dtype=jnp.float32) * 0.02, 'out_b': jax.random.normal(ks[4], (d,), dtype=jnp.float32) * 0.02}
    _L1_attn_all = _L1_attn_setup()
    _L1_attn_in = {k: v for k, v in _L1_attn_all.items() if k in ('qkv_w', 'qkv_b', 'out_w', 'out_b')}
    del _L1_attn_all

    def _L1_ffn_setup():
        import jax, jax.numpy as jnp
        import numpy as np
        D = 128
        E = 8
        K = 2
        EXP = 4
        LN_EPS = 1e-05
        key = jax.random.key(seed)
        ks = jax.random.split(key, 8)
        B, T = (8, 512)
        Dh = D * EXP
        x = jax.random.normal(ks[0], (B, T, D), dtype=jnp.float32)
        ln_g = jnp.ones((D,), dtype=jnp.float32)
        ln_b = jnp.zeros((D,), dtype=jnp.float32)
        lim_r = np.sqrt(6.0 / (D + E)).astype(np.float32)
        w_r = jax.random.uniform(ks[1], (E, D), dtype=jnp.float32, minval=-lim_r, maxval=lim_r)
        b_r = jnp.zeros((E,), dtype=jnp.float32)
        lim1 = np.sqrt(6.0 / (D + Dh)).astype(np.float32)
        W1 = jax.random.uniform(ks[2], (E, D, Dh), dtype=jnp.float32, minval=-lim1, maxval=lim1)
        b1 = jnp.zeros((E, Dh), dtype=jnp.float32)
        W2 = jax.random.uniform(ks[3], (E, Dh, D), dtype=jnp.float32, minval=-lim1, maxval=lim1)
        b2 = jnp.zeros((E, D), dtype=jnp.float32)
        return {'x': x, 'ln_g': ln_g, 'ln_b': ln_b, 'w_r': w_r, 'b_r': b_r, 'W1': W1, 'b1': b1, 'W2': W2, 'b2': b2}
    _L1_ffn_all = _L1_ffn_setup()
    _L1_ffn_in = {k: v for k, v in _L1_ffn_all.items() if k in ('ln_g', 'ln_b', 'w_r', 'b_r', 'W1', 'b1', 'W2', 'b2')}
    del _L1_ffn_all
    return {'x': x, 'L0_tok_weight': _L0_tok_in['weight'], 'L0_attn_Wq': _L0_attn_in['Wq'], 'L0_attn_bq': _L0_attn_in['bq'], 'L0_attn_Wk': _L0_attn_in['Wk'], 'L0_attn_bk': _L0_attn_in['bk'], 'L0_attn_Wv': _L0_attn_in['Wv'], 'L0_attn_bv': _L0_attn_in['bv'], 'L0_attn_Wo': _L0_attn_in['Wo'], 'L0_attn_bo': _L0_attn_in['bo'], 'L0_ffn_Ins_tk': _L0_ffn_in['Ins_tk'], 'L0_ffn_gate_w': _L0_ffn_in['gate_w'], 'L0_ffn_expert_w': _L0_ffn_in['expert_w'], 'L0_ffn_expert_b': _L0_ffn_in['expert_b'], 'L0_ffn_gamma_w': _L0_ffn_in['gamma_w'], 'L0_ffn_beta_w': _L0_ffn_in['beta_w'], 'L0_ffn_rmod_w': _L0_ffn_in['rmod_w'], 'L1_attn_qkv_w': _L1_attn_in['qkv_w'], 'L1_attn_qkv_b': _L1_attn_in['qkv_b'], 'L1_attn_out_w': _L1_attn_in['out_w'], 'L1_attn_out_b': _L1_attn_in['out_b'], 'L1_ffn_ln_g': _L1_ffn_in['ln_g'], 'L1_ffn_ln_b': _L1_ffn_in['ln_b'], 'L1_ffn_w_r': _L1_ffn_in['w_r'], 'L1_ffn_b_r': _L1_ffn_in['b_r'], 'L1_ffn_W1': _L1_ffn_in['W1'], 'L1_ffn_b1': _L1_ffn_in['b1'], 'L1_ffn_W2': _L1_ffn_in['W2'], 'L1_ffn_b2': _L1_ffn_in['b2']}

def reference(x, L0_tok_weight, L0_attn_Wq, L0_attn_bq, L0_attn_Wk, L0_attn_bk, L0_attn_Wv, L0_attn_bv, L0_attn_Wo, L0_attn_bo, L0_ffn_Ins_tk, L0_ffn_gate_w, L0_ffn_expert_w, L0_ffn_expert_b, L0_ffn_gamma_w, L0_ffn_beta_w, L0_ffn_rmod_w, L1_attn_qkv_w, L1_attn_qkv_b, L1_attn_out_w, L1_attn_out_b, L1_ffn_ln_g, L1_ffn_ln_b, L1_ffn_w_r, L1_ffn_b_r, L1_ffn_W1, L1_ffn_b1, L1_ffn_W2, L1_ffn_b2):
    import jax
    import jax.numpy as jnp

    def _L0_tok_ref(tensor, weight):
        import jax, jax.numpy as jnp
        import numpy as np
        VOCAB = 8000
        DIM = 128
        PAD_IDX = 0
        return jnp.take(weight, tensor, axis=0)

    def _L0_attn_ref(x, Wq, bq, Wk, bk, Wv, bv, Wo, bo):
        import jax, jax.numpy as jnp
        import numpy as np
        import math
        EMB = 128
        HEADS = 8
        b, n, e = x.shape
        h = HEADS
        d = e // h

        def split_heads(t):
            return t.reshape(b, n, h, d).transpose(0, 2, 1, 3)
        q = split_heads(x @ Wq + bq)
        k = split_heads(x @ Wk + bk)
        v = split_heads(x @ Wv + bv)
        energy = jnp.einsum('bhqd,bhkd->bhqk', q, k)
        att = jax.nn.softmax(energy / jnp.sqrt(jnp.float32(e)), axis=-1)
        out = jnp.einsum('bhqk,bhkd->bhqd', att, v)
        out = out.transpose(0, 2, 1, 3).reshape(b, n, e)
        return out @ Wo + bo

    def _L0_ffn_ref(x, Ins_tk, gate_w, expert_w, expert_b, gamma_w, beta_w, rmod_w):
        import jax, jax.numpy as jnp
        import numpy as np
        B, C, IN_LEN, OUT_LEN, E, TOP_K, N_I = (1, 2048, 128, 128, 8, 2, 16)
        Bx, Cx, L = x.shape
        xf = x.reshape(-1, L)
        ins = Ins_tk[0]
        router_gamma = jnp.mean(ins @ rmod_w, axis=0)
        logits = xf @ gate_w + router_gamma
        probs = jax.nn.softmax(logits.astype(jnp.float32), axis=-1)
        rw, sel = jax.lax.top_k(probs, TOP_K)
        combine = jnp.sum(jax.nn.one_hot(sel, E, dtype=rw.dtype) * rw[..., None], axis=1)
        gam = jnp.mean(ins @ gamma_w.T, axis=0)
        bet = jnp.einsum('nh,ehd->ed', ins, beta_w) / N_I
        eo = jnp.einsum('nl,eld->end', xf, expert_w) + expert_b[:, None, :]
        mod = gam[:, None, None] * eo + bet[:, None, :]
        out = jnp.einsum('ne,end->nd', combine, mod)
        return out.reshape(Bx, Cx, OUT_LEN)

    def _L1_attn_ref(x, qkv_w, qkv_b, out_w, out_b):
        import jax, jax.numpy as jnp
        import numpy as np
        N_HEADS = 8
        b, s, d = x.shape
        h = N_HEADS
        c = d // h
        factor = 1.0 / jnp.sqrt(jnp.asarray(c, dtype=x.dtype))
        qkv = x @ qkv_w.T + qkv_b
        qkv = qkv.reshape(b, s, h, 3, c)
        q, k, v = (qkv[..., 0, :], qkv[..., 1, :], qkv[..., 2, :])
        scores = jnp.einsum('bshc,bthc->bhst', q, k) * factor
        attn = jax.nn.softmax(scores, axis=-1)
        ctx = jnp.einsum('bhst,bthc->bshc', attn, v).reshape(b, s, d)
        return ctx @ out_w.T + out_b

    def _L1_ffn_ref(x, ln_g, ln_b, w_r, b_r, W1, b1, W2, b2):
        import jax, jax.numpy as jnp
        import numpy as np
        D = 128
        E = 8
        K = 2
        EXP = 4
        LN_EPS = 1e-05
        B, T, d = x.shape
        mu = jnp.mean(x, axis=-1, keepdims=True)
        var = jnp.mean(jnp.square(x - mu), axis=-1, keepdims=True)
        h = (x - mu) * jax.lax.rsqrt(var + LN_EPS) * ln_g + ln_b
        logits = jnp.einsum('btd,ed->bte', h, w_r) + b_r
        topk_vals, topk_idx = jax.lax.top_k(logits, K)
        gates = jax.nn.softmax(topk_vals, axis=-1)
        hf = h.reshape(B * T, d)
        hid = jax.nn.gelu(jnp.einsum('nd,edf->nef', hf, W1) + b1, approximate=False)
        expert_stack = jnp.einsum('nef,efd->ned', hid, W2) + b2
        idx_flat = topk_idx.reshape(B * T, K)
        gates_flat = gates.reshape(B * T, K)
        gathered = jnp.take_along_axis(expert_stack, idx_flat[:, :, None], axis=1)
        mixed = jnp.sum(gathered * gates_flat[:, :, None], axis=1).reshape(B, T, d)
        return x + mixed
    h = _L0_tok_ref(x, L0_tok_weight)
    h = h + _L0_attn_ref(_layernorm(h, axis=-1), L0_attn_Wq, L0_attn_bq, L0_attn_Wk, L0_attn_bk, L0_attn_Wv, L0_attn_bv, L0_attn_Wo, L0_attn_bo)
    h = h + _L0_ffn_ref(_layernorm(h, axis=-1), L0_ffn_Ins_tk, L0_ffn_gate_w, L0_ffn_expert_w, L0_ffn_expert_b, L0_ffn_gamma_w, L0_ffn_beta_w, L0_ffn_rmod_w)
    h = h + _L1_attn_ref(_layernorm(h, axis=-1), L1_attn_qkv_w, L1_attn_qkv_b, L1_attn_out_w, L1_attn_out_b)
    h = h + _L1_ffn_ref(_layernorm(h, axis=-1), L1_ffn_ln_g, L1_ffn_ln_b, L1_ffn_w_r, L1_ffn_b_r, L1_ffn_W1, L1_ffn_b1, L1_ffn_W2, L1_ffn_b2)
    return h

_drawn_inputs = setup_inputs


def setup_inputs(seed=0):
    import zlib

    import numpy as np

    out = dict(_drawn_inputs(seed))
    spreads = {'L0_ffn_expert_b': (0.0, 0.8),
     'L1_ffn_ln_g': (1.0, 0.2),
     'L1_ffn_ln_b': (0.0, 0.1),
     'L1_ffn_b_r': (0.0, 0.3),
     'L1_ffn_b1': (0.0, 0.372),
     'L1_ffn_b2': (0.0, 0.295)}
    factors = {'L0_attn_Wq': 7.18,
     'L0_attn_bq': 8.0,
     'L0_attn_Wk': 7.448,
     'L0_attn_bk': 64.0,
     'L0_attn_Wv': 3.779,
     'L0_ffn_Ins_tk': 2.827,
     'L0_ffn_gate_w': 3.349,
     'L0_ffn_expert_w': 7.304,
     'L0_ffn_gamma_w': 8.0,
     'L0_ffn_beta_w': 3.058,
     'L0_ffn_rmod_w': 6.139,
     'L1_attn_qkv_w': 7.578,
     'L1_attn_qkv_b': 7.038,
     'L1_attn_out_w': 5.431,
     'L1_attn_out_b': 4.014}
    for name, (base, spread) in spreads.items():
        noise = np.random.default_rng([zlib.crc32(name.encode()), seed]).standard_normal(out[name].shape)
        drawn = base * np.exp(spread * noise) if base else spread * noise
        out[name] = jnp.asarray(drawn.astype(out[name].dtype))
    for name, factor in factors.items():
        out[name] = (out[name] * factor).astype(out[name].dtype)
    return out
```

```python
from contextlib import ExitStack

import concourse.bass as bass
from concourse import mybir

ALU = mybir.AluOpType
ACT = mybir.ActivationFunctionType
AX = mybir.AxisListType
F32 = mybir.dt.float32
BF16 = mybir.dt.bfloat16
I32 = mybir.dt.int32

P = 128
BATCH = 2
SEQ = 2048
D = 128
HEADS = 8
DH = D // HEADS
TILES = BATCH * SEQ // P
BH = BATCH * HEADS
SEQ_TILES = SEQ // P
N = 512
CHUNKS = BATCH * SEQ // N
PER = N // P
E = 8
FF = 512
FC = FF // P
EPS = 1e-5
BIG = 3e38
SCALES = (float(D) ** -0.5, float(DH) ** -0.5)
PARTS = 3
Q_PART = (0, 0, 0, 1, 1, 2)
K_PART = (0, 1, 2, 0, 1, 0)
SLOTS = len(Q_PART)
SROWS = SLOTS * DH
MROW = SROWS


class Kit:

    def __init__(self, nc, ctx):
        self.nc, self.ctx = nc, ctx

    def sbuf(self, name, shape, dt=F32):
        return self.ctx.enter_context(self.nc.sbuf_tensor(name, shape, dt))

    def sem(self, name):
        return self.ctx.enter_context(self.nc.semaphore(name))


def embed(nc, k, ids_dram, table, h, ident):
    ids = k.sbuf("ids", [P, TILES], I32)
    ids_in, rows_in, blank = k.sem("ids_in"), k.sem("rows_in"), k.sem("blank")
    with nc.Block() as block:

        @block.gpsimd
        def _(pool):
            pool.dma_start(ids[:, :], ids_dram[:, :]).then_inc(ids_in, 16)
            pool.memset(ident[:, :], 0.0).then_inc(blank, 1)
            pool.wait_ge(blank, 1)
            pool.affine_select(out=ident[:, :], in_=ident[:, :], compare_op=ALU.not_equal, fill=1.0,
                               base=0, pattern=[[-1, P]], channel_multiplier=1).then_inc(blank, 1)
            pool.wait_ge(ids_in, 16)
            for t in range(TILES):
                pool.indirect_dma_start(h[:, t, :], None, table[:, :],
                                        bass.IndirectOffsetOnAxis(ap=ids[:, t:t + 1], axis=0)).then_inc(rows_in, 16)
            pool.wait_ge(rows_in, 16 * TILES)


def layer_norm(nc, k, tag, src, dst, banks, ident, xT=None, gain=None, bias=None):
    G = 8
    groups = TILES // G
    stats, mv, std, rstd = k.stats, k.mv, k.std, k.rstd
    stats_done, moments, var_ready = k.sem(tag + "stats"), k.sem(tag + "moments"), k.sem(tag + "var")
    std_ready, rstd_ready, normed = k.sem(tag + "std"), k.sem(tag + "rstd"), k.sem(tag + "normed")
    turned, copied = k.sem(tag + "turned"), k.sem(tag + "copied")
    with nc.Block() as block:

        @block.vector
        def _(dve):
            def moments_of(g):
                for t in range(g * G, g * G + G):
                    dve.bn_stats(stats[:, t, :], src[:, t, :]).then_inc(stats_done, 1)
                dve.wait_ge(stats_done, (g + 1) * G)
                for t in range(g * G, g * G + G):
                    dve.bn_aggr(mv[:, t, :], stats[:, t, :]).then_inc(moments, 1)
                dve.wait_ge(moments, (g + 1) * G)
                s = slice(g * G, g * G + G)
                dve.tensor_scalar(std[:, s], mv[:, s, 1], EPS, None, ALU.add).then_inc(var_ready, 1)

            moments_of(0)
            for g in range(groups):
                if g + 1 < groups:
                    moments_of(g + 1)
                s = slice(g * G, g * G + G)
                dve.wait_ge(std_ready, g + 1)
                dve.reciprocal(rstd[:, s], std[:, s]).then_inc(rstd_ready, 1)
                dve.wait_ge(rstd_ready, g + 1)
                for t in range(g * G, g * G + G):
                    dve.tensor_scalar(dst[:, t, :], src[:, t, :], mv[:, t, 0:1], rstd[:, t:t + 1],
                                      ALU.subtract, ALU.mult).then_inc(normed, 1)

        @block.scalar
        def _(act):
            for g in range(groups):
                s = slice(g * G, g * G + G)
                act.wait_ge(var_ready, g + 1)
                act.activation(std[:, s], std[:, s], ACT.Sqrt).then_inc(std_ready, 1)
            for c in range(CHUNKS if xT is not None else 0):
                act.wait_ge(turned, c + 1)
                out = xT[:, c * N:(c + 1) * N]
                if gain is None:
                    act.activation(out, banks[:, c % 4, :], ACT.Copy).then_inc(copied, 1)
                else:
                    act.activation(out, banks[:, c % 4, :], ACT.Identity, bias=bias, scale=gain).then_inc(copied, 1)

        @block.tensor
        def _(pe):
            for c in range(CHUNKS if xT is not None else 0):
                pe.wait_ge(normed, (c + 1) * PER)
                if c >= 4:
                    pe.wait_ge(copied, c - 3)
                for j in range(PER):
                    mm = pe.transpose(banks[:, c % 4, j * P:(j + 1) * P], dst[:, c * PER + j, :], ident[:, :])
                mm.then_inc(turned, 1)


def project_qkv(nc, k, tag, xT, w, b, bv_row, parts_dram, v_all, banks, part_ring, rest_ring):
    R = 4
    made, first_cut, rest, second_cut = k.sem(tag + "made"), k.sem(tag + "cut1"), k.sem(tag + "rest"), k.sem(tag + "cut2")
    third_cut, v_taken = k.sem(tag + "cut3"), k.sem(tag + "v_taken")
    stored = [k.sem(tag + f"stored{s}") for s in range(R)]

    def bank(c, which):
        return banks[:, (c % 2) * 3 + which, :]

    with nc.Block() as block:

        @block.tensor
        def _(pe):
            for c in range(CHUNKS):
                x = xT[:, c * N:(c + 1) * N]
                if c >= 2:
                    pe.wait_ge(rest, 2 * (c - 1))
                for which in range(2):
                    pe.matmul(bank(c, which), w[:, which, :], x, start=True, stop=True).then_inc(made, 1)
                if c >= 2:
                    pe.wait_ge(v_taken, c - 1)
                for j in range(PER):
                    mm = pe.matmul(bank(c, 2)[:, j * P:(j + 1) * P], xT[:, c * N + j * P:c * N + (j + 1) * P],
                                   w[:, 2, :], start=True, stop=True)
                mm.then_inc(made, 1)

        @block.scalar
        def _(act):
            def first(m):
                c, which = m // 2, m % 2
                if m >= R:
                    act.wait_ge(stored[m % R], 16 * (m // R))
                act.wait_ge(made, 3 * c + which + 1)
                act.activation(part_ring[:, m % R, 0, :], bank(c, which), ACT.Identity,
                               bias=b[:, which:which + 1]).then_inc(first_cut, 1)

            first(0)
            for m in range(2 * CHUNKS):
                if m + 1 < 2 * CHUNKS:
                    first(m + 1)
                act.wait_ge(rest, m + 1)
                act.activation(part_ring[:, m % R, 1, :], rest_ring[:, m % R, :], ACT.Copy).then_inc(second_cut, 1)

        @block.vector
        def _(dve):
            def third(m):
                dve.wait_ge(second_cut, m + 1)
                dve.tensor_tensor(part_ring[:, m % R, 2, :], rest_ring[:, m % R, :], part_ring[:, m % R, 1, :],
                                  ALU.subtract).then_inc(third_cut, 1)

            for m in range(2 * CHUNKS):
                c, which = m // 2, m % 2
                dve.wait_ge(first_cut, m + 1)
                dve.scalar_tensor_tensor(rest_ring[:, m % R, :], bank(c, which), b[:, which:which + 1],
                                         part_ring[:, m % R, 0, :], ALU.add, ALU.subtract).then_inc(rest, 1)
                if m >= 1:
                    third(m - 1)
                if which == 1:
                    bi, t0 = c * PER // SEQ_TILES, c * PER % SEQ_TILES
                    dve.wait_ge(made, 3 * c + 3)
                    for j in range(PER):
                        vt = dve.tensor_tensor(
                            v_all[:, bi * HEADS:(bi + 1) * HEADS, t0 + j, :],
                            bank(c, 2)[:, j * P:(j + 1) * P].rearrange("p (h d) -> p h d", d=DH),
                            bv_row[:, :].rearrange("p (h d) -> p h d", d=DH), ALU.add)
                    vt.then_inc(v_taken, 1)
            third(2 * CHUNKS - 1)

        @block.sync
        def _(sp):
            for m in range(2 * CHUNKS):
                c, which = m // 2, m % 2
                bi, col = c * N // SEQ, c * N % SEQ
                sp.wait_ge(third_cut, m + 1)
                sp.dma_start(parts_dram[which, :, bi * P:(bi + 1) * P, col:col + N].rearrange("s p n -> p s n"),
                             part_ring[:, m % R, :, :]).then_inc(stored[m % R], 16)
            for s in range(R):
                sp.wait_ge(stored[s], 16 * (2 * CHUNKS // R))


def attention(nc, k, tag, scale, parts_dram, q_st, k_st, v_all, v_st, probs, o_sb, attn, h, bo_row, banks, ident):
    U = 4
    G = SEQ_TILES
    PV_LEAD, RING = 2, 2
    ST_LEAD = PV_LEAD + RING
    S_LEAD = ST_LEAD + G + 5
    NST, NS, SETS = 2, 4, 4
    ORDER = (("ST", 0), ("ST", 1), ("S", 0), ("S", 1), ("S", 2), ("S", 3), ("ST", 2), ("ST", 3))
    STEPS = SETS * G
    LOOPS = BH // SETS - 1
    TOTAL = BH * G
    st_bank, s_bank, o_bank = 0, NST, NST + NS

    made = [k.sem(tag + f"stack_in{s}") for s in range(SETS)]
    mrow_in = k.sem(tag + "mrow_in")
    s_ready, s_used, mx_ready = k.sem(tag + "s_ready"), k.sem(tag + "s_used"), k.sem(tag + "mx_ready")
    m_cut, m_cut2, m_turned = k.sem(tag + "m_cut"), k.sem(tag + "m_cut2"), k.sem(tag + "m_turned")
    st_ready, exp_done, pv_done = k.sem(tag + "st_ready"), k.sem(tag + "exp_done"), k.sem(tag + "pv_done")
    v_ready, o_copied, o_turned = k.sem(tag + "v_ready"), k.sem(tag + "o_copied"), k.sem(tag + "o_turned")
    o_rec, o_free, primed, h_done = k.sem(tag + "o_rec"), k.sem(tag + "o_free"), k.sem(tag + "primed"), k.sem(tag + "h_done")
    mx, negm, mrest, mparts, mturn, rec = k.mx, k.negm, k.mrest, k.mparts, k.mturn, k.rec

    heads = attn[:, :, :].rearrange("p (b t) (h d) -> p b t h d", b=BATCH, h=HEADS)

    class At:

        def __init__(self, i, tau, lead):
            self.s = tau + lead
            self.g = i * STEPS + self.s
            self.n = i * SETS + self.s // G
            self.in_head = self.s % G

    def rounds(eng, body):
        with eng.Fori(0, LOOPS) as i:
            body(i, False)
        body(LOOPS, True)

    def live(at, last, lead):
        return not last or at.s < STEPS

    with nc.Block() as block:

        @block.sync
        def _(sp):
            def load(n, s):
                for rows, order, which in ((q_st, Q_PART, 0), (k_st, K_PART, 1)):
                    for slot, part in enumerate(order):
                        sp.dma_start(rows[slot * DH:(slot + 1) * DH, s, :],
                                     parts_dram[which, part, bass.ds(n * DH, DH), :]).then_inc(made[s], 16)

            def mrows(n, s):
                sp.wait_ge(m_turned, n + 1)
                if isinstance(n, int) and n == 0:
                    pass
                else:
                    sp.wait_ge(mrow_in, n * 16 * 4 * PARTS)
                for a in range(4):
                    for part in range(PARTS):
                        sp.dma_start(
                            q_st[MROW + part:MROW + part + 1, s, :].rearrange("p (t a r) -> p t a r", a=4, r=32)[:, :, a, :],
                            mturn[32 * a:32 * a + SEQ_TILES, s % 2, 32 * part:32 * part + 32]).then_inc(mrow_in, 16)

            for s in range(SETS):
                load(s, s)
            mrows(0, 0)

            def body(i, last):
                for j in range(SETS):
                    n = i * SETS + j
                    if not (last and j == SETS - 1):
                        mrows(n + 1, (j + 1) % SETS)
                    if not last:
                        sp.wait_ge(st_ready, (n + 1) * G * U)
                        load(n + SETS, j)
            rounds(sp, body)

        @block.tensor
        def _(pe):
            def scores(at, u):
                s = at.s // G % SETS
                if u == 0 and at.in_head == 0:
                    pe.wait_ge(made[s], (at.n // SETS + 1 if isinstance(at.n, int) else at.n // SETS + 1) * 16 * 2 * SLOTS)
                bank = s_bank + u % NS
                if not (isinstance(at.g, int) and at.g * U + u < NS):
                    pe.wait_ge(s_used, at.g * U + (u - NS + 1))
                q, key = at.in_head, u
                pe.matmul(banks[:, bank, :], q_st[0:SROWS, s, q * P:(q + 1) * P],
                          k_st[0:SROWS, s, key * N:(key + 1) * N], start=True, stop=True).then_inc(s_ready, 1)

            def scores_t(at, u):
                s = at.s // G % SETS
                if u == 0 and at.in_head == 0:
                    pe.wait_ge(mrow_in, (at.n + 1) * 16 * 4 * PARTS)
                bank = st_bank + u % NST
                if not (isinstance(at.g, int) and at.g * U + u < NST):
                    pe.wait_ge(exp_done, at.g * U + (u - NST + 1))
                pe.matmul(banks[:, bank, :], k_st[0:MROW + PARTS, s, at.in_head * P:(at.in_head + 1) * P],
                          q_st[0:MROW + PARTS, s, u * N:(u + 1) * N], start=True, stop=True).then_inc(st_ready, 1)

            def values(at):
                two = at.s // G % 2
                if at.in_head == 0:
                    pe.wait_ge(v_ready, at.n + 1)
                    pe.wait_ge(o_free, at.n + 1)
                pe.wait_ge(exp_done, (at.g + 1) * U)
                for u in range(U):
                    mm = pe.matmul(banks[32 * u:32 * u + 32, o_bank + two, :], v_st[:, two, at.in_head, :],
                                   probs[:, at.s % RING, u, :], start=at.in_head == 0, stop=at.in_head == G - 1)
                mm.then_inc(pv_done, 1)

            def turn(at):
                two = at.s // G % 2
                pe.wait_ge(o_copied, at.n + 1)
                for j in range(4):
                    mm = pe.transpose(banks[:, o_bank + two, j * P:(j + 1) * P], o_sb[:, two, j * P:(j + 1) * P], ident[:, :])
                mm.then_inc(o_turned, 1)

            pe.wait_ge(primed, 1)
            for g in range(S_LEAD):
                lead_st = g - (S_LEAD - ST_LEAD)
                lead_pv = g - (S_LEAD - PV_LEAD)
                if lead_pv >= 0:
                    values(At(0, lead_pv, 0))
                for stream, u in ORDER:
                    if stream == "S":
                        scores(At(0, g, 0), u)
                    elif lead_st >= 0:
                        scores_t(At(0, lead_st, 0), u)

            def body(i, last):
                for tau in range(STEPS):
                    fin, pv, st, s = (At(i, tau, lead) for lead in (0, PV_LEAD, ST_LEAD, S_LEAD))
                    if live(pv, last, PV_LEAD):
                        values(pv)
                    for stream, u in ORDER:
                        if stream == "ST" and live(st, last, ST_LEAD):
                            scores_t(st, u)
                        if stream == "S" and live(s, last, S_LEAD):
                            scores(s, u)
                    if fin.in_head == G - 1:
                        turn(fin)
            rounds(pe, body)

        @block.scalar
        def _(act):
            def exps(at):
                if not (isinstance(at.g, int) and at.g < RING):
                    act.wait_ge(pv_done, at.g - RING + 1)
                for u in range(U):
                    act.wait_ge(st_ready, at.g * U + u + 1)
                    act.activation(probs[:, at.s % RING, u, :], banks[:, st_bank + u % NST, :], ACT.Exp,
                                   scale=scale).then_inc(exp_done, 1)

            def copy_out(at):
                two = at.s // G % 2
                act.wait_ge(pv_done, (at.n + 1) * G)
                act.activation(o_sb[:, two, :], banks[:, o_bank + two, :], ACT.Copy).then_inc(o_copied, 1)

            for g in range(ST_LEAD):
                exps(At(0, g, 0))

            def body(i, last):
                for tau in range(STEPS):
                    fin, st = At(i, tau, 0), At(i, tau, ST_LEAD)
                    if live(st, last, ST_LEAD):
                        exps(st)
                    if fin.in_head == G - 1:
                        copy_out(fin)
            rounds(act, body)

        @block.vector
        def _(dve):
            def maxima(at):
                two = at.s // G % 2
                for u in range(U):
                    dve.wait_ge(s_ready, at.g * U + u + 1)
                    dve.tensor_reduce(mx[:, two, at.in_head, u:u + 1], banks[:, s_bank + u % NS, :], AX.X,
                                      ALU.max).then_inc(s_used, 1)

            def head_maximum(at):
                two = at.s // G % 2
                dve.wait_ge(s_used, (at.n + 1) * G * U)
                dve.tensor_reduce(negm[:, two, :], mx[:, two, :, :], AX.X, ALU.max, negate=True).then_inc(mx_ready, 1)

            def turn_maximum(at):
                two = at.s // G % 2
                dve.wait_ge(m_cut, 3 * (at.n + 1))
                if not (isinstance(at.n, int) and at.n < 2):
                    dve.wait_ge(mrow_in, (at.n - 1) * 16 * 4 * PARTS)
                dve.transpose(mturn[:, two, :], mparts[:, two, :, :].rearrange("p c t -> p (c t)")).then_inc(m_turned, 1)

            def divide(at):
                two = at.s // G % 2
                dve.wait_ge(o_turned, at.n + 1)
                view = banks[:, o_bank + two, :].rearrange("p (j c r) -> p c j r", j=4, c=4)
                dve.reciprocal(rec[:, two, :, :], view[:, :, :, DH]).then_inc(o_rec, 1)
                dve.wait_ge(o_rec, at.n + 1)
                for c in range(4):
                    out = heads[:, bass.ds(at.n // HEADS, 1), 4 * c:4 * c + 4, bass.ds(at.n % HEADS, 1), :].rearrange(
                        "p b t h d -> p (b t) (h d)")
                    d = dve.tensor_tensor(out, view[:, c, :, 0:DH],
                                          rec[:, two, c, :].unsqueeze(2).to_broadcast([P, 4, DH]), ALU.mult)
                d.then_inc(o_free, 1)

            dve.memset(k.nothing[:, :], 0.0)
            dve.memset(mparts[:, :, :, :], 0.0).then_inc(m_cut2, 1)
            dve.memset(k_st[MROW:MROW + PARTS, :, :], 1.0).then_inc(primed, 1)
            dve.memset(rec[:, :, :, :], 0.0).then_inc(o_free, 2)
            for g in range(S_LEAD):
                maxima(At(0, g, 0))
                if g % G == G - 1:
                    head_maximum(At(0, g, 0))
                if g % G == 0 and g >= G:
                    turn_maximum(At(0, g - G, 0))

            def body(i, last):
                for tau in range(STEPS):
                    fin, s = At(i, tau, 0), At(i, tau, S_LEAD)
                    if live(s, last, S_LEAD):
                        maxima(s)
                        if s.in_head == G - 1:
                            head_maximum(s)
                    before = At(i, tau, S_LEAD - 1)
                    if before.in_head == G - 1 and live(before, last, S_LEAD):
                        turn_maximum(before)
                    if fin.in_head == G - 1:
                        divide(fin)
            rounds(dve, body)

        @block.gpsimd
        def _(pool):
            def stage_v(n, two):
                src = v_all[:, bass.ds(n * SEQ_TILES, SEQ_TILES), :] if not isinstance(n, int) else \
                    v_all[:, n * SEQ_TILES:(n + 1) * SEQ_TILES, :]
                pool.wait_ge(h_done, 2)
                pool.tensor_copy(v_st[:, two, :, 0:DH], src).then_inc(v_ready, 1)

            def cut_maximum(n, two):
                pool.wait_ge(m_cut2, 1)
                pool.wait_ge(mx_ready, n + 1)
                if not (isinstance(n, int) and n < 2):
                    pool.wait_ge(m_turned, n - 1)
                nothing = k.nothing[:, :]
                part = [mparts[:, two, p, 0:SEQ_TILES] for p in range(PARTS)]
                pool.tensor_tensor(part[0], negm[:, two, :], nothing, ALU.add).then_inc(m_cut, 1)
                pool.wait_ge(m_cut, 3 * n + 1)
                pool.tensor_tensor(mrest[:, two, :], negm[:, two, :], part[0], ALU.subtract).then_inc(m_cut2, 1)
                pool.wait_ge(m_cut2, n + 2)
                pool.tensor_tensor(part[1], mrest[:, two, :], nothing, ALU.add).then_inc(m_cut, 1)
                pool.wait_ge(m_cut, 3 * n + 2)
                pool.tensor_tensor(part[2], mrest[:, two, :], part[1], ALU.subtract).then_inc(m_cut, 1)

            pool.memset(v_st[:, :, :, :], 0.0).then_inc(h_done, 1)
            pool.wait_ge(h_done, 1)
            pool.memset(v_st[:, :, :, DH:DH + 1], 1.0).then_inc(h_done, 1)
            stage_v(0, 0)
            stage_v(1, 1)
            for c in range(CHUNKS):
                x = h[:, c * PER:(c + 1) * PER, :]
                pool.tensor_tensor(x, x, bo_row[:, :].unsqueeze(1).to_broadcast([P, PER, P]), ALU.add).then_inc(h_done, 1)
            cut_maximum(0, 0)

            def body(i, last):
                for j in range(SETS):
                    n = i * SETS + j
                    if not (last and j == SETS - 1):
                        cut_maximum(n + 1, (j + 1) % 2)
                    if not (last and j >= SETS - 2):
                        pool.wait_ge(pv_done, (n + 1) * G)
                        stage_v(n + 2, j % 2)
            rounds(pool, body)


def project_out(nc, k, tag, attn, wo, h, banks, ident, turned_sb):
    turned, copied, made, added = k.sem(tag + "turned"), k.sem(tag + "copied"), k.sem(tag + "made"), k.sem(tag + "added")
    with nc.Block() as block:

        @block.tensor
        def _(pe):
            def turn(c):
                if c >= 2:
                    pe.wait_ge(copied, c - 1)
                for j in range(PER):
                    mm = pe.transpose(banks[:, c % 2, j * P:(j + 1) * P], attn[:, c * PER + j, :], ident[:, :])
                mm.then_inc(turned, 1)

            def mult(c):
                pe.wait_ge(copied, c + 1)
                if c >= 2:
                    pe.wait_ge(added, c - 1)
                for j in range(PER):
                    mm = pe.matmul(banks[:, 2 + c % 2, j * P:(j + 1) * P], turned_sb[:, c % 2, j * P:(j + 1) * P],
                                   wo, start=True, stop=True)
                mm.then_inc(made, 1)

            turn(0)
            for c in range(CHUNKS):
                if c + 1 < CHUNKS:
                    turn(c + 1)
                mult(c)

        @block.scalar
        def _(act):
            for c in range(CHUNKS):
                act.wait_ge(turned, c + 1)
                if c >= 2:
                    act.wait_ge(made, c - 1)
                act.activation(turned_sb[:, c % 2, :], banks[:, c % 2, :], ACT.Copy).then_inc(copied, 1)

        @block.vector
        def _(dve):
            for c in range(CHUNKS):
                dve.wait_ge(made, c + 1)
                x = h[:, c * PER:(c + 1) * PER, :]
                dve.tensor_tensor(x, banks[:, 2 + c % 2, :].rearrange("p (t d) -> p t d", t=PER), x,
                                  ALU.add).then_inc(added, 1)


def route(nc, k, tag, xT, w_router, offset_row, all_experts, banks, weights, ident, weights_t, prep=None):
    logits, shifted, ex, pick, score, sel1 = (k.route[:, i, :, :] for i in range(6))
    top, den = k.top[:, :], k.den[:, :]
    step, logit_ready, ex_ready = k.sem(tag + "step"), k.sem(tag + "logits"), k.sem(tag + "ex")
    shift_ready, w_ready, turned, copied = k.sem(tag + "shift"), k.sem(tag + "w"), k.sem(tag + "turned"), k.sem(tag + "copied")

    def wide(x):
        return x.unsqueeze(2).to_broadcast([P, TILES, E])

    with nc.Block() as block:

        @block.tensor
        def _(pe):
            for t in range(TILES):
                mm = pe.matmul(banks[:, 0, t * E:(t + 1) * E], xT[:, t * P:(t + 1) * P], w_router,
                               start=True, stop=True)
            mm.then_inc(logit_ready, 1)
            pe.wait_ge(w_ready, 1)
            for c in range(CHUNKS):
                if c >= 2:
                    pe.wait_ge(copied, c - 1)
                for j in range(PER):
                    mm = pe.transpose(banks[0:E, 1 + c % 2, j * P:(j + 1) * P], weights[:, c * PER + j, :], ident[:, :])
                mm.then_inc(turned, 1)

        @block.scalar
        def _(act):
            act.wait_ge(shift_ready, 1)
            act.activation(ex, shifted, ACT.Exp).then_inc(ex_ready, 1)
            for c in range(CHUNKS):
                act.wait_ge(turned, c + 1)
                act.activation(weights_t[:, c * N:(c + 1) * N], banks[0:E, 1 + c % 2, :], ACT.Copy).then_inc(copied, 1)

        @block.vector
        def _(dve):
            n = [0]

            def then(ins):
                n[0] += 1
                ins.then_inc(step, 1)
                dve.wait_ge(step, n[0])

            dve.wait_ge(logit_ready, 1)
            then(dve.tensor_tensor(logits, banks[:, 0, 0:TILES * E].rearrange("p (t e) -> p t e", e=E),
                                   offset_row.unsqueeze(1).to_broadcast([P, TILES, E]), ALU.add))
            then(dve.tensor_reduce(top, logits, AX.X, ALU.max))
            then(dve.tensor_tensor(shifted, logits, wide(top), ALU.subtract))
            dve.tensor_scalar(pick, shifted, 0.0, None, ALU.is_ge).then_inc(shift_ready, 1)
            dve.wait_ge(shift_ready, 1)
            rank = k.rank[:, :].unsqueeze(1).to_broadcast([P, TILES, E])
            then(dve.tensor_tensor(score, pick, rank, ALU.mult))
            then(dve.tensor_reduce(top, score, AX.X, ALU.max))
            then(dve.tensor_tensor(sel1, score, wide(top), ALU.is_equal))
            then(dve.scalar_tensor_tensor(logits, sel1, -BIG, shifted, ALU.mult, ALU.add))
            then(dve.tensor_reduce(top, logits, AX.X, ALU.max))
            then(dve.tensor_tensor(pick, logits, wide(top), ALU.is_equal))
            then(dve.tensor_tensor(score, pick, rank, ALU.mult))
            then(dve.tensor_reduce(top, score, AX.X, ALU.max))
            then(dve.tensor_tensor(pick, score, wide(top), ALU.is_equal))
            then(dve.tensor_tensor(sel1, sel1, pick, ALU.add))
            dve.wait_ge(ex_ready, 1)
            then(dve.tensor_tensor(score, sel1, ex, ALU.mult))
            then(dve.tensor_reduce(den, ex if all_experts else score, AX.X, ALU.add))
            then(dve.reciprocal(top, den))
            dve.tensor_tensor(weights[:, :, :], score, wide(top), ALU.mult).then_inc(w_ready, 1)


def mixture_constants(nc, k, ins, w16, expert_b, beta_w, banks):
    mean, mean_wide, mean_diag, sixteenth = k.ins_mean, k.mean_wide, k.mean_diag, k.sixteenth
    set_, mean_made, mean_out, wide_ready, made, done = (k.sem("c_" + s) for s in ("set", "mean", "mean_out", "wide", "made", "done"))
    with nc.Block() as block:

        @block.vector
        def _(dve):
            dve.memset(sixteenth[:, :], 1.0 / 16).then_inc(set_, 1)
            dve.memset(mean_diag[:, :, :], 0.0).then_inc(set_, 1)
            dve.memset(mean_wide[:, :], 1.0).then_inc(set_, 1)
            dve.wait_ge(mean_made, 1)
            dve.tensor_copy(mean[:, :], banks[:, 0, 0:1]).then_inc(mean_out, 1)
            dve.wait_ge(mean_out, 1)
            dve.wait_ge(set_, 3)
            dve.tensor_scalar(mean_wide[:, :], mean_wide[:, :], mean[:, :], None, ALU.mult).then_inc(wide_ready, 1)
            for e in range(E):
                dve.tensor_copy(mean_diag[:, e, e:e + 1], mean[:, :]).then_inc(wide_ready, 1)
            dve.wait_ge(made, 3)
            dve.tensor_copy(k.gamma_router[:, :], banks[:, 1, 0:2 * E]).then_inc(done, 1)
            dve.tensor_copy(k.gamma_col[:, :], banks[0:E, 2, 0:1]).then_inc(done, 1)
            dve.wait_ge(done, 2)
            dve.scalar_tensor_tensor(k.offsets[:, :], expert_b, k.gamma_col[:, :], banks[0:E, 3, 0:D],
                                     ALU.mult, ALU.add).then_inc(done, 1)

        @block.tensor
        def _(pe):
            pe.wait_ge(set_, 1)
            pe.matmul(banks[:, 0, 0:1], ins, sixteenth[:, :], start=True, stop=True).then_inc(mean_made, 1)
            pe.wait_ge(wide_ready, 1 + E)
            pe.matmul(banks[:, 1, 0:2 * E], mean_wide[:, :], w16, start=True, stop=True).then_inc(made, 1)
            pe.matmul(banks[0:E, 2, 0:1], w16[:, 0:E], mean[:, :], start=True, stop=True).then_inc(made, 1)
            for e in range(E):
                mm = pe.matmul(banks[0:E, 3, 0:D], mean_diag[:, e, :], beta_w[:, e, :], start=e == 0, stop=e == E - 1)
            mm.then_inc(made, 1)


def mix_linear(nc, k, xT, expert_w, comb, comb_t, offsets, h, banks):
    made, offset_made, off_done, taken, scaled = k.sem("l_made"), k.sem("l_offset"), k.sem("l_offdone"), k.sem("l_taken"), k.sem("l_scaled")
    cg = k.route[:, 0, :, :]
    with nc.Block() as block:

        @block.tensor
        def _(pe):
            for t in range(TILES):
                if t % PER == 0:
                    c = t // PER
                    if c >= 2:
                        pe.wait_ge(off_done, c - 1)
                    for j in range(PER):
                        mm = pe.matmul(banks[:, 6 + c % 2, j * P:(j + 1) * P], comb_t[:, (t + j) * P:(t + j + 1) * P],
                                       offsets, start=True, stop=True)
                    mm.then_inc(offset_made, 1)
                if t >= 3:
                    pe.wait_ge(taken, (t - 2) * E)
                for half in range(2):
                    mm = pe.matmul(banks[:, 2 * (t % 3) + half, :], xT[:, t * P:(t + 1) * P],
                                   expert_w[:, half * N:(half + 1) * N], start=True, stop=True)
                mm.then_inc(made, 1)

        @block.vector
        def _(dve):
            dve.tensor_tensor(cg, comb[:, :, :], k.gamma_router[:, 0:E].unsqueeze(1).to_broadcast([P, TILES, E]),
                              ALU.mult).then_inc(scaled, 1)
            dve.wait_ge(scaled, 1)
            for t in range(TILES):
                if t % PER == 0:
                    c = t // PER
                    dve.wait_ge(offset_made, c + 1)
                    x = h[:, t:t + PER, :]
                    dve.tensor_tensor(x, banks[:, 6 + c % 2, :].rearrange("p (t d) -> p t d", t=PER), x,
                                      ALU.add).then_inc(off_done, 1)
                    dve.wait_ge(off_done, c + 1)
                dve.wait_ge(made, t + 1)
                for e in range(E):
                    if e:
                        dve.wait_ge(taken, t * E + e)
                    dve.scalar_tensor_tensor(h[:, t, :], banks[:, 2 * (t % 3) + e // PER, (e % PER) * D:(e % PER + 1) * D],
                                             cg[:, t, e:e + 1], h[:, t, :], ALU.mult, ALU.add).then_inc(taken, 1)


def mix_mlp(nc, k, zT, w1, b1, w2, b2, gates, gates_t, y, h, out, banks, hid):
    base, up, act_done, down, taken, stored = (k.sem("m_" + s) for s in ("base", "up", "gelu", "down", "taken", "stored"))
    off_made, off_done = k.sem("m_offset"), k.sem("m_offdone")
    NUP = 3
    tokens = out.rearrange("b (t p) d -> p (b t) d", p=P)
    with nc.Block() as block:

        @block.gpsimd
        def _(pool):
            for c in range(CHUNKS):
                x = h[:, c * PER:(c + 1) * PER, :]
                pool.tensor_tensor(x, x, y[:, c * PER:(c + 1) * PER, :], ALU.add).then_inc(base, 1)

        @block.tensor
        def _(pe):
            for c in range(CHUNKS):
                if c >= 2:
                    pe.wait_ge(off_done, c - 1)
                for j in range(PER):
                    t = c * PER + j
                    mm = pe.matmul(banks[:, 6 + c % 2, j * P:(j + 1) * P], gates_t[:, t * P:(t + 1) * P], b2,
                                   start=True, stop=True)
                mm.then_inc(off_made, 1)

            def project_up(c, e):
                for f in range(FC):
                    u = e * FC + f
                    if not (isinstance(c, int) and u < NUP):
                        pe.wait_ge(act_done, c * E * FC + (u - NUP + 1))
                    rhs = zT[:, bass.ds(c * N, N)] if not isinstance(c, int) else zT[:, c * N:(c + 1) * N]
                    pe.matmul(banks[:, u % NUP, :], w1[:, e, f * P:(f + 1) * P], rhs, start=True, stop=True).then_inc(up, 1)

            def project_down(c, e):
                pe.wait_ge(act_done, c * E * FC + (e + 1) * FC)
                if not (isinstance(c, int) and e < 2):
                    pe.wait_ge(taken, (c * E + (e - 1)) * PER)
                for j in range(PER):
                    for f in range(FC):
                        mm = pe.matmul(banks[:, 4 + e % 2, j * P:(j + 1) * P], hid[:, e % 2, f, j * P:(j + 1) * P],
                                       w2[:, e, f, :], start=f == 0, stop=f == FC - 1)
                mm.then_inc(down, 1)

            def chunk(c):
                project_up(c, 0)
                for e in range(E):
                    if e + 1 < E:
                        project_up(c, e + 1)
                    project_down(c, e)

            chunk(0)
            with pe.Fori(1, CHUNKS) as c:
                chunk(c)

        @block.scalar
        def _(act):
            def chunk(c):
                for e in range(E):
                    if not (isinstance(c, int) and e < 2):
                        act.wait_ge(down, c * E + (e - 1))
                    for f in range(FC):
                        u = e * FC + f
                        act.wait_ge(up, c * E * FC + (u + 1))
                        act.activation(hid[:, e % 2, f, :], banks[:, u % NUP, :], ACT.Gelu,
                                       bias=b1[:, e, f:f + 1]).then_inc(act_done, 1)
            chunk(0)
            with act.Fori(1, CHUNKS) as c:
                chunk(c)

        @block.vector
        def _(dve):
            for c in range(CHUNKS):
                dve.wait_ge(base, c + 1)
                dve.wait_ge(off_made, c + 1)
                x = h[:, c * PER:(c + 1) * PER, :]
                dve.tensor_tensor(x, banks[:, 6 + c % 2, :].rearrange("p (t d) -> p t d", t=PER), x,
                                  ALU.add).then_inc(off_done, 1)
            dve.wait_ge(off_done, CHUNKS)

            def chunk(c):
                for e in range(E):
                    dve.wait_ge(down, c * E + (e + 1))
                    for j in range(PER):
                        if isinstance(c, int):
                            x, g = h[:, c * PER + j, :], gates[:, c * PER + j, e:e + 1]
                        else:
                            x = h[:, bass.ds(c * PER + j, 1), :].rearrange("p t d -> p (t d)")
                            g = gates[:, bass.ds(c * PER + j, 1), e:e + 1].rearrange("p t e -> p (t e)")
                        if e:
                            dve.wait_ge(taken, c * E * PER + ((e - 1) * PER + j + 1))
                        dve.scalar_tensor_tensor(x, banks[:, 4 + e % 2, j * P:(j + 1) * P], g, x,
                                                 ALU.mult, ALU.add).then_inc(taken, 1)
            chunk(0)
            with dve.Fori(1, CHUNKS) as c:
                chunk(c)

        @block.sync
        def _(sp):
            for c in range(CHUNKS):
                sp.wait_ge(taken, (c + 1) * E * PER)
                sp.dma_start(tokens[:, c * PER:(c + 1) * PER, :], h[:, c * PER:(c + 1) * PER, :]).then_inc(stored, 16)
            sp.wait_ge(stored, 16 * CHUNKS)


def program(nc, ids, table, attn_w, attn_b, bv, bo, ins, gate_w, expert_w, expert_b, gamma_rmod, beta_w,
            ln_gb, w_r, b_r, w1, b1, w2, b2, out):
    with ExitStack() as ctx:
        k = Kit(nc, ctx)
        h, y = k.sbuf("h", [P, TILES, D]), k.sbuf("y", [P, TILES, D])
        xT = k.sbuf("xT", [P, TILES * P])
        v_all, attn = k.sbuf("v_all", [P, BH * SEQ_TILES, DH]), k.sbuf("attn", [P, TILES, D])
        q_st, k_st = k.sbuf("q_st", [P, 4, SEQ], BF16), k.sbuf("k_st", [P, 4, SEQ], BF16)
        probs = k.sbuf("probs", [P, 2, 4, N])
        v_st, o_sb = k.sbuf("v_st", [P, 2, SEQ_TILES, 32]), k.sbuf("o_sb", [P, 2, N])
        ident = k.sbuf("ident", [P, P])
        k.stats, k.mv = k.sbuf("stats", [P, TILES, 6]), k.sbuf("mv", [P, TILES, 2])
        k.std, k.rstd = k.sbuf("std", [P, TILES]), k.sbuf("rstd", [P, TILES])
        k.mx, k.negm, k.mrest = k.sbuf("mx", [P, 2, SEQ_TILES, 4]), k.sbuf("negm", [P, 2, SEQ_TILES]), k.sbuf("mrest", [P, 2, SEQ_TILES])
        k.mparts, k.mturn = k.sbuf("mparts", [P, 2, PARTS, 32], BF16), k.sbuf("mturn", [P, 2, PARTS * 32], BF16)
        k.nothing = k.sbuf("nothing", [P, SEQ_TILES])
        k.rec = k.sbuf("rec", [P, 2, 4, 4])
        k.route = k.sbuf("route", [P, 6, TILES, E])
        k.top, k.den, k.rank = k.sbuf("top", [P, TILES]), k.sbuf("den", [P, TILES]), k.sbuf("rank", [P, E])
        weights = k.sbuf("weights", [P, TILES, E])
        w_sb, b_sb = k.sbuf("w_sb", [P, 2, 4, D]), k.sbuf("b_sb", [P, 2, 2])
        bv_row, bo_row = k.sbuf("bv_row", [P, 2, D]), k.sbuf("bo_row", [P, 2, D])
        ins_sb, w16 = k.sbuf("ins_sb", [16, D]), k.sbuf("w16", [P, 2 * E])
        router = k.sbuf("router", [P, 2, E])
        eb_sb, br_row, b2_sb = k.sbuf("eb_sb", [E, D]), k.sbuf("br_row", [P, E]), k.sbuf("b2_sb", [E, D])
        ln_sb, b1_sb = k.sbuf("ln_sb", [P, 2]), k.sbuf("b1_sb", [P, E, FC])
        k.ins_mean, k.mean_wide, k.mean_diag = k.sbuf("ins_mean", [P, 1]), k.sbuf("mean_wide", [P, P]), k.sbuf("mean_diag", [P, E, E])
        k.sixteenth, k.gamma_router = k.sbuf("sixteenth", [16, 1]), k.sbuf("gamma_router", [P, 2 * E])
        k.gamma_col, k.offsets = k.sbuf("gamma_col", [E, 1]), k.sbuf("offsets", [E, D])
        ew_sb = k.sbuf("ew_sb", [P, E * D])
        w1_sb, w2_sb = k.sbuf("w1_sb", [P, E, FF]), k.sbuf("w2_sb", [P, E, FC, D])
        banks = ctx.enter_context(nc.psum_tensor("banks", [P, 8, N], F32))
        parts_dram = nc.dram_tensor("qk_parts", [2, PARTS, BATCH * P, SEQ], BF16).ap()

        part_ring = k_st[:, 0:3, :].rearrange("p s n -> p (s n)").rearrange("p (r s n) -> p r s n", r=4, s=PARTS)
        rest_ring = probs[:, 0, :, :]
        beta_sb = probs[:, :, :, :].rearrange("p a b n -> p (a b n)")[:, 0:E * D].rearrange("p (e d) -> p e d", e=E)
        wt = attn[0:E, :, :].rearrange("p t d -> p (t d)")
        z = v_all[:, :, :].rearrange("p t d -> p (t d)").rearrange("p (t d) -> p t d", d=D)
        hid = q_st[:, :, :].rearrange("p s n -> p (s n)").bitcast(F32)
        loads = k.sem("loads")
        ranked = k.sem("ranked")

        with nc.Block() as block:
            @block.sync
            def _(sp):
                pairs = [(w_sb[:, :, :, :], attn_w), (b_sb[:, :, :], attn_b), (ins_sb[:, :], ins), (w16[:, :], gamma_rmod),
                         (router[:, 0, :], gate_w), (router[:, 1, :], w_r), (eb_sb[:, :], expert_b), (b2_sb[:, :], b2),
                         (br_row[:, :], b_r.partition_broadcast(P)), (ln_sb[:, :], ln_gb), (b1_sb[:, :, :], b1),
                         (ew_sb[:, :], expert_w), (w1_sb[:, :, :], w1), (w2_sb[:, :, :, :], w2)]
                for l in range(2):
                    pairs += [(bv_row[:, l, :], bv[l].partition_broadcast(P)), (bo_row[:, l, :], bo[l].partition_broadcast(P))]
                for dst, src in pairs:
                    sp.dma_start(dst, src).then_inc(loads, 16)
                sp.wait_ge(loads, 16 * len(pairs))

            @block.vector
            def _(dve):
                for e in range(E):
                    dve.memset(k.rank[:, e:e + 1], float(E - e)).then_inc(ranked, 1)

        embed(nc, k, ids, table, h, ident)
        for l in range(2):
            tag = f"a{l}_"
            layer_norm(nc, k, tag + "n", h, y, banks, ident, xT)
            project_qkv(nc, k, tag + "p", xT, w_sb[:, l], b_sb[:, l], bv_row[:, l], parts_dram,
                        v_all[:, :, :].rearrange("p (b t) d -> p b t d", b=BH), banks, part_ring, rest_ring)
            attention(nc, k, tag, SCALES[l], parts_dram, q_st, k_st, v_all, v_st, probs, o_sb, attn, h,
                      bo_row[:, l], banks, ident)
            project_out(nc, k, tag + "o", attn, w_sb[:, l, 3, :], h, banks, ident, o_sb)
            if l == 0:
                layer_norm(nc, k, "f0_n", h, y, banks, ident, xT)
                beta_in = k.sem("beta_in")
                with nc.Block() as block:
                    @block.sync
                    def _(sp):
                        sp.dma_start(beta_sb, beta_w).then_inc(beta_in, 16)
                        sp.wait_ge(beta_in, 16)
                mixture_constants(nc, k, ins_sb[:, :], w16[:, :], eb_sb[:, :], beta_sb, banks)
                route(nc, k, "f0_r", xT, router[:, 0, :], k.gamma_router[:, E:2 * E], True, banks, weights, ident, wt)
                mix_linear(nc, k, xT, ew_sb, weights, wt, k.offsets[:, :], h, banks)
        layer_norm(nc, k, "f1_n", h, y, banks, ident)
        layer_norm(nc, k, "f1_m", y, z, banks, ident, xT, gain=ln_sb[:, 0:1], bias=ln_sb[:, 1:2])
        route(nc, k, "f1_r", xT, router[:, 1, :], br_row[:, :], False, banks, weights, ident, wt)
        mix_mlp(nc, k, xT, w1_sb, b1_sb, w2_sb, b2_sb[:, :], weights, wt, y, h, out, banks,
                hid.rearrange("p (s f n) -> p s f n", s=2, f=FC))


def kernel(**inputs):
    import numpy as np
    import concourse.bacc as bacc
    from concourse.bass_utils import run_bass_kernel_spmd as run

    a = {name: np.asarray(x) for name, x in inputs.items()}
    qkv = a["L1_attn_qkv_w"].reshape(HEADS, 3, DH, D).transpose(1, 3, 0, 2).reshape(3, D, D)
    qkv_b = a["L1_attn_qkv_b"].reshape(HEADS, 3, DH).transpose(1, 0, 2).reshape(3, D)
    mats = [[a["L0_attn_Wq"], a["L0_attn_Wk"], a["L0_attn_Wv"], a["L0_attn_Wo"]],
            [qkv[0], qkv[1], qkv[2], a["L1_attn_out_w"].T]]
    arrays = {
        "ids": a["x"].reshape(TILES, P).T,
        "table": a["L0_tok_weight"],
        "attn_w": np.array(mats).transpose(2, 0, 1, 3),
        "attn_b": np.array([[a["L0_attn_bq"], a["L0_attn_bk"]], [qkv_b[0], qkv_b[1]]]).transpose(2, 0, 1),
        "bv": np.array([a["L0_attn_bv"], qkv_b[2]]),
        "bo": np.array([a["L0_attn_bo"], a["L1_attn_out_b"]]),
        "ins": a["L0_ffn_Ins_tk"][0],
        "gate_w": a["L0_ffn_gate_w"],
        "expert_w": a["L0_ffn_expert_w"].transpose(1, 0, 2).reshape(D, E * D),
        "expert_b": a["L0_ffn_expert_b"],
        "gamma_rmod": np.concatenate([a["L0_ffn_gamma_w"].T, a["L0_ffn_rmod_w"]], axis=1),
        "beta_w": a["L0_ffn_beta_w"].transpose(1, 0, 2),
        "ln_gb": np.array([a["L1_ffn_ln_g"], a["L1_ffn_ln_b"]]).T,
        "w_r": a["L1_ffn_w_r"].T,
        "b_r": a["L1_ffn_b_r"],
        "w1": a["L1_ffn_W1"].transpose(1, 0, 2),
        "b1": a["L1_ffn_b1"].reshape(E, FC, P).transpose(2, 0, 1),
        "w2": a["L1_ffn_W2"].reshape(E, FC, P, D).transpose(2, 0, 1, 3),
        "b2": a["L1_ffn_b2"],
    }
    nc = bacc.Bacc("TRN2", target_bir_lowering=False, num_devices=1)
    feed, aps = {}, []
    for name, x in arrays.items():
        x = np.ascontiguousarray(x)
        feed[f"in_{name}"] = x
        aps.append(nc.dram_tensor(f"in_{name}", x.shape, mybir.dt.from_np(x.dtype), kind="ExternalInput").ap())
    out = nc.dram_tensor("out", (BATCH, SEQ, D), F32, kind="ExternalOutput").ap()
    program(nc, *aps, out)
    return run(nc, [feed], core_ids=[0]).results[0]["out"]
```

```python
from contextlib import ExitStack

import concourse.bass as bass
from concourse import mybir

ALU = mybir.AluOpType
ACT = mybir.ActivationFunctionType
AX = mybir.AxisListType
F32 = mybir.dt.float32
BF16 = mybir.dt.bfloat16
I32 = mybir.dt.int32

P = 128
BATCH = 2
SEQ = 2048
D = 128
HEADS = 8
DH = D // HEADS
TILES = BATCH * SEQ // P
BH = BATCH * HEADS
SEQ_TILES = SEQ // P
N = 512
CHUNKS = BATCH * SEQ // N
PER = N // P
E = 8
FF = 512
FC = FF // P
EPS = 1e-5
TOKENS = BATCH * SEQ
BEST = 2
ROWS = 2 * P
SORTED_TILES = (BEST * TOKENS - E) // ROWS + E
PER_PART = SORTED_TILES * ROWS // P
COUNT_STEPS = TOKENS // ROWS
BIG = 3e38
SCALES = (float(D) ** -0.5, float(DH) ** -0.5)
PARTS = 3
Q_PART = (0, 0, 0, 1, 1, 2)
K_PART = (0, 1, 2, 0, 1, 0)
SLOTS = len(Q_PART)
SROWS = SLOTS * DH
MROW = SROWS


class Kit:

    def __init__(self, nc, ctx):
        self.nc, self.ctx = nc, ctx
        self.phase, self.cleared = [], []

    def sbuf(self, name, shape, dt=F32):
        return self.ctx.enter_context(self.nc.sbuf_tensor(name, shape, dt))

    def lasting_sem(self, name):
        return self.ctx.enter_context(self.nc.semaphore(name))

    def sem(self, name):
        sem = self.nc.alloc_semaphore(name=name)
        self.phase.append(sem)
        return sem

    def end_phase(self):
        for sem in self.cleared:
            self.nc.release_semaphore(sem)
        for sem in self.phase:
            self.nc.gpsimd.sem_clear(sem)
        self.phase, self.cleared = [], self.phase


def gather(pool, k, ids_dram, table, h, ident, rows_in):
    pool.dma_start(k.ids[:, :], ids_dram[:, :]).then_inc(k.ids_in, 16)
    pool.memset(ident[:, :], 0.0).then_inc(k.blank, 1)
    pool.wait_ge(k.blank, 1)
    pool.affine_select(out=ident[:, :], in_=ident[:, :], compare_op=ALU.not_equal, fill=1.0,
                       base=0, pattern=[[-1, P]], channel_multiplier=1).then_inc(k.blank, 1)
    pool.wait_ge(k.ids_in, 16)
    for t in range(TILES):
        pool.indirect_dma_start(h[:, t, :], None, table[:, :],
                                bass.IndirectOffsetOnAxis(ap=k.ids[:, t:t + 1], axis=0)).then_inc(rows_in[t // LN_GROUP], 16)


LN_GROUP = 8


def layer_norm(nc, k, tag, src, dst, banks, ident, xT=None, gain=None, bias=None, rows_in=None,
               at_start=None, router=None):
    G = LN_GROUP
    groups = TILES // G
    stats, mv, std, rstd, shift = k.stats, k.mv, k.std, k.rstd, k.shift
    stats_done, moments, var_ready = k.sem(tag + "stats"), k.sem(tag + "moments"), k.sem(tag + "var")
    std_ready, rstd_ready, shift_ready = k.sem(tag + "std"), k.sem(tag + "rstd"), k.sem(tag + "shift")
    turned, copied = k.sem(tag + "turned"), k.sem(tag + "copied")
    by_pool, by_act = k.sem(tag + "by_pool"), k.sem(tag + "by_act")
    pool_tiles = [] if rows_in is not None else list(range(0, TILES, 2))
    act_tiles = [t for t in range(TILES) if t not in pool_tiles]
    at_start = at_start or {}
    with nc.Block() as block:

        @block.vector
        def _(dve):
            if "vector" in at_start:
                at_start["vector"](dve)

            def moments_of(g):
                if rows_in is not None:
                    dve.wait_ge(rows_in[g], 16 * G)
                for t in range(g * G, g * G + G):
                    dve.bn_stats(stats[:, t, :], src[:, t, :]).then_inc(stats_done, 1)
                dve.wait_ge(stats_done, (g + 1) * G)
                for t in range(g * G, g * G + G):
                    dve.bn_aggr(mv[:, t, :], stats[:, t, :]).then_inc(moments, 1)
                dve.wait_ge(moments, (g + 1) * G)
                s = slice(g * G, g * G + G)
                dve.tensor_scalar(std[:, s], mv[:, s, 1], EPS, None, ALU.add).then_inc(var_ready, 1)

            def scales_of(g):
                s = slice(g * G, g * G + G)
                dve.wait_ge(std_ready, g + 1)
                dve.reciprocal(rstd[:, s], std[:, s]).then_inc(rstd_ready, 1)
                dve.wait_ge(rstd_ready, g + 1)
                dve.scalar_tensor_tensor(shift[:, s], mv[:, s, 0], -1.0, rstd[:, s], ALU.mult,
                                         ALU.mult).then_inc(shift_ready, 1)

            for g in range(groups):
                moments_of(g)
                if g:
                    scales_of(g - 1)
            scales_of(groups - 1)

        @block.gpsimd
        def _(pool):
            if "gpsimd" in at_start:
                at_start["gpsimd"](pool)
            for t in pool_tiles:
                pool.wait_ge(shift_ready, t // G + 1)
                pool.tensor_scalar(dst[:, t, :], src[:, t, :], rstd[:, t:t + 1], shift[:, t:t + 1],
                                   ALU.mult, ALU.add).then_inc(by_pool, 1)

        @block.scalar
        def _(act):
            def root(g):
                s = slice(g * G, g * G + G)
                act.wait_ge(var_ready, g + 1)
                act.activation(std[:, s], std[:, s], ACT.Sqrt).then_inc(std_ready, 1)

            def copies(g):
                for c in range(g * G // PER, (g + 1) * G // PER if xT is not None else 0):
                    act.wait_ge(turned, c + 1)
                    out = xT[:, c * N:(c + 1) * N]
                    if gain is None:
                        act.activation(out, banks[:, c % 4, :], ACT.Copy).then_inc(copied, 1)
                    else:
                        act.activation(out, banks[:, c % 4, :], ACT.Identity, bias=bias, scale=gain).then_inc(copied, 1)

            root(0)
            for g in range(groups):
                if g + 1 < groups:
                    root(g + 1)
                act.wait_ge(shift_ready, g + 1)
                for t in act_tiles:
                    if t // G == g:
                        act.activation(dst[:, t, :], src[:, t, :], ACT.Identity, bias=shift[:, t:t + 1],
                                       scale=rstd[:, t:t + 1]).then_inc(by_act, 1)
                if g:
                    copies(g - 1)
            copies(groups - 1)

        @block.tensor
        def _(pe):
            if "tensor" in at_start:
                at_start["tensor"](pe)
            if rows_in is not None:
                pe.wait_ge(k.blank, 2)

            def logits(c):
                pe.wait_ge(copied, c + 1)
                for t in range(c * PER, (c + 1) * PER):
                    pe.matmul(banks[:, 4, t * E:(t + 1) * E], xT[:, t * P:(t + 1) * P], router, start=True, stop=True)

            for c in range(CHUNKS if xT is not None else 0):
                for done, tiles in ((by_pool, pool_tiles), (by_act, act_tiles)):
                    if tiles:
                        pe.wait_ge(done, sum(t < (c + 1) * PER for t in tiles))
                if c >= 4:
                    pe.wait_ge(copied, c - 3)
                for j in range(PER):
                    mm = pe.transpose(banks[:, c % 4, j * P:(j + 1) * P], dst[:, c * PER + j, :], ident[:, :])
                mm.then_inc(turned, 1)
                if router is not None and c >= 2:
                    logits(c - 2)
            if router is not None:
                logits(CHUNKS - 2)
                logits(CHUNKS - 1)

        @block.sync
        def _(sp):
            if "sync" in at_start:
                at_start["sync"](sp)


def project_qkv(nc, k, tag, xT, w, b, bv_row, parts_dram, v_all, banks, part_ring, rest_ring, load_stacks):
    R = 4
    PER_BATCH = 2 * CHUNKS // BATCH
    made, first_cut, rest, second_cut = k.sem(tag + "made"), k.sem(tag + "cut1"), k.sem(tag + "rest"), k.sem(tag + "cut2")
    third_cut, v_taken = k.sem(tag + "cut3"), k.sem(tag + "v_taken")
    stored = k.parts_stored
    assert CHUNKS // BATCH * 2 % R == 0

    def bank(c, which):
        return banks[:, (c % 2) * 3 + which, :]

    with nc.Block() as block:

        @block.tensor
        def _(pe):
            for c in range(CHUNKS):
                x = xT[:, c * N:(c + 1) * N]
                if c >= 2:
                    pe.wait_ge(rest, 2 * (c - 1))
                for which in range(2):
                    pe.matmul(bank(c, which), w[:, which, :], x, start=True, stop=True).then_inc(made, 1)
                if c >= 2:
                    pe.wait_ge(v_taken, c - 1)
                for j in range(PER):
                    mm = pe.matmul(bank(c, 2)[:, j * P:(j + 1) * P], xT[:, c * N + j * P:c * N + (j + 1) * P],
                                   w[:, 2, :], start=True, stop=True)
                mm.then_inc(made, 1)

        @block.scalar
        def _(act):
            def first(m):
                c, which = m // 2, m % 2
                if m >= R:
                    act.wait_ge(stored[(m - R) // PER_BATCH][m % R], 16 * ((m - R) % PER_BATCH // R + 1 + k.layer * (PER_BATCH // R)))
                act.wait_ge(made, 3 * c + which + 1)
                act.activation(part_ring[:, m % R, 0, :], bank(c, which), ACT.Identity,
                               bias=b[:, which:which + 1]).then_inc(first_cut, 1)

            if k.layer:
                act.wait_ge(k.slots_blank, 16)
            first(0)
            for m in range(2 * CHUNKS):
                if m + 1 < 2 * CHUNKS:
                    first(m + 1)
                act.wait_ge(rest, m + 1)
                act.activation(part_ring[:, m % R, 1, :], rest_ring[:, m % R, :], ACT.Copy).then_inc(second_cut, 1)

        @block.vector
        def _(dve):
            def third(m):
                dve.wait_ge(second_cut, m + 1)
                dve.tensor_tensor(part_ring[:, m % R, 2, :], rest_ring[:, m % R, :], part_ring[:, m % R, 1, :],
                                  ALU.subtract).then_inc(third_cut, 1)

            for m in range(2 * CHUNKS):
                c, which = m // 2, m % 2
                dve.wait_ge(first_cut, m + 1)
                dve.scalar_tensor_tensor(rest_ring[:, m % R, :], bank(c, which), b[:, which:which + 1],
                                         part_ring[:, m % R, 0, :], ALU.add, ALU.subtract).then_inc(rest, 1)
                if m >= 1:
                    third(m - 1)
                if which == 1:
                    bi, t0 = c * PER // SEQ_TILES, c * PER % SEQ_TILES
                    dve.wait_ge(made, 3 * c + 3)
                    for j in range(PER):
                        vt = dve.tensor_tensor(
                            v_all[:, bi * HEADS:(bi + 1) * HEADS, t0 + j, :],
                            bank(c, 2)[:, j * P:(j + 1) * P].rearrange("p (h d) -> p h d", d=DH),
                            bv_row[:, :].rearrange("p (h d) -> p h d", d=DH), ALU.add)
                    vt.then_inc(v_taken, 1)
            third(2 * CHUNKS - 1)

        @block.sync
        def _(sp):
            for m in range(2 * CHUNKS):
                c, which = m // 2, m % 2
                bi, col = c * N // SEQ, c * N % SEQ
                sp.wait_ge(third_cut, m + 1)
                sp.dma_start(parts_dram[which, :, bi * P:(bi + 1) * P, col:col + N].rearrange("s p n -> p s n"),
                             part_ring[:, m % R, :, :]).then_inc(stored[bi][m % R], 16)
                if m == PER_BATCH + 3:
                    for s in range(R):
                        sp.wait_ge(stored[0][s], 16 * PER_BATCH // R * (k.layer + 1))
                    load_stacks(sp, 0, 0)


def stack_loader(k, parts_dram, q_st, k_st):
    def load_stacks(sp, n, s):
        for rows, order, which in ((q_st, Q_PART, 0), (k_st, K_PART, 1)):
            for slot, part in enumerate(order):
                sp.dma_start(rows[slot * DH:(slot + 1) * DH, s, :],
                             parts_dram[which, part, bass.ds(n * DH, DH), :]).then_inc(k.stack_in[s], 16)
    return load_stacks


def attention(nc, k, tag, scale, parts_dram, q_st, k_st, v_all, v_st, probs, o_sb, attn, h, bo_row, banks, ident, m_dram, load_stacks):
    U = 4
    G = SEQ_TILES
    PV_LEAD, RING = 1, 2
    ST_LEAD = PV_LEAD + RING
    S_LEAD = ST_LEAD + G + 4
    NST, NS, SETS = 2, 4, 4
    ORDER = (("ST", 0), ("ST", 1), ("S", 0), ("S", 1), ("S", 2), ("S", 3), ("ST", 2), ("ST", 3))
    STEPS = SETS * G
    LOOPS = BH // SETS - 1
    TOTAL = BH * G
    st_bank, s_bank, o_bank = 0, NST, NST + NS

    made = k.stack_in
    before = k.layer * (BH // SETS)
    mrow_in, m_out = k.sem(tag + "mrow_in"), k.sem(tag + "m_out")
    s_ready, s_used, mx_ready = k.sem(tag + "s_ready"), k.sem(tag + "s_used"), k.sem(tag + "mx_ready")
    m_cut, m_cut2, m_turned = k.sem(tag + "m_cut"), k.sem(tag + "m_cut2"), k.sem(tag + "m_turned")
    st_ready, exp_done, pv_done = k.sem(tag + "st_ready"), k.sem(tag + "exp_done"), k.sem(tag + "pv_done")
    v_ready, o_copied, o_turned = k.sem(tag + "v_ready"), k.sem(tag + "o_copied"), k.sem(tag + "o_turned")
    o_rec, o_free, primed, h_done = k.sem(tag + "o_rec"), k.sem(tag + "o_free"), k.sem(tag + "primed"), k.sem(tag + "h_done")
    mx, negm, mrest, mparts, mturn, rec = k.mx, k.negm, k.mrest, k.mparts, k.mturn, k.rec

    heads = attn[:, :, :].rearrange("p (b t) (h d) -> p b t h d", b=BATCH, h=HEADS)

    class At:

        def __init__(self, i, tau, lead):
            self.s = tau + lead
            self.g = i * STEPS + self.s
            self.n = i * SETS + self.s // G
            self.in_head = self.s % G

    def rounds(eng, body):
        with eng.Fori(0, LOOPS) as i:
            body(i, False)
        body(LOOPS, True)

    def live(at, last, lead):
        return not last or at.s < STEPS

    def st_place(at, u):
        tail = at.g - (TOTAL - S_LEAD + ST_LEAD) if isinstance(at.g, int) else -1
        if tail < 0:
            return st_bank + u % NST, NST
        return st_bank + u, U if tail else (NST, NST, None, None)[u]

    with nc.Block() as block:

        @block.sync
        def _(sp):
            def mrows(n, s):
                sp.wait_ge(m_turned, n + 1)
                sp.dma_start(m_dram[s % 2], mturn[:, s % 2, :]).then_inc(m_out, 16)
                sp.wait_ge(m_out, (n + 1) * 16)
                rows = m_dram[s % 2].rearrange("(a t) (c r) -> c t a r", a=4, r=32)
                for a in range(4):
                    sp.dma_start(q_st[MROW:MROW + PARTS, s, :].rearrange("p (t a r) -> p t a r", a=4, r=32)[:, :, a, :],
                                 rows[:, 0:SEQ_TILES, a, :]).then_inc(mrow_in, 16)

            for s in range(1, SETS):
                load_stacks(sp, s, s)
            mrows(0, 0)
            for s in range(4):
                sp.wait_ge(k.parts_stored[BATCH - 1][s], 16 * (k.layer + 1) * (2 * CHUNKS // BATCH // 4))

            def body(i, last):
                for j in range(SETS):
                    n = i * SETS + j
                    if not (last and j == SETS - 1):
                        mrows(n + 1, (j + 1) % SETS)
                    if not last:
                        sp.wait_ge(st_ready, (n + 1) * G * U)
                        load_stacks(sp, n + SETS, j)
            rounds(sp, body)

        @block.tensor
        def _(pe):
            def scores(at, u):
                s = at.s // G % SETS
                if u == 0 and at.in_head == 0:
                    pe.wait_ge(made[s], (at.n // SETS + (1 + before)) * 16 * 2 * SLOTS)
                bank = s_bank + u % NS
                if not (isinstance(at.g, int) and at.g * U + u < NS):
                    pe.wait_ge(s_used, at.g * U + (u - NS + 1))
                q, key = at.in_head, u
                pe.matmul(banks[:, bank, :], q_st[0:SROWS, s, q * P:(q + 1) * P],
                          k_st[0:SROWS, s, key * N:(key + 1) * N], start=True, stop=True).then_inc(s_ready, 1)

            def scores_t(at, u):
                s = at.s // G % SETS
                if u == 0 and at.in_head == 0:
                    pe.wait_ge(mrow_in, (at.n + 1) * 16 * 4)
                bank, ago = st_place(at, u)
                if ago is None:
                    pe.wait_ge(s_used, TOTAL * U)
                elif not (isinstance(at.g, int) and at.g * U + u < ago):
                    pe.wait_ge(exp_done, at.g * U + (u - ago + 1))
                pe.matmul(banks[:, bank, :], k_st[0:MROW + PARTS, s, at.in_head * P:(at.in_head + 1) * P],
                          q_st[0:MROW + PARTS, s, u * N:(u + 1) * N], start=True, stop=True).then_inc(st_ready, 1)

            def values(at):
                two = at.s // G % 2
                if at.in_head == 0:
                    pe.wait_ge(v_ready, at.n + 1)
                    pe.wait_ge(o_free, at.n + 1)
                pe.wait_ge(exp_done, (at.g + 1) * U)
                for u in range(U):
                    mm = pe.matmul(banks[32 * u:32 * u + 32, o_bank + two, :], v_st[:, two, at.in_head, :],
                                   probs[:, at.s % RING, u, :], start=at.in_head == 0, stop=at.in_head == G - 1)
                mm.then_inc(pv_done, 1)

            def turn(at):
                two = at.s // G % 2
                pe.wait_ge(o_copied, at.n + 1)
                for j in range(4):
                    mm = pe.transpose(banks[:, o_bank + two, j * P:(j + 1) * P], o_sb[:, two, j * P:(j + 1) * P], ident[:, :])
                mm.then_inc(o_turned, 1)

            pe.wait_ge(primed, 1)
            for g in range(S_LEAD):
                lead_st = g - (S_LEAD - ST_LEAD)
                lead_pv = g - (S_LEAD - PV_LEAD)
                if lead_pv >= 0:
                    values(At(0, lead_pv, 0))
                for stream, u in ORDER:
                    if stream == "S":
                        scores(At(0, g, 0), u)
                    elif lead_st >= 0:
                        scores_t(At(0, lead_st, 0), u)

            def body(i, last):
                for tau in range(STEPS):
                    fin, pv, st, s = (At(i, tau, lead) for lead in (0, PV_LEAD, ST_LEAD, S_LEAD))
                    if live(pv, last, PV_LEAD):
                        values(pv)
                    for stream, u in ORDER:
                        if stream == "ST" and live(st, last, ST_LEAD):
                            scores_t(st, u)
                        if stream == "S" and live(s, last, S_LEAD):
                            scores(s, u)
                    if fin.in_head == G - 1:
                        turn(fin)
            rounds(pe, body)

        @block.scalar
        def _(act):
            def exps(at):
                if not (isinstance(at.g, int) and at.g < RING):
                    act.wait_ge(pv_done, at.g - RING + 1)
                for u in range(U):
                    act.wait_ge(st_ready, at.g * U + u + 1)
                    act.activation(probs[:, at.s % RING, u, :], banks[:, st_place(at, u)[0], :], ACT.Exp,
                                   scale=scale).then_inc(exp_done, 1)

            def copy_out(at):
                two = at.s // G % 2
                act.wait_ge(pv_done, (at.n + 1) * G)
                act.activation(o_sb[:, two, :], banks[:, o_bank + two, :], ACT.Copy).then_inc(o_copied, 1)

            for g in range(ST_LEAD):
                exps(At(0, g, 0))

            def body(i, last):
                for tau in range(STEPS):
                    fin, st = At(i, tau, 0), At(i, tau, ST_LEAD)
                    if fin.in_head == G - 1:
                        copy_out(fin)
                    if live(st, last, ST_LEAD):
                        exps(st)
            rounds(act, body)

        @block.vector
        def _(dve):
            def maxima(at):
                two = at.s // G % 2
                for u in range(0, U, 2):
                    dve.wait_ge(s_ready, at.g * U + u + 2)
                    pair = banks[:, s_bank + u:s_bank + u + 2, :].rearrange("p b n -> p (b n)")
                    dve.tensor_reduce(mx[:, two, at.in_head, u // 2:u // 2 + 1], pair, AX.X, ALU.max).then_inc(s_used, 2)

            def head_maximum(at):
                two = at.s // G % 2
                dve.wait_ge(s_used, (at.n + 1) * G * U)
                dve.tensor_reduce(negm[:, two, :], mx[:, two, :, :], AX.X, ALU.max, negate=True).then_inc(mx_ready, 1)

            def turn_maximum(at):
                two = at.s // G % 2
                dve.wait_ge(m_cut, 3 * (at.n + 1))
                if not (isinstance(at.n, int) and at.n < 2):
                    dve.wait_ge(m_out, (at.n - 1) * 16)
                dve.transpose(mturn[:, two, :], mparts[:, two, :, :].rearrange("p c t -> p (c t)")).then_inc(m_turned, 1)

            def divide(at):
                two = at.s // G % 2
                dve.wait_ge(o_turned, at.n + 1)
                view = banks[:, o_bank + two, :].rearrange("p (j c r) -> p c j r", j=4, c=4)
                dve.reciprocal(rec[:, two, :, :], view[:, :, :, DH]).then_inc(o_rec, 1)
                dve.wait_ge(o_rec, at.n + 1)
                for c in range(4):
                    out = heads[:, bass.ds(at.n // HEADS, 1), 4 * c:4 * c + 4, bass.ds(at.n % HEADS, 1), :].rearrange(
                        "p b t h d -> p (b t) (h d)")
                    d = dve.tensor_tensor(out, view[:, c, :, 0:DH],
                                          rec[:, two, c, :].unsqueeze(2).to_broadcast([P, 4, DH]), ALU.mult)
                d.then_inc(o_free, 1)

            dve.memset(k.nothing[:, :], 0.0)
            dve.memset(mparts[:, :, :, :], 0.0).then_inc(m_cut2, 1)
            dve.memset(k_st[MROW:MROW + PARTS, :, :], 1.0).then_inc(primed, 1)
            dve.memset(rec[:, :, :, :], 0.0).then_inc(o_free, 2)
            for g in range(S_LEAD):
                maxima(At(0, g, 0))
                if g % G == G - 1:
                    head_maximum(At(0, g, 0))
                if g % G == 0 and g >= G:
                    turn_maximum(At(0, g - G, 0))

            def body(i, last):
                for tau in range(STEPS):
                    fin, s = At(i, tau, 0), At(i, tau, S_LEAD)
                    if live(s, last, S_LEAD):
                        maxima(s)
                        if s.in_head == G - 1:
                            head_maximum(s)
                    before = At(i, tau, S_LEAD - 1)
                    if before.in_head == G - 1 and live(before, last, S_LEAD):
                        turn_maximum(before)
                    if fin.in_head == G - 1:
                        divide(fin)
            rounds(dve, body)

        @block.gpsimd
        def _(pool):
            def stage_v(n, two):
                src = v_all[:, bass.ds(n * SEQ_TILES, SEQ_TILES), :] if not isinstance(n, int) else \
                    v_all[:, n * SEQ_TILES:(n + 1) * SEQ_TILES, :]
                pool.wait_ge(h_done, 2)
                pool.tensor_copy(v_st[:, two, :, 0:DH], src).then_inc(v_ready, 1)

            def cut_maximum(n, two):
                pool.wait_ge(m_cut2, 1)
                pool.wait_ge(mx_ready, n + 1)
                if not (isinstance(n, int) and n < 2):
                    pool.wait_ge(m_turned, n - 1)
                nothing = k.nothing[:, :]
                part = [mparts[:, two, p, 0:SEQ_TILES] for p in range(PARTS)]
                pool.tensor_tensor(part[0], negm[:, two, :], nothing, ALU.add).then_inc(m_cut, 1)
                pool.wait_ge(m_cut, 3 * n + 1)
                pool.tensor_tensor(mrest[:, two, :], negm[:, two, :], part[0], ALU.subtract).then_inc(m_cut2, 1)
                pool.wait_ge(m_cut2, n + 2)
                pool.tensor_tensor(part[1], mrest[:, two, :], nothing, ALU.add).then_inc(m_cut, 1)
                pool.wait_ge(m_cut, 3 * n + 2)
                pool.tensor_tensor(part[2], mrest[:, two, :], part[1], ALU.subtract).then_inc(m_cut, 1)

            pool.memset(v_st[:, :, :, :], 0.0).then_inc(h_done, 1)
            pool.wait_ge(h_done, 1)
            pool.memset(v_st[:, :, :, DH:DH + 1], 1.0).then_inc(h_done, 1)
            stage_v(0, 0)
            stage_v(1, 1)
            for c in range(CHUNKS):
                x = h[:, c * PER:(c + 1) * PER, :]
                pool.tensor_tensor(x, x, bo_row[:, :].unsqueeze(1).to_broadcast([P, PER, P]), ALU.add).then_inc(h_done, 1)
            cut_maximum(0, 0)

            def body(i, last):
                for j in range(SETS):
                    n = i * SETS + j
                    if not (last and j == SETS - 1):
                        cut_maximum(n + 1, (j + 1) % 2)
                    if not (last and j >= SETS - 2):
                        pool.wait_ge(pv_done, (n + 1) * G)
                        stage_v(n + 2, j % 2)
            rounds(pool, body)


def project_out(nc, k, tag, attn, wo, h, banks, ident, turned_sb):
    turned, copied, made, added = k.sem(tag + "turned"), k.sem(tag + "copied"), k.sem(tag + "made"), k.sem(tag + "added")
    with nc.Block() as block:

        @block.tensor
        def _(pe):
            def turn(c):
                if c >= 2:
                    pe.wait_ge(copied, c - 1)
                for j in range(PER):
                    mm = pe.transpose(banks[:, c % 2, j * P:(j + 1) * P], attn[:, c * PER + j, :], ident[:, :])
                mm.then_inc(turned, 1)

            def mult(c):
                pe.wait_ge(copied, c + 1)
                if c >= 2:
                    pe.wait_ge(added, c - 1)
                for j in range(PER):
                    mm = pe.matmul(banks[:, 2 + c % 2, j * P:(j + 1) * P], turned_sb[:, c % 2, j * P:(j + 1) * P],
                                   wo, start=True, stop=True)
                mm.then_inc(made, 1)

            turn(0)
            for c in range(CHUNKS):
                if c + 1 < CHUNKS:
                    turn(c + 1)
                mult(c)

        @block.scalar
        def _(act):
            for c in range(CHUNKS):
                act.wait_ge(turned, c + 1)
                if c >= 2:
                    act.wait_ge(made, c - 1)
                act.activation(turned_sb[:, c % 2, :], banks[:, c % 2, :], ACT.Copy).then_inc(copied, 1)

        @block.vector
        def _(dve):
            for c in range(CHUNKS):
                dve.wait_ge(made, c + 1)
                x = h[:, c * PER:(c + 1) * PER, :]
                dve.tensor_tensor(x, banks[:, 2 + c % 2, :].rearrange("p (t d) -> p t d", t=PER), x,
                                  ALU.add).then_inc(added, 1)


def route(nc, k, tag, offset_row, all_experts, banks, weights, ident, weights_t, blank_slots=None):
    logits, shifted, ex, pick, score, sel1 = (k.route[:, i, :, :] for i in range(6))
    both = logits
    top, den = k.top[:, :], k.den[:, :]
    step, ex_ready = k.sem(tag + "step"), k.sem(tag + "ex")
    shift_ready, w_ready, turned, copied = k.sem(tag + "shift"), k.sem(tag + "w"), k.sem(tag + "turned"), k.sem(tag + "copied")

    def wide(x):
        return x.unsqueeze(2).to_broadcast([P, TILES, E])

    with nc.Block() as block:

        @block.tensor
        def _(pe):
            if weights_t is not None:
                pe.wait_ge(w_ready, 1)
            for c in range(CHUNKS if weights_t is not None else 0):
                if c >= 2:
                    pe.wait_ge(copied, c - 1)
                for j in range(PER):
                    mm = pe.transpose(banks[0:E, 1 + c % 2, j * P:(j + 1) * P], weights[:, c * PER + j, :], ident[:, :])
                mm.then_inc(turned, 1)

        @block.scalar
        def _(act):
            act.wait_ge(shift_ready, 1)
            act.activation(ex, shifted, ACT.Exp).then_inc(ex_ready, 1)
            for c in range(CHUNKS if weights_t is not None else 0):
                act.wait_ge(turned, c + 1)
                act.activation(weights_t[:, c * N:(c + 1) * N], banks[0:E, 1 + c % 2, :], ACT.Copy).then_inc(copied, 1)

        @block.vector
        def _(dve):
            n = [0]

            def then(ins):
                n[0] += 1
                ins.then_inc(step, 1)
                dve.wait_ge(step, n[0])

            then(dve.tensor_tensor(logits, banks[:, 4, 0:TILES * E].rearrange("p (t e) -> p t e", e=E),
                                   offset_row.unsqueeze(1).to_broadcast([P, TILES, E]), ALU.add))
            then(dve.tensor_reduce(top, logits, AX.X, ALU.max))
            then(dve.tensor_tensor(shifted, logits, wide(top), ALU.subtract))
            dve.tensor_scalar(pick, shifted, 0.0, None, ALU.is_ge).then_inc(shift_ready, 1)
            dve.wait_ge(shift_ready, 1)
            rank = k.rank[:, :].unsqueeze(1).to_broadcast([P, TILES, E])
            then(dve.tensor_tensor(score, pick, rank, ALU.mult))
            then(dve.tensor_reduce(top, score, AX.X, ALU.max))
            then(dve.tensor_tensor(sel1, score, wide(top), ALU.is_equal))
            then(dve.scalar_tensor_tensor(logits, sel1, -BIG, shifted, ALU.mult, ALU.add))
            then(dve.tensor_reduce(top, logits, AX.X, ALU.max))
            then(dve.tensor_tensor(pick, logits, wide(top), ALU.is_equal))
            then(dve.tensor_tensor(score, pick, rank, ALU.mult))
            then(dve.tensor_reduce(top, score, AX.X, ALU.max))
            then(dve.tensor_tensor(pick, score, wide(top), ALU.is_equal))
            then(dve.tensor_tensor(both, sel1, pick, ALU.add))
            dve.wait_ge(ex_ready, 1)
            then(dve.tensor_tensor(score, both, ex, ALU.mult))
            then(dve.tensor_reduce(den, ex if all_experts else score, AX.X, ALU.add))
            then(dve.reciprocal(top, den))
            dve.tensor_tensor(weights[:, :, :], score, wide(top), ALU.mult).then_inc(w_ready, 1)

        if blank_slots is not None:
            slots_dram, rows_sb = blank_slots
            zeroed = k.sem(tag + "zeroed")

            @block.gpsimd
            def _(pool):
                pool.memset(rows_sb[:, :, :], 0.0).then_inc(zeroed, 1)
                pool.wait_ge(zeroed, 1)
                pool.tensor_copy(rows_sb[:, :, D:D + 1], k.pad_dst.unsqueeze(2)).then_inc(zeroed, 1)

            @block.sync
            def _(sp):
                sp.wait_ge(zeroed, 2)
                sp.dma_start(slots_dram.rearrange("(p j) c -> p j c", p=P), rows_sb[:, :, :]).then_inc(k.slots_blank, 16)


def mixture_constants(k, ins, w16, expert_b, beta_w, banks, loaded):
    mean, mean_wide, mean_diag, sixteenth = k.ins_mean, k.mean_wide, k.mean_diag, k.sixteenth
    set_, mean_made, mean_out, wide_ready, made, done = (k.sem("c_" + s) for s in ("set", "mean", "mean_out", "wide", "made", "done"))

    def vector(dve):
        dve.memset(sixteenth[:, :], 1.0 / 16).then_inc(set_, 1)
        dve.memset(mean_diag[:, :, :], 0.0).then_inc(set_, 1)
        dve.memset(mean_wide[:, :], 1.0).then_inc(set_, 1)
        for e in range(E):
            dve.memset(k.rank[:, e:e + 1], float(E - e))
        dve.memset(k.ones[:, :], 1.0)
        dve.wait_ge(mean_made, 1)
        dve.tensor_copy(mean[:, :], banks[:, 4, 0:1]).then_inc(mean_out, 1)
        dve.wait_ge(mean_out, 1)
        dve.wait_ge(set_, 3)
        dve.tensor_scalar(mean_wide[:, :], mean_wide[:, :], mean[:, :], None, ALU.mult).then_inc(wide_ready, 1)
        for e in range(E):
            dve.tensor_copy(mean_diag[:, e, e:e + 1], mean[:, :]).then_inc(wide_ready, 1)
        dve.wait_ge(made, 3)
        dve.tensor_copy(k.gamma_router[:, :], banks[:, 5, 0:2 * E]).then_inc(done, 1)
        dve.tensor_copy(k.gamma_col[:, :], banks[0:E, 6, 0:1]).then_inc(done, 1)
        dve.wait_ge(done, 2)
        dve.scalar_tensor_tensor(k.offsets[:, :], expert_b, k.gamma_col[:, :], banks[0:E, 7, 0:D],
                                 ALU.mult, ALU.add).then_inc(done, 1)

    def tensor(pe):
        pe.wait_ge(set_, 1)
        pe.wait_ge(*loaded)
        pe.matmul(banks[:, 4, 0:1], ins, sixteenth[:, :], start=True, stop=True).then_inc(mean_made, 1)
        pe.wait_ge(wide_ready, 1 + E)
        pe.matmul(banks[:, 5, 0:2 * E], mean_wide[:, :], w16, start=True, stop=True).then_inc(made, 1)
        pe.matmul(banks[0:E, 6, 0:1], w16[:, 0:E], mean[:, :], start=True, stop=True).then_inc(made, 1)
        for e in range(E):
            mm = pe.matmul(banks[0:E, 7, 0:D], mean_diag[:, e, :], beta_w[:, e, :], start=e == 0, stop=e == E - 1)
        mm.then_inc(made, 1)

    return {"vector": vector, "tensor": tensor}


def mix_linear(nc, k, xT, expert_w, comb, comb_t, offsets, h, banks, scaled_sb, half_sum):
    made, offset_made, off_done, taken = k.sem("l_made"), k.sem("l_offset"), k.sem("l_offdone"), k.sem("l_taken")
    cg_ready, scaled, paired, summed, added = (k.sem("l_" + s) for s in ("cg", "scaled", "paired", "summed", "added"))
    cg = k.route[:, 0, :, :]
    EH = E // 2
    SLOT = 3
    with nc.Block() as block:

        @block.tensor
        def _(pe):
            for t in range(TILES):
                if t % PER == 0:
                    c = t // PER
                    if c >= 2:
                        pe.wait_ge(off_done, c - 1)
                    for j in range(PER):
                        mm = pe.matmul(banks[:, 6 + c % 2, j * P:(j + 1) * P], comb_t[:, (t + j) * P:(t + j + 1) * P],
                                       offsets, start=True, stop=True)
                    mm.then_inc(offset_made, 1)
                for half in range(2):
                    if t >= SLOT:
                        pe.wait_ge((taken, scaled)[half], (t - SLOT + 1) * EH)
                    pe.matmul(banks[:, 2 * (t % SLOT) + half, :], xT[:, t * P:(t + 1) * P],
                              expert_w[:, half * N:(half + 1) * N], start=True, stop=True).then_inc(made, 1)

        @block.scalar
        def _(act):
            act.wait_ge(cg_ready, 1)
            for t in range(TILES):
                act.wait_ge(made, 2 * t + 2)
                if t >= 2:
                    act.wait_ge(paired, t - 1)
                for e in range(EH):
                    act.activation(scaled_sb[:, t % 2, e, :], banks[:, 2 * (t % SLOT) + 1, e * D:(e + 1) * D], ACT.Copy,
                                   scale=cg[:, t, EH + e:EH + e + 1]).then_inc(scaled, 1)

        @block.gpsimd
        def _(pool):
            for t in range(TILES):
                pool.wait_ge(scaled, (t + 1) * EH)
                if t >= 2:
                    pool.wait_ge(added, t - 1)
                pairs = scaled_sb[:, t % 2, :, :]
                pool.tensor_tensor(half_sum[:, t % 2, :, :], pairs[:, 0:2, :], pairs[:, 2:4, :], ALU.add).then_inc(paired, 1)
                pool.wait_ge(paired, t + 1)
                pool.tensor_tensor(half_sum[:, t % 2, 0, :], half_sum[:, t % 2, 0, :], half_sum[:, t % 2, 1, :],
                                   ALU.add).then_inc(summed, 1)

        @block.vector
        def _(dve):
            def add_sum(t):
                dve.wait_ge(summed, t + 1)
                dve.wait_ge(taken, (t + 1) * EH)
                dve.tensor_tensor(h[:, t, :], h[:, t, :], half_sum[:, t % 2, 0, :], ALU.add).then_inc(added, 1)

            dve.tensor_tensor(cg, comb[:, :, :], k.gamma_router[:, 0:E].unsqueeze(1).to_broadcast([P, TILES, E]),
                              ALU.mult).then_inc(cg_ready, 1)
            dve.wait_ge(cg_ready, 1)
            for t in range(TILES):
                if t % PER == 0:
                    c = t // PER
                    dve.wait_ge(offset_made, c + 1)
                    x = h[:, t:t + PER, :]
                    dve.tensor_tensor(x, banks[:, 6 + c % 2, :].rearrange("p (t d) -> p t d", t=PER), x,
                                      ALU.add).then_inc(off_done, 1)
                    dve.wait_ge(off_done, c + 1)
                dve.wait_ge(made, 2 * t + 1)
                for e in range(EH):
                    if e:
                        dve.wait_ge(taken, t * EH + e)
                    dve.scalar_tensor_tensor(h[:, t, :], banks[:, 2 * (t % SLOT), e * D:(e + 1) * D],
                                             cg[:, t, e:e + 1], h[:, t, :], ALU.mult, ALU.add).then_inc(taken, 1)
                if t:
                    add_sum(t - 1)
            add_sum(TILES - 1)


class SortedTile:

    def __init__(self, i, first):
        self.i, self.first, self.slot = i, first, first % 4

    def index(self, add=0):
        return self.i * 4 + (self.first + add)

    def use(self, add=0):
        return self.i + (self.first // 4 + add)

    def after(self, n):
        return SortedTile(self.i, self.first + n)

    def known(self, limit):
        return not isinstance(self.i, int) or self.i * 4 + self.first < limit


def sorted_tiles(eng, body):
    for first in range(4):
        body(SortedTile(0, first))
    passes = (SORTED_TILES - 4 - 1) // 4
    with eng.Fori(0, passes) as i:
        for first in range(4, 8):
            body(SortedTile(i, first))
    for first in range(4 + 4 * passes, SORTED_TILES):
        body(SortedTile(0, first))


def mix_mlp(nc, k, rows_sb, slots_dram, y_dram, experts, b2, gain, bias, gates, gates_t, y, h, out, banks, ident, bufs):
    weight_ring, row_ring, zt_ring, hid, y_ring, best_y, second_y = bufs
    both, second, best = k.route[:, 0, :, :], k.route[:, 3, :, :], k.route[:, 5, :, :]
    ids, slot_ids, expert_rows = k.dst_ids, k.slot_ids, k.expert_rows
    step, row_sums, counts_made = k.sem("m_step"), k.sem("m_row_sums"), k.sem("m_counts")
    experts_known, slots_known, doubled, sent = (k.sem("m_" + n) for n in ("experts", "slots", "doubled", "sent"))
    turned, gates_out, off_made, off_done = (k.sem("m_" + n) for n in ("g_turned", "g_out", "offset", "off_done"))
    base, gate_ready = k.sem("m_base"), k.sem("m_gate")
    row_in, w_in, y_out = ([k.sem(f"m_{n}{s}") for s in range(4)] for n in ("row_in", "w_in", "y_out"))
    z_turned, z_copied, up, act_done, down, y_copied = (k.sem("m_" + n) for n in ("z_turned", "z_copied", "up", "gelu", "down", "y_copied"))
    best_in, second_in = ([k.sem(f"m_{n}{g}") for g in range(4)] for n in ("best_in", "second_in"))
    settled = [k.sem(f"m_settled{i}") for i in range(2)]
    added, stored = k.sem("m_added"), k.sem("m_stored")
    tokens = out.rearrange("b (t p) d -> p (b t) d", p=P)
    slot_rows = slots_dram.rearrange("(s f p) c -> p s f c", p=P, f=ROWS // P)
    token_rows = y_dram[0:BEST * TOKENS, :].rearrange("(w t p) d -> p w t d", p=P, w=BEST)
    FINAL = TILES // 4
    HALVES = ROWS // P

    def used(s):
        return (SORTED_TILES - s + 3) // 4

    with nc.Block() as block:

        @block.vector
        def _(dve):
            n = [0]

            def then(ins):
                n[0] += 1
                ins.then_inc(step, 1)
                dve.wait_ge(step, n[0])

            row_sum, at, tiles, end = (k.small[:, i, :] for i in range(4))
            dve.tensor_reduce(row_sum, both.rearrange("p t e -> p e t"), AX.X, ALU.add).then_inc(row_sums, 1)
            old, new = both, k.route[:, 1, :, :]
            spare = k.route[:, 4, :, :]
            reach = 1
            while reach < TILES:
                dve.tensor_copy(new[:, 0:reach, :], old[:, 0:reach, :]).then_inc(step, 1)
                n[0] += 1
                then(dve.tensor_tensor(new[:, reach:, :], old[:, reach:, :], old[:, 0:TILES - reach, :], ALU.add))
                old, new, spare = new, spare, new
                reach *= 2
            upto = old
            dve.wait_ge(counts_made, 1)
            steps = k.count_steps.unsqueeze(1).to_broadcast([P, E, COUNT_STEPS])
            then(dve.tensor_tensor(k.over[:, :, :], banks[:, 0, E:2 * E].unsqueeze(2).to_broadcast([P, E, COUNT_STEPS]),
                                   steps, ALU.is_gt))
            then(dve.tensor_reduce(tiles, k.over[:, :, :], AX.X, ALU.add))
            then(dve.tensor_copy(end[:, 0:1], tiles[:, 0:1]))
            for e in range(1, E):
                then(dve.tensor_tensor(end[:, e:e + 1], end[:, e - 1:e], tiles[:, e:e + 1], ALU.add))
            ends = end[:, 0:E - 1].unsqueeze(1).to_broadcast([P, SORTED_TILES, E - 1])
            then(dve.tensor_tensor(k.past[:, :, :], k.tile_index.unsqueeze(2).to_broadcast([P, SORTED_TILES, E - 1]),
                                   ends, ALU.is_ge))
            then(dve.tensor_reduce(k.tile_expert[:, :], k.past[:, :, :], AX.X, ALU.add))
            then(dve.tensor_scalar(k.tile_expert[:, :], k.tile_expert[:, :], float(P), k.partition, ALU.mult, ALU.add))
            dve.tensor_copy(expert_rows[:, 0:3], k.tile_expert[:, 0:3]).then_inc(experts_known, 1)
            then(dve.tensor_tensor(at, end, tiles, ALU.subtract))
            then(dve.tensor_scalar(at, at, float(ROWS), -1.0, ALU.mult, ALU.add))
            then(dve.tensor_tensor(at, at, banks[:, 0, 0:E], ALU.add))
            then(dve.tensor_tensor(upto, upto, at.unsqueeze(1).to_broadcast([P, TILES, E]), ALU.add))
            for which, mask in enumerate((best, second)):
                then(dve.tensor_tensor(new, upto, mask, ALU.mult))
                then(dve.tensor_reduce(k.slot_of[:, which, :], new, AX.X, ALU.add))
            dve.tensor_copy(slot_ids[:, :, :], k.slot_of[:, :, :]).then_inc(slots_known, 1)
            for which, mask in enumerate((best, second)):
                then(dve.tensor_tensor(new, gates[:, :, :], mask, ALU.mult))
                then(dve.tensor_reduce(k.gate_of[:, which, :], new, AX.X, ALU.add))
            for c in range(CHUNKS):
                dve.wait_ge(off_made, c + 1)
                x = h[:, c * PER:(c + 1) * PER, :]
                dve.wait_ge(base, c + 1)
                dve.tensor_tensor(x, banks[:, 4 + c % 2, :].rearrange("p (t d) -> p t d", t=PER), x,
                                  ALU.add).then_inc(off_done, 1)

            def z_out(tile):
                dve.wait_ge(z_turned, tile.index(1))
                dve.tensor_scalar(zt_ring[:, tile.slot, :], banks[:, tile.first % 2, 0:ROWS], gain, bias, ALU.mult,
                                  ALU.add).then_inc(z_copied, 1)

            def body(tile):
                if tile.after(2).known(SORTED_TILES):
                    z_out(tile.after(2))
                ahead = tile.after(3)
                if ahead.known(SORTED_TILES):
                    if isinstance(tile.i, int):
                        rows = k.tile_expert[:, ahead.first:ahead.first + 1]
                    else:
                        rows = k.tile_expert[:, bass.ds(ahead.index(), 1)]
                    dve.tensor_copy(expert_rows[:, ahead.slot:ahead.slot + 1], rows).then_inc(experts_known, 1)
                if tile.first >= 4:
                    dve.wait_ge(y_out[tile.slot], tile.use() * (16 * HALVES))
                dve.wait_ge(down, tile.index(1))
                dve.tensor_copy(ids[:, tile.slot, :], row_ring[:, tile.slot, :, D:D + 1].rearrange("p f c -> p (f c)")).then_inc(y_copied, 1)
                dve.tensor_copy(y_ring[:, tile.slot, :], banks[:, 6 + tile.first % 2, 0:ROWS]).then_inc(y_copied, 1)

            z_out(SortedTile(0, 0))
            z_out(SortedTile(0, 1))
            sorted_tiles(dve, body)
            for g in range(TILES // FINAL):
                for which, (rows, arrived) in enumerate(((best_y, best_in), (second_y, second_in))):
                    dve.wait_ge(arrived[g], 16)
                    for t in range(g * FINAL, (g + 1) * FINAL):
                        if which:
                            dve.wait_ge(added, 2 * g * FINAL + t % FINAL + 1)
                        elif not t:
                            dve.wait_ge(off_done, CHUNKS)
                        dve.scalar_tensor_tensor(h[:, t, :], rows[:, t, :], k.gate_of[:, which, t:t + 1], h[:, t, :],
                                                 ALU.mult, ALU.add).then_inc(added, 1)

        @block.tensor
        def _(pe):
            pe.wait_ge(row_sums, 1)
            pe.matmul(banks[:, 0, 0:E], k.lower, k.small[:, 0, :], start=True, stop=True)
            pe.matmul(banks[:, 0, E:2 * E], k.ones[:, :], k.small[:, 0, :], start=True, stop=True).then_inc(counts_made, 1)

            def offsets(c):
                pe.wait_ge(gates_out, c + 1)
                if c >= 2:
                    pe.wait_ge(off_done, c - 1)
                for j in range(PER):
                    t = c * PER + j
                    mm = pe.matmul(banks[:, 4 + c % 2, j * P:(j + 1) * P], gates_t[:, t * P:(t + 1) * P], b2,
                                   start=True, stop=True)
                mm.then_inc(off_made, 1)

            for c in range(CHUNKS):
                if c >= 2:
                    pe.wait_ge(gates_out, c - 1)
                for j in range(PER):
                    mm = pe.transpose(banks[0:E, 2 + c % 2, j * P:(j + 1) * P], gates[:, c * PER + j, :], ident[:, :])
                mm.then_inc(turned, 1)
                if c:
                    offsets(c - 1)
            offsets(CHUNKS - 1)
            pe.wait_ge(slots_known, 1)
            pe.wait_ge(off_done, CHUNKS)

            def turn(tile):
                pe.wait_ge(row_in[tile.slot], tile.use(1) * 16)
                for f in range(HALVES):
                    mm = pe.transpose(banks[:, tile.first % 2, f * P:(f + 1) * P], row_ring[:, tile.slot, f, 0:D], ident[:, :])
                mm.then_inc(z_turned, 1)

            def project_up(tile):
                pe.wait_ge(w_in[tile.slot], tile.use(1) * 16)
                pe.wait_ge(z_copied, tile.index(1))
                w1 = weight_ring[tile.slot]
                for f in range(FC):
                    mm = pe.matmul(banks[:, 2 + tile.first % 2 * 2 + f // 2, f % 2 * ROWS:(f % 2 + 1) * ROWS],
                                   w1[:, f * P:(f + 1) * P], zt_ring[:, tile.slot, :], start=True, stop=True)
                    if f % 2:
                        mm.then_inc(up, 1)

            def project_down(tile):
                pe.wait_ge(act_done, tile.index(1) * FC)
                if tile.first >= 2:
                    pe.wait_ge(y_copied, tile.index(-1) * 2)
                w2 = weight_ring[tile.slot][:, FF:2 * FF]
                for half in range(HALVES):
                    for f in range(FC):
                        mm = pe.matmul(banks[:, 6 + tile.first % 2, half * P:(half + 1) * P],
                                       hid[:, tile.first % 2, f, half * P:(half + 1) * P], w2[:, f * D:(f + 1) * D],
                                       start=f == 0, stop=f == FC - 1)
                mm.then_inc(down, 1)

            def body(tile):
                if tile.after(2).known(SORTED_TILES):
                    turn(tile.after(2))
                if tile.after(1).known(SORTED_TILES):
                    project_up(tile.after(1))
                project_down(tile)

            turn(SortedTile(0, 0))
            turn(SortedTile(0, 1))
            project_up(SortedTile(0, 0))
            sorted_tiles(pe, body)

        @block.scalar
        def _(act):
            for c in range(CHUNKS):
                s = slice(c * PER, (c + 1) * PER)
                act.activation(rows_sb[:, TILES + c * PER:TILES + (c + 1) * PER, 0:D], rows_sb[:, s, 0:D], ACT.Copy).then_inc(doubled, 1)
            for c in range(CHUNKS):
                act.wait_ge(turned, c + 1)
                act.activation(gates_t[:, c * N:(c + 1) * N], banks[0:E, 2 + c % 2, :], ACT.Copy).then_inc(gates_out, 1)

            def body(tile):
                if tile.first >= 2:
                    act.wait_ge(down, tile.index(-1))
                for f in range(FC):
                    if f % 2 == 0:
                        act.wait_ge(up, tile.index() * (FC // 2) + (f // 2 + 1))
                    act.activation(hid[:, tile.first % 2, f, :],
                                   banks[:, 2 + tile.first % 2 * 2 + f // 2, f % 2 * ROWS:(f % 2 + 1) * ROWS], ACT.Gelu,
                                   bias=weight_ring[tile.slot][:, 2 * FF + f:2 * FF + f + 1]).then_inc(act_done, 1)

            sorted_tiles(act, body)

        @block.gpsimd
        def _(pool):
            def settle(which, tile):
                if tile.first >= 1:
                    pool.wait_ge(settled[which], tile.index())
                pool.tensor_tensor(k.held[:, which:which + 1], k.nothing[:, 0:1], k.nothing[:, 0:1], ALU.add).then_inc(settled[which], 1)

            def weights_of(tile):
                rows = expert_rows[:, tile.slot:tile.slot + 1]
                pool.indirect_dma_start(weight_ring[tile.slot], None, experts[:, :],
                                        bass.IndirectOffsetOnAxis(ap=rows, axis=0)).then_inc(w_in[tile.slot], 16)

            for which in range(BEST):
                pool.tensor_copy(rows_sb[:, which * TILES:(which + 1) * TILES, D:D + 1],
                                 k.token_dst[:, which * TILES:(which + 1) * TILES].unsqueeze(2)).then_inc(doubled, 1)
            pool.wait_ge(experts_known, 1)
            for first in range(3):
                weights_of(SortedTile(0, first))
            pool.wait_ge(slots_known, 1)
            pool.wait_ge(doubled, BEST + CHUNKS)
            pool.wait_ge(k.slots_blank, 16)
            for t in range(TILES):
                for which in range(BEST):
                    pool.indirect_dma_start(slots_dram[:, :], bass.IndirectOffsetOnAxis(ap=slot_ids[:, which, t:t + 1], axis=0),
                                            rows_sb[:, which * TILES + t, :], None).then_inc(sent, 16)
            for c in range(CHUNKS):
                x = h[:, c * PER:(c + 1) * PER, :]
                pool.tensor_tensor(x, x, y[:, c * PER:(c + 1) * PER, :], ALU.add).then_inc(base, 1)

            def send_back(tile):
                pool.wait_ge(y_copied, tile.index(1) * 2)
                settle(1, tile)
                for half in range(HALVES):
                    pool.indirect_dma_start(y_dram[:, :], bass.IndirectOffsetOnAxis(ap=ids[:, tile.slot, half:half + 1], axis=0),
                                            y_ring[:, tile.slot, half * P:(half + 1) * P], None).then_inc(y_out[tile.slot], 16)

            def body(tile):
                if tile.after(3).known(SORTED_TILES):
                    if tile.first >= 1:
                        pool.wait_ge(down, tile.index())
                    pool.wait_ge(experts_known, tile.index(2))
                    settle(0, tile)
                    weights_of(tile.after(3))
                if tile.first >= 1:
                    send_back(tile.after(-1))

            sorted_tiles(pool, body)
            send_back(SortedTile(0, SORTED_TILES - 1))

        @block.sync
        def _(sp):
            sp.wait_ge(sent, 16 * BEST * TILES)

            def body(tile):
                if tile.first >= 4:
                    sp.wait_ge(y_copied, tile.index(-3) * 2)
                if isinstance(tile.i, int):
                    rows = slot_rows[:, tile.first, :, :]
                else:
                    rows = slot_rows[:, bass.ds(tile.index(), 1), :, :].rearrange("p s f c -> p (s f) c")
                sp.dma_start(row_ring[:, tile.slot, :, :], rows).then_inc(row_in[tile.slot], 16)

            sorted_tiles(sp, body)
            for s in range(4):
                sp.wait_ge(y_out[s], 16 * HALVES * used(s))
            for g in range(TILES // FINAL):
                s = slice(g * FINAL, (g + 1) * FINAL)
                sp.dma_start(best_y[:, s, :], token_rows[:, 0, s, :]).then_inc(best_in[g], 16)
                sp.dma_start(second_y[:, s, :], token_rows[:, 1, s, :]).then_inc(second_in[g], 16)
            for g in range(TILES // FINAL):
                s = slice(g * FINAL, (g + 1) * FINAL)
                sp.wait_ge(added, 2 * (g + 1) * FINAL)
                sp.dma_start(tokens[:, s, :], h[:, s, :]).then_inc(stored, 16)
            sp.wait_ge(stored, 16 * (TILES // FINAL))


def program(nc, ids, table, attn_w, attn_b, bv, bo, ins, gate_w, expert_w, expert_b, gamma_rmod, beta_w,
            ln_gb, w_r, b_r, experts, b2, shape_consts, out):
    with ExitStack() as ctx:
        k = Kit(nc, ctx)
        h, y = k.sbuf("h", [P, TILES, D]), k.sbuf("y", [P, TILES, D])
        xT = k.sbuf("xT", [P, TILES * P])
        v_all, attn = k.sbuf("v_all", [P, BH * SEQ_TILES, DH]), k.sbuf("attn", [P, TILES, D])
        q_st, k_st = k.sbuf("q_st", [P, 4, SEQ], BF16), k.sbuf("k_st", [P, 4, SEQ], BF16)
        probs = k.sbuf("probs", [P, 2, 4, N])
        v_st, o_sb = k.sbuf("v_st", [P, 2, SEQ_TILES, 32]), k.sbuf("o_sb", [P, 2, N])
        ident = k.sbuf("ident", [P, P])
        k.stats, k.mv = k.sbuf("stats", [P, TILES, 6]), k.sbuf("mv", [P, TILES, 2])
        k.std, k.rstd, k.shift = (k.sbuf(name, [P, TILES]) for name in ("std", "rstd", "shift"))
        k.ids, k.ids_in, k.blank = k.sbuf("ids", [P, TILES], I32), k.lasting_sem("ids_in"), k.lasting_sem("blank")
        k.mx, k.negm, k.mrest = k.sbuf("mx", [P, 2, SEQ_TILES, 2]), k.sbuf("negm", [P, 2, SEQ_TILES]), k.sbuf("mrest", [P, 2, SEQ_TILES])
        k.mparts, k.mturn = k.sbuf("mparts", [P, 2, PARTS, 32], BF16), k.sbuf("mturn", [P, 2, PARTS * 32], BF16)
        k.held = k.sbuf("held", [P, 2])
        k.nothing = k.sbuf("nothing", [P, SEQ_TILES])
        k.rec = k.sbuf("rec", [P, 2, 4, 4])
        k.route = k.sbuf("route", [P, 6, TILES, E])
        k.top, k.den, k.rank = k.sbuf("top", [P, TILES]), k.sbuf("den", [P, TILES]), k.sbuf("rank", [P, E])
        weights = k.sbuf("weights", [P, TILES, E])
        w_sb, b_sb = k.sbuf("w_sb", [P, 2, 4, D]), k.sbuf("b_sb", [P, 2, 2])
        bv_row, bo_row = k.sbuf("bv_row", [P, 2, D]), k.sbuf("bo_row", [P, 2, D])
        ins_sb, w16 = k.sbuf("ins_sb", [16, D]), k.sbuf("w16", [P, 2 * E])
        router = k.sbuf("router", [P, 2, E])
        eb_sb, br_row, b2_sb = k.sbuf("eb_sb", [E, D]), k.sbuf("br_row", [P, E]), k.sbuf("b2_sb", [E, D])
        ln_sb = k.sbuf("ln_sb", [P, 2])
        k.ins_mean, k.mean_wide, k.mean_diag = k.sbuf("ins_mean", [P, 1]), k.sbuf("mean_wide", [P, P]), k.sbuf("mean_diag", [P, E, E])
        k.sixteenth, k.gamma_router = k.sbuf("sixteenth", [16, 1]), k.sbuf("gamma_router", [P, 2 * E])
        k.gamma_col, k.offsets = k.sbuf("gamma_col", [E, 1]), k.sbuf("offsets", [E, D])
        ew_sb = k.sbuf("ew_sb", [P, E * D])
        rows_sb = k.sbuf("rows_sb", [P, PER_PART, D + 1])
        consts = k.sbuf("consts", [P, shape_consts.shape[1]])
        widths = (P, COUNT_STEPS, SORTED_TILES, 1, BEST * TILES, PER_PART)
        starts = [sum(widths[:i]) for i in range(len(widths))]
        k.lower, k.count_steps, k.tile_index, k.partition, k.token_dst, k.pad_dst = (
            consts[:, a:a + w] for a, w in zip(starts, widths))
        k.ones, k.small, k.over = k.sbuf("ones", [P, P]), k.sbuf("small", [P, 4, E]), k.sbuf("over", [P, E, COUNT_STEPS])
        k.past, k.tile_expert = k.sbuf("past", [P, SORTED_TILES, E - 1]), k.sbuf("tile_expert", [P, SORTED_TILES])
        k.expert_rows, k.slot_ids = k.sbuf("expert_rows", [P, 4], I32), k.sbuf("slot_ids", [P, BEST, TILES], I32)
        k.slot_of, k.gate_of = k.sbuf("slot_of", [P, BEST, TILES]), k.sbuf("gate_of", [P, BEST, TILES])
        k.dst_ids, k.slots_blank = k.sbuf("dst_ids", [P, 4, ROWS // P], I32), k.lasting_sem("slots_blank")
        banks = ctx.enter_context(nc.psum_tensor("banks", [P, 8, N], F32))
        m_dram = nc.dram_tensor("m_rows", [2, P, PARTS * 32], BF16).ap()
        parts_dram = nc.dram_tensor("qk_parts", [2, PARTS, BATCH * P, SEQ], BF16).ap()
        slots_dram = nc.dram_tensor("slots", [SORTED_TILES * ROWS, D + 1], F32).ap()
        y_dram = nc.dram_tensor("expert_rows_out", [BEST * TOKENS + SORTED_TILES * ROWS, D], F32).ap()

        rows_flat = rows_sb[:, :, :].rearrange("p j c -> p (j c)")
        part_ring = rows_flat[:, 0:4 * PARTS * N // 2].bitcast(BF16).rearrange("p (r s n) -> p r s n", r=4, s=PARTS)
        load_stacks = stack_loader(k, parts_dram, q_st, k_st)
        rest_ring = probs[:, 0, :, :]
        beta_sb = probs[:, :, :, :].rearrange("p a b n -> p (a b n)")[:, 0:E * D].rearrange("p (e d) -> p e d", e=E)
        wt = attn[0:E, :, :].rearrange("p t d -> p (t d)")
        z = rows_sb[:, 0:TILES, 0:D]
        v_flat = v_all[:, :, :].rearrange("p t d -> p (t d)")
        q_f32, k_f32 = (st[:, :, :].rearrange("p s n -> p (s n)").bitcast(F32) for st in (q_st, k_st))
        early = [(ins_sb[:, :], ins), (w16[:, :], gamma_rmod), (eb_sb[:, :], expert_b), (beta_sb, beta_w),
                 (w_sb[:, :, :, :], attn_w), (b_sb[:, :, :], attn_b), (router[:, 0, :], gate_w)]
        early += [(row[:, l, :], b[l].partition_broadcast(P)) for row, b in ((bv_row, bv), (bo_row, bo)) for l in range(2)]
        late = [(router[:, 1, :], w_r), (b2_sb[:, :], b2), (br_row[:, :], b_r.partition_broadcast(P)), (ln_sb[:, :], ln_gb),
                (ew_sb[:, :], expert_w), (consts[:, :], shape_consts)]
        k.stack_in = [k.lasting_sem(f"stack_in{s}") for s in range(4)]
        k.parts_stored = [[k.lasting_sem(f"parts_stored{b}_{s}") for s in range(4)] for b in range(BATCH)]
        early_in, late_in = k.lasting_sem("early_in"), k.lasting_sem("late_in")
        rows_in = [k.lasting_sem(f"rows_in{g}") for g in range(TILES // LN_GROUP)]

        def load(sp):
            for dst, src in early:
                sp.dma_start(dst, src).then_inc(early_in, 16)
            for dst, src in late:
                sp.dma_start(dst, src).then_inc(late_in, 16)
            sp.wait_ge(early_in, 16 * len(early))
            sp.wait_ge(late_in, 16 * len(late))

        start = mixture_constants(k, ins_sb[:, :], w16[:, :], eb_sb[:, :], beta_sb, banks, (early_in, 16 * len(early)))
        start["sync"] = load
        start["gpsimd"] = lambda pool: gather(pool, k, ids, table, h, ident, rows_in)
        for l in range(2):
            tag, k.layer = f"a{l}_", l
            layer_norm(nc, k, tag + "n", h, y, banks, ident, xT, rows_in=None if l else rows_in,
                       at_start=None if l else start)
            k.end_phase()
            project_qkv(nc, k, tag + "p", xT, w_sb[:, l], b_sb[:, l], bv_row[:, l], parts_dram,
                        v_all[:, :, :].rearrange("p (b t) d -> p b t d", b=BH), banks, part_ring, rest_ring,
                        load_stacks)
            k.end_phase()
            attention(nc, k, tag, SCALES[l], parts_dram, q_st, k_st, v_all, v_st, probs, o_sb, attn, h,
                      bo_row[:, l], banks, ident, m_dram, load_stacks)
            k.end_phase()
            project_out(nc, k, tag + "o", attn, w_sb[:, l, 3, :], h, banks, ident, o_sb)
            k.end_phase()
            if l == 0:
                layer_norm(nc, k, "f0_n", h, y, banks, ident, xT, router=router[:, 0, :])
                k.end_phase()
                route(nc, k, "f0_r", k.gamma_router[:, E:2 * E], True, banks, weights, ident, wt,
                      blank_slots=(slots_dram, rows_sb))
                k.end_phase()
                mix_linear(nc, k, xT, ew_sb, weights, wt, k.offsets[:, :], h, banks, q_f32.rearrange("p (s e d) -> p s e d", e=PER, d=D),
                           k_f32.rearrange("p (s e d) -> p s e d", e=2, d=D))
                k.end_phase()
        layer_norm(nc, k, "f1_n", h, y, banks, ident)
        k.end_phase()
        layer_norm(nc, k, "f1_m", y, z, banks, ident, xT, gain=ln_sb[:, 0:1], bias=ln_sb[:, 1:2],
                   router=router[:, 1, :])
        k.end_phase()
        route(nc, k, "f1_r", br_row[:, :], False, banks, weights, ident, None)
        k.end_phase()
        W_ROW, R_ROW = experts.shape[1], ROWS // P * (D + 1)
        weight_ring = [flat[:, at:at + W_ROW] for flat in (v_flat, k_f32) for at in (0, W_ROW)]
        bufs = (weight_ring,
                v_flat[:, 2 * W_ROW:2 * W_ROW + 4 * R_ROW].rearrange("p (s f c) -> p s f c", s=4, c=D + 1),
                q_f32[:, 0:4 * ROWS].rearrange("p (s n) -> p s n", s=4),
                q_f32[:, 4 * ROWS:4 * ROWS + 2 * FC * ROWS].rearrange("p (s f n) -> p s f n", s=2, f=FC),
                q_f32[:, (4 + 2 * FC) * ROWS:(8 + 2 * FC) * ROWS].rearrange("p (s n) -> p s n", s=4),
                xT[:, :].rearrange("p (t d) -> p t d", d=D),
                probs[:, :, :, :].rearrange("p a b n -> p (a b n)").rearrange("p (t d) -> p t d", d=D))
        mix_mlp(nc, k, rows_sb, slots_dram, y_dram, experts, b2_sb[:, :], ln_sb[:, 0:1], ln_sb[:, 1:2], weights, wt, y, h, out, banks, ident, bufs)


def shape_consts(np):
    p = np.arange(P).reshape(P, 1)
    rows = lambda x: np.broadcast_to(x, (P, len(x)))
    parts = [p < np.arange(P), rows(ROWS * np.arange(COUNT_STEPS)), rows(np.arange(SORTED_TILES)), p,
             np.arange(BEST * TILES) * P + p, BEST * TOKENS + p * PER_PART + np.arange(PER_PART)]
    return np.concatenate([np.asarray(x, np.float32) for x in parts], axis=1)


def kernel(**inputs):
    import numpy as np
    import concourse.bacc as bacc
    from concourse.bass_utils import run_bass_kernel_spmd as run

    a = {name: np.asarray(x) for name, x in inputs.items()}
    qkv = a["L1_attn_qkv_w"].reshape(HEADS, 3, DH, D).transpose(1, 3, 0, 2).reshape(3, D, D)
    qkv_b = a["L1_attn_qkv_b"].reshape(HEADS, 3, DH).transpose(1, 0, 2).reshape(3, D)
    mats = [[a["L0_attn_Wq"], a["L0_attn_Wk"], a["L0_attn_Wv"], a["L0_attn_Wo"]],
            [qkv[0], qkv[1], qkv[2], a["L1_attn_out_w"].T]]
    arrays = {
        "ids": a["x"].reshape(TILES, P).T,
        "table": a["L0_tok_weight"],
        "attn_w": np.array(mats).transpose(2, 0, 1, 3),
        "attn_b": np.array([[a["L0_attn_bq"], a["L0_attn_bk"]], [qkv_b[0], qkv_b[1]]]).transpose(2, 0, 1),
        "bv": np.array([a["L0_attn_bv"], qkv_b[2]]),
        "bo": np.array([a["L0_attn_bo"], a["L1_attn_out_b"]]),
        "ins": a["L0_ffn_Ins_tk"][0],
        "gate_w": a["L0_ffn_gate_w"],
        "expert_w": a["L0_ffn_expert_w"].transpose(1, 0, 2).reshape(D, E * D),
        "expert_b": a["L0_ffn_expert_b"],
        "gamma_rmod": np.concatenate([a["L0_ffn_gamma_w"].T, a["L0_ffn_rmod_w"]], axis=1),
        "beta_w": a["L0_ffn_beta_w"].transpose(1, 0, 2),
        "ln_gb": np.array([a["L1_ffn_ln_g"], a["L1_ffn_ln_b"]]).T,
        "w_r": a["L1_ffn_w_r"].T,
        "b_r": a["L1_ffn_b_r"],
        "experts": np.concatenate([a["L1_ffn_W1"], a["L1_ffn_W2"].reshape(E, FC, P, D).transpose(0, 2, 1, 3).reshape(E, P, FF),
                                   a["L1_ffn_b1"].reshape(E, FC, P).transpose(0, 2, 1)], axis=2).reshape(E * P, 2 * FF + FC),
        "b2": a["L1_ffn_b2"],
        "shape_consts": shape_consts(np),
    }
    nc = bacc.Bacc("TRN2", target_bir_lowering=False, num_devices=1)
    feed, aps = {}, []
    for name, x in arrays.items():
        x = np.ascontiguousarray(x)
        feed[f"in_{name}"] = x
        aps.append(nc.dram_tensor(f"in_{name}", x.shape, mybir.dt.from_np(x.dtype), kind="ExternalInput").ap())
    out = nc.dram_tensor("out", (BATCH, SEQ, D), F32, kind="ExternalOutput").ap()
    program(nc, *aps, out)
    return run(nc, [feed], core_ids=[0]).results[0]["out"]
```

```python
from contextlib import ExitStack

import concourse.bass as bass
from concourse import mybir

ALU = mybir.AluOpType
ACT = mybir.ActivationFunctionType
AX = mybir.AxisListType
F32 = mybir.dt.float32
BF16 = mybir.dt.bfloat16
I32 = mybir.dt.int32

P = 128
BATCH = 2
SEQ = 2048
D = 128
HEADS = 8
DH = D // HEADS
TILES = BATCH * SEQ // P
BH = BATCH * HEADS
SEQ_TILES = SEQ // P
N = 512
CHUNKS = BATCH * SEQ // N
PER = N // P
E = 8
FF = 512
FC = FF // P
EPS = 1e-5
TOKENS = BATCH * SEQ
BEST = 2
ROWS = 2 * P
SENT = TILES - PER
SORTED_TILES = (BEST * SENT * P - E) // ROWS + E
PER_PART = SORTED_TILES * ROWS // P
COUNT_STEPS = SENT * P // ROWS
BIG = 3e38
SCALES = (float(D) ** -0.5, float(DH) ** -0.5)
PARTS = 3
Q_PART = (0, 0, 0, 1, 1, 2)
K_PART = (0, 1, 2, 0, 1, 0)
SLOTS = len(Q_PART)
SROWS = SLOTS * DH
MROW = SROWS


class Kit:

    def __init__(self, nc, ctx):
        self.nc, self.ctx = nc, ctx
        self.phase, self.cleared = [], []

    def sbuf(self, name, shape, dt=F32):
        return self.ctx.enter_context(self.nc.sbuf_tensor(name, shape, dt))

    def lasting_sem(self, name):
        return self.ctx.enter_context(self.nc.semaphore(name))

    def sem(self, name):
        sem = self.nc.alloc_semaphore(name=name)
        self.phase.append(sem)
        return sem

    def end_phase(self):
        for sem in self.cleared:
            self.nc.release_semaphore(sem)
        for sem in self.phase:
            self.nc.gpsimd.sem_clear(sem)
        self.phase, self.cleared = [], self.phase


def gather(pool, k, ids_dram, table, h, ident, rows_in):
    pool.dma_start(k.ids[:, :], ids_dram[:, :]).then_inc(k.ids_in, 16)
    pool.memset(ident[:, :], 0.0).then_inc(k.blank, 1)
    pool.wait_ge(k.blank, 1)
    pool.affine_select(out=ident[:, :], in_=ident[:, :], compare_op=ALU.not_equal, fill=1.0,
                       base=0, pattern=[[-1, P]], channel_multiplier=1).then_inc(k.blank, 1)
    pool.wait_ge(k.ids_in, 16)
    for t in range(TILES):
        pool.indirect_dma_start(h[:, t, :], None, table[:, :],
                                bass.IndirectOffsetOnAxis(ap=k.ids[:, t:t + 1], axis=0)).then_inc(rows_in[t // LN_GROUP], 16)


LN_GROUP = 8


def layer_norm(nc, k, tag, src, dst, banks, ident, xT=None, gain=None, bias=None, rows_in=None,
               at_start=None, router=None, then=None):
    G = LN_GROUP
    groups = TILES // G
    then = then or {}
    own = (6, 7) if then else (0, 1, 2)
    stats, mv, std, rstd, shift = k.stats, k.mv, k.std, k.rstd, k.shift
    stats_done, moments, var_ready = k.sem(tag + "stats"), k.sem(tag + "moments"), k.sem(tag + "var")
    std_ready, rstd_ready, shift_ready = k.sem(tag + "std"), k.sem(tag + "rstd"), k.sem(tag + "shift")
    turned, copied = k.sem(tag + "turned"), k.sem(tag + "copied")
    by_pool, by_act, by_dve = (k.sem(tag + "by_" + name) for name in ("pool", "act", "dve"))
    dve_tiles = list(range(TILES)) if then else []
    pool_tiles = [] if then else list(range(0, TILES, 2))
    act_tiles = [] if then else list(range(1, TILES, 2))
    at_start = at_start or {}
    with nc.Block() as block:

        @block.vector
        def _(dve):
            if "vector" in at_start:
                at_start["vector"](dve)

            def moments_of(g):
                if rows_in is not None:
                    dve.wait_ge(rows_in[g], 16 * G)
                for t in range(g * G, g * G + G):
                    dve.bn_stats(stats[:, t, :], src[:, t, :]).then_inc(stats_done, 1)
                dve.wait_ge(stats_done, (g + 1) * G)
                for t in range(g * G, g * G + G):
                    dve.bn_aggr(mv[:, t, :], stats[:, t, :]).then_inc(moments, 1)
                dve.wait_ge(moments, (g + 1) * G)
                s = slice(g * G, g * G + G)
                dve.tensor_scalar(std[:, s], mv[:, s, 1], EPS, None, ALU.add).then_inc(var_ready, 1)

            def scales_of(g):
                s = slice(g * G, g * G + G)
                dve.wait_ge(std_ready, g + 1)
                dve.reciprocal(rstd[:, s], std[:, s]).then_inc(rstd_ready, 1)
                dve.wait_ge(rstd_ready, g + 1)
                dve.scalar_tensor_tensor(shift[:, s], mv[:, s, 0], -1.0, rstd[:, s], ALU.mult,
                                         ALU.mult).then_inc(shift_ready, 1)

            if then:
                for g in range(groups):
                    moments_of(g)
                    scales_of(g)
                    dve.wait_ge(shift_ready, g + 1)
                    for t in range(g * G, g * G + G):
                        dve.tensor_scalar(dst[:, t, :], src[:, t, :], rstd[:, t:t + 1], shift[:, t:t + 1],
                                          ALU.mult, ALU.add).then_inc(by_dve, 1)
                    if g:
                        then["vector"](dve, g - 1)
                then["vector"](dve, groups - 1)
                then["vector_end"](dve)
            else:
                for g in range(groups):
                    moments_of(g)
                    if g:
                        scales_of(g - 1)
                scales_of(groups - 1)

        @block.gpsimd
        def _(pool):
            if "gpsimd" in at_start:
                at_start["gpsimd"](pool)
            for t in pool_tiles:
                pool.wait_ge(shift_ready, t // G + 1)
                pool.tensor_scalar(dst[:, t, :], src[:, t, :], rstd[:, t:t + 1], shift[:, t:t + 1],
                                   ALU.mult, ALU.add).then_inc(by_pool, 1)
            if then:
                then["gpsimd"](pool)

        @block.scalar
        def _(act):
            def root(g):
                s = slice(g * G, g * G + G)
                act.wait_ge(var_ready, g + 1)
                act.activation(std[:, s], std[:, s], ACT.Sqrt).then_inc(std_ready, 1)

            def copies(g):
                for c in range(g * G // PER, (g + 1) * G // PER if xT is not None else 0):
                    act.wait_ge(turned, c + 1)
                    out = xT[:, c * N:(c + 1) * N]
                    turned_rows = banks[:, own[c % len(own)], :]
                    if gain is None:
                        act.activation(out, turned_rows, ACT.Copy).then_inc(copied, 1)
                    else:
                        act.activation(out, turned_rows, ACT.Identity, bias=bias, scale=gain).then_inc(copied, 1)

            if then:
                for g in range(groups):
                    root(g)
                    if g:
                        then["scalar"](act, g - 1)
                    copies(g)
                then["scalar"](act, groups - 1)
                return
            root(0)
            for g in range(groups):
                if g + 1 < groups:
                    root(g + 1)
                act.wait_ge(shift_ready, g + 1)
                for t in act_tiles:
                    if t // G == g:
                        act.activation(dst[:, t, :], src[:, t, :], ACT.Identity, bias=shift[:, t:t + 1],
                                       scale=rstd[:, t:t + 1]).then_inc(by_act, 1)
                if g:
                    copies(g - 1)
            copies(groups - 1)

        @block.tensor
        def _(pe):
            if "tensor" in at_start:
                at_start["tensor"](pe)
            if rows_in is not None:
                pe.wait_ge(k.blank, 2)

            def logits(c):
                pe.wait_ge(copied, c + 1)
                for t in range(c * PER, (c + 1) * PER):
                    pe.matmul(banks[:, 4, t * E:(t + 1) * E], xT[:, t * P:(t + 1) * P], router, start=True, stop=True)

            def turn(c):
                for done, tiles in ((by_pool, pool_tiles), (by_act, act_tiles), (by_dve, dve_tiles)):
                    if tiles:
                        pe.wait_ge(done, sum(t < (c + 1) * PER for t in tiles))
                if c >= len(own):
                    pe.wait_ge(copied, c - len(own) + 1)
                for j in range(PER):
                    mm = pe.transpose(banks[:, own[c % len(own)], j * P:(j + 1) * P], dst[:, c * PER + j, :], ident[:, :])
                mm.then_inc(turned, 1)

            per_group = G // PER
            for g in range(groups if xT is not None else 0):
                if then and g:
                    pe.wait_ge(copied, g * per_group)
                    then["tensor"](pe, g - 1)
                for c in range(g * per_group, (g + 1) * per_group):
                    turn(c)
                    if router is not None and c >= 2:
                        logits(c - 2)
            if then:
                pe.wait_ge(copied, CHUNKS)
                then["tensor"](pe, groups - 1)
            if router is not None:
                logits(CHUNKS - 2)
                logits(CHUNKS - 1)

        @block.sync
        def _(sp):
            if "sync" in at_start:
                at_start["sync"](sp)
            if then:
                then["sync"](sp)


def project_qkv(k, tag, xT, w, b, bv_row, parts_dram, v_all, banks, part_ring, rest_ring, load_stacks, CG):
    R = 4
    PER_BATCH = 2 * CHUNKS // BATCH
    made, first_cut, rest, second_cut = k.sem(tag + "made"), k.sem(tag + "cut1"), k.sem(tag + "rest"), k.sem(tag + "cut2")
    third_cut, v_taken = k.sem(tag + "cut3"), k.sem(tag + "v_taken")
    stored = k.parts_stored
    assert CHUNKS // BATCH * 2 % R == 0

    def bank(c, which):
        return banks[:, (c % 2) * 3 + which, :]

    def loaded(eng, g):
        if k.layer == 0 and g == 0:
            eng.wait_ge(*k.weights_in)

    def tensor(pe, g):
        loaded(pe, g)
        for c in range(g * CG, (g + 1) * CG):
            x = xT[:, c * N:(c + 1) * N]
            if c >= 2:
                pe.wait_ge(rest, 2 * (c - 1))
            for which in range(2):
                pe.matmul(bank(c, which), w[:, which, :], x, start=True, stop=True).then_inc(made, 1)
            if c >= 2:
                pe.wait_ge(v_taken, c - 1)
            for j in range(PER):
                mm = pe.matmul(bank(c, 2)[:, j * P:(j + 1) * P], xT[:, c * N + j * P:c * N + (j + 1) * P],
                               w[:, 2, :], start=True, stop=True)
            mm.then_inc(made, 1)

    def scalar(act, g):
        def first(m):
            c, which = m // 2, m % 2
            if m >= R:
                act.wait_ge(stored[(m - R) // PER_BATCH][m % R], 16 * ((m - R) % PER_BATCH // R + 1 + k.layer * (PER_BATCH // R)))
            act.wait_ge(made, 3 * c + which + 1)
            act.activation(part_ring[:, m % R, 0, :], bank(c, which), ACT.Identity,
                           bias=b[:, which:which + 1]).then_inc(first_cut, 1)

        loaded(act, g)
        if k.layer and g == 0:
            act.wait_ge(k.slots_blank, 16)
        end = 2 * CG * (g + 1)
        first(2 * CG * g)
        for m in range(2 * CG * g, end):
            if m + 1 < end:
                first(m + 1)
            act.wait_ge(rest, m + 1)
            act.activation(part_ring[:, m % R, 1, :], rest_ring[:, m % R, :], ACT.Copy).then_inc(second_cut, 1)

    def third(dve, m):
        dve.wait_ge(second_cut, m + 1)
        dve.tensor_tensor(part_ring[:, m % R, 2, :], rest_ring[:, m % R, :], part_ring[:, m % R, 1, :],
                          ALU.subtract).then_inc(third_cut, 1)

    def vector(dve, g):
        loaded(dve, g)
        for m in range(2 * CG * g, 2 * CG * (g + 1)):
            c, which = m // 2, m % 2
            dve.wait_ge(first_cut, m + 1)
            dve.scalar_tensor_tensor(rest_ring[:, m % R, :], bank(c, which), b[:, which:which + 1],
                                     part_ring[:, m % R, 0, :], ALU.add, ALU.subtract).then_inc(rest, 1)
            if m >= 1:
                third(dve, m - 1)
            if which == 1:
                bi, t0 = c * PER // SEQ_TILES, c * PER % SEQ_TILES
                dve.wait_ge(made, 3 * c + 3)
                for j in range(PER):
                    vt = dve.tensor_tensor(
                        v_all[:, bi * HEADS:(bi + 1) * HEADS, t0 + j, :],
                        bank(c, 2)[:, j * P:(j + 1) * P].rearrange("p (h d) -> p h d", d=DH),
                        bv_row[:, :].rearrange("p (h d) -> p h d", d=DH), ALU.add)
                vt.then_inc(v_taken, 1)

    def sync(sp):
        for m in range(2 * CHUNKS):
            c, which = m // 2, m % 2
            bi, col = c * N // SEQ, c * N % SEQ
            sp.wait_ge(third_cut, m + 1)
            sp.dma_start(parts_dram[which, :, bi * P:(bi + 1) * P, col:col + N].rearrange("s p n -> p s n"),
                         part_ring[:, m % R, :, :]).then_inc(stored[bi][m % R], 16)

    def gpsimd(pool):
        for s in range(R):
            pool.wait_ge(stored[0][s], 16 * PER_BATCH // R * (k.layer + 1))
        load_stacks(pool, 0, 0, k.first_in)

    return {"tensor": tensor, "scalar": scalar, "vector": vector, "sync": sync, "gpsimd": gpsimd,
            "vector_end": lambda dve: third(dve, 2 * CHUNKS - 1)}


def all_groups(nc, parts):
    with nc.Block() as block:

        @block.tensor
        def _(pe):
            parts["tensor"](pe, 0)

        @block.scalar
        def _(act):
            parts["scalar"](act, 0)

        @block.vector
        def _(dve):
            parts["vector"](dve, 0)
            parts["vector_end"](dve)

        @block.sync
        def _(sp):
            parts["sync"](sp)

        @block.gpsimd
        def _(pool):
            parts["gpsimd"](pool)


def stack_loader(k, parts_dram, q_st, k_st):
    def load_stacks(sp, n, s, first=None):
        for rows, order, which in ((q_st, Q_PART, 0), (k_st, K_PART, 1)):
            for slot, part in enumerate(order):
                sp.dma_start(rows[slot * DH:(slot + 1) * DH, s, :],
                             parts_dram[which, part, bass.ds(n * DH, DH), :]).then_inc(k.stack_in[s] if first is None else first, 16)
    return load_stacks


def attention(nc, k, tag, scale, parts_dram, q_st, k_st, v_all, v_st, probs, o_sb, attn, h, bo_row, banks, ident, m_dram, load_stacks):
    U = 4
    G = SEQ_TILES
    PV_LEAD, RING = 1, 2
    ST_LEAD = PV_LEAD + RING
    S_LEAD = ST_LEAD + G + 4
    NST, NS, SETS = 2, 4, 4
    ORDER = (("ST", 0), ("ST", 1), ("S", 0), ("S", 1), ("S", 2), ("S", 3), ("ST", 2), ("ST", 3))
    STEPS = SETS * G
    LOOPS = BH // SETS - 1
    TOTAL = BH * G
    st_bank, s_bank, o_bank = 0, NST, NST + NS

    made = k.stack_in
    before = [k.layer * (BH // SETS - (s == 0)) - (s == 0) for s in range(SETS)]
    mrow_in, m_out = k.sem(tag + "mrow_in"), k.sem(tag + "m_out")
    s_ready, s_used, mx_ready = k.sem(tag + "s_ready"), k.sem(tag + "s_used"), k.sem(tag + "mx_ready")
    m_cut, m_cut2, m_turned = k.sem(tag + "m_cut"), k.sem(tag + "m_cut2"), k.sem(tag + "m_turned")
    st_ready, exp_done, pv_done = k.sem(tag + "st_ready"), k.sem(tag + "exp_done"), k.sem(tag + "pv_done")
    v_ready, o_copied, o_turned = k.sem(tag + "v_ready"), k.sem(tag + "o_copied"), k.sem(tag + "o_turned")
    o_rec, o_free, primed, h_done = k.sem(tag + "o_rec"), k.sem(tag + "o_free"), k.sem(tag + "primed"), k.sem(tag + "h_done")
    mx, negm, mrest, mparts, mturn, rec = k.mx, k.negm, k.mrest, k.mparts, k.mturn, k.rec

    heads = attn[:, :, :].rearrange("p (b t) (h d) -> p b t h d", b=BATCH, h=HEADS)

    class At:

        def __init__(self, i, tau, lead):
            self.s = tau + lead
            self.g = i * STEPS + self.s
            self.n = i * SETS + self.s // G
            self.in_head = self.s % G

    def rounds(eng, body):
        with eng.Fori(0, LOOPS) as i:
            body(i, False)
        body(LOOPS, True)

    def live(at, last, lead):
        return not last or at.s < STEPS

    def st_place(at, u):
        tail = at.g - (TOTAL - S_LEAD + ST_LEAD) if isinstance(at.g, int) else -1
        if tail < 0:
            return st_bank + u % NST, NST
        return st_bank + u, U if tail else (NST, NST, None, None)[u]

    with nc.Block() as block:

        @block.sync
        def _(sp):
            def mrows(n, s):
                sp.wait_ge(m_turned, n + 1)
                sp.dma_start(m_dram[s % 2], mturn[:, s % 2, :]).then_inc(m_out, 16)
                sp.wait_ge(m_out, (n + 1) * 16)
                rows = m_dram[s % 2].rearrange("(a t) (c r) -> c t a r", a=4, r=32)
                for a in range(4):
                    sp.dma_start(q_st[MROW:MROW + PARTS, s, :].rearrange("p (t a r) -> p t a r", a=4, r=32)[:, :, a, :],
                                 rows[:, 0:SEQ_TILES, a, :]).then_inc(mrow_in, 16)

            for s in range(1, SETS):
                load_stacks(sp, s, s)
            mrows(0, 0)
            for s in range(4):
                sp.wait_ge(k.parts_stored[BATCH - 1][s], 16 * (k.layer + 1) * (2 * CHUNKS // BATCH // 4))

            def body(i, last):
                for j in range(SETS):
                    n = i * SETS + j
                    if not (last and j == SETS - 1):
                        mrows(n + 1, (j + 1) % SETS)
                    if not last:
                        sp.wait_ge(st_ready, (n + 1) * G * U)
                        load_stacks(sp, n + SETS, j)
            rounds(sp, body)

        @block.tensor
        def _(pe):
            def scores(at, u):
                s = at.s // G % SETS
                if u == 0 and at.in_head == 0:
                    if isinstance(at.n, int) and at.n == 0:
                        pe.wait_ge(k.first_in, (k.layer + 1) * 16 * 2 * SLOTS)
                    else:
                        pe.wait_ge(made[s], (at.n // SETS + (1 + before[s])) * 16 * 2 * SLOTS)
                bank = s_bank + u % NS
                if not (isinstance(at.g, int) and at.g * U + u < NS):
                    pe.wait_ge(s_used, at.g * U + (u - NS + 1))
                q, key = at.in_head, u
                pe.matmul(banks[:, bank, :], q_st[0:SROWS, s, q * P:(q + 1) * P],
                          k_st[0:SROWS, s, key * N:(key + 1) * N], start=True, stop=True).then_inc(s_ready, 1)

            def scores_t(at, u):
                s = at.s // G % SETS
                if u == 0 and at.in_head == 0:
                    pe.wait_ge(mrow_in, (at.n + 1) * 16 * 4)
                bank, ago = st_place(at, u)
                if ago is None:
                    pe.wait_ge(s_used, TOTAL * U)
                elif not (isinstance(at.g, int) and at.g * U + u < ago):
                    pe.wait_ge(exp_done, at.g * U + (u - ago + 1))
                pe.matmul(banks[:, bank, :], k_st[0:MROW + PARTS, s, at.in_head * P:(at.in_head + 1) * P],
                          q_st[0:MROW + PARTS, s, u * N:(u + 1) * N], start=True, stop=True).then_inc(st_ready, 1)

            def values(at):
                two = at.s // G % 2
                if at.in_head == 0:
                    pe.wait_ge(v_ready, at.n + 1)
                    pe.wait_ge(o_free, at.n + 1)
                pe.wait_ge(exp_done, (at.g + 1) * U)
                for u in range(U):
                    mm = pe.matmul(banks[32 * u:32 * u + 32, o_bank + two, :], v_st[:, two, at.in_head, :],
                                   probs[:, at.s % RING, u, :], start=at.in_head == 0, stop=at.in_head == G - 1)
                mm.then_inc(pv_done, 1)

            def turn(at):
                two = at.s // G % 2
                pe.wait_ge(o_copied, at.n + 1)
                for j in range(4):
                    mm = pe.transpose(banks[:, o_bank + two, j * P:(j + 1) * P], o_sb[:, two, j * P:(j + 1) * P], ident[:, :])
                mm.then_inc(o_turned, 1)

            pe.wait_ge(primed, 1)
            for g in range(S_LEAD):
                lead_st = g - (S_LEAD - ST_LEAD)
                lead_pv = g - (S_LEAD - PV_LEAD)
                if lead_pv >= 0:
                    values(At(0, lead_pv, 0))
                for stream, u in ORDER:
                    if stream == "S":
                        scores(At(0, g, 0), u)
                    elif lead_st >= 0:
                        scores_t(At(0, lead_st, 0), u)

            def body(i, last):
                for tau in range(STEPS):
                    fin, pv, st, s = (At(i, tau, lead) for lead in (0, PV_LEAD, ST_LEAD, S_LEAD))
                    if live(pv, last, PV_LEAD):
                        values(pv)
                    for stream, u in ORDER:
                        if stream == "ST" and live(st, last, ST_LEAD):
                            scores_t(st, u)
                        if stream == "S" and live(s, last, S_LEAD):
                            scores(s, u)
                    if fin.in_head == G - 1:
                        turn(fin)
            rounds(pe, body)

        @block.scalar
        def _(act):
            def exps(at):
                if not (isinstance(at.g, int) and at.g < RING):
                    act.wait_ge(pv_done, at.g - RING + 1)
                for u in range(U):
                    act.wait_ge(st_ready, at.g * U + u + 1)
                    act.activation(probs[:, at.s % RING, u, :], banks[:, st_place(at, u)[0], :], ACT.Exp,
                                   scale=scale).then_inc(exp_done, 1)

            def copy_out(at):
                two = at.s // G % 2
                act.wait_ge(pv_done, (at.n + 1) * G)
                act.activation(o_sb[:, two, :], banks[:, o_bank + two, :], ACT.Copy).then_inc(o_copied, 1)

            for g in range(ST_LEAD):
                exps(At(0, g, 0))

            def body(i, last):
                for tau in range(STEPS):
                    fin, st = At(i, tau, 0), At(i, tau, ST_LEAD)
                    if fin.in_head == G - 1:
                        copy_out(fin)
                    if live(st, last, ST_LEAD):
                        exps(st)
            rounds(act, body)

        @block.vector
        def _(dve):
            def maxima(at):
                two = at.s // G % 2
                for u in range(0, U, 2):
                    dve.wait_ge(s_ready, at.g * U + u + 2)
                    pair = banks[:, s_bank + u:s_bank + u + 2, :].rearrange("p b n -> p (b n)")
                    dve.tensor_reduce(mx[:, two, at.in_head, u // 2:u // 2 + 1], pair, AX.X, ALU.max).then_inc(s_used, 2)

            def head_maximum(at):
                two = at.s // G % 2
                dve.wait_ge(s_used, (at.n + 1) * G * U)
                dve.tensor_reduce(negm[:, two, :], mx[:, two, :, :], AX.X, ALU.max, negate=True).then_inc(mx_ready, 1)

            def turn_maximum(at):
                two = at.s // G % 2
                dve.wait_ge(m_cut, 3 * (at.n + 1))
                if not (isinstance(at.n, int) and at.n < 2):
                    dve.wait_ge(m_out, (at.n - 1) * 16)
                dve.transpose(mturn[:, two, :], mparts[:, two, :, :].rearrange("p c t -> p (c t)")).then_inc(m_turned, 1)

            def divide(at):
                two = at.s // G % 2
                dve.wait_ge(o_turned, at.n + 1)
                view = banks[:, o_bank + two, :].rearrange("p (j c r) -> p c j r", j=4, c=4)
                dve.reciprocal(rec[:, two, :, :], view[:, :, :, DH]).then_inc(o_rec, 1)
                dve.wait_ge(o_rec, at.n + 1)
                for c in range(4):
                    out = heads[:, bass.ds(at.n // HEADS, 1), 4 * c:4 * c + 4, bass.ds(at.n % HEADS, 1), :].rearrange(
                        "p b t h d -> p (b t) (h d)")
                    d = dve.tensor_tensor(out, view[:, c, :, 0:DH],
                                          rec[:, two, c, :].unsqueeze(2).to_broadcast([P, 4, DH]), ALU.mult)
                d.then_inc(o_free, 1)

            dve.memset(k.nothing[:, :], 0.0)
            dve.memset(mparts[:, :, :, :], 0.0).then_inc(m_cut2, 1)
            dve.memset(k_st[MROW:MROW + PARTS, :, :], 1.0).then_inc(primed, 1)
            dve.memset(rec[:, :, :, :], 0.0).then_inc(o_free, 2)
            for g in range(S_LEAD):
                maxima(At(0, g, 0))
                if g % G == G - 1:
                    head_maximum(At(0, g, 0))
                if g % G == 0 and g >= G:
                    turn_maximum(At(0, g - G, 0))

            def body(i, last):
                for tau in range(STEPS):
                    fin, s = At(i, tau, 0), At(i, tau, S_LEAD)
                    if live(s, last, S_LEAD):
                        maxima(s)
                        if s.in_head == G - 1:
                            head_maximum(s)
                    before = At(i, tau, S_LEAD - 1)
                    if before.in_head == G - 1 and live(before, last, S_LEAD):
                        turn_maximum(before)
                    if fin.in_head == G - 1:
                        divide(fin)
            rounds(dve, body)

        @block.gpsimd
        def _(pool):
            def stage_v(n, two):
                src = v_all[:, bass.ds(n * SEQ_TILES, SEQ_TILES), :] if not isinstance(n, int) else \
                    v_all[:, n * SEQ_TILES:(n + 1) * SEQ_TILES, :]
                pool.wait_ge(h_done, 2)
                pool.tensor_copy(v_st[:, two, :, 0:DH], src).then_inc(v_ready, 1)

            def cut_maximum(n, two):
                pool.wait_ge(m_cut2, 1)
                pool.wait_ge(mx_ready, n + 1)
                if not (isinstance(n, int) and n < 2):
                    pool.wait_ge(m_turned, n - 1)
                nothing = k.nothing[:, :]
                part = [mparts[:, two, p, 0:SEQ_TILES] for p in range(PARTS)]
                pool.tensor_tensor(part[0], negm[:, two, :], nothing, ALU.add).then_inc(m_cut, 1)
                pool.wait_ge(m_cut, 3 * n + 1)
                pool.tensor_tensor(mrest[:, two, :], negm[:, two, :], part[0], ALU.subtract).then_inc(m_cut2, 1)
                pool.wait_ge(m_cut2, n + 2)
                pool.tensor_tensor(part[1], mrest[:, two, :], nothing, ALU.add).then_inc(m_cut, 1)
                pool.wait_ge(m_cut, 3 * n + 2)
                pool.tensor_tensor(part[2], mrest[:, two, :], part[1], ALU.subtract).then_inc(m_cut, 1)

            pool.memset(v_st[:, :, :, :], 0.0).then_inc(h_done, 1)
            pool.wait_ge(h_done, 1)
            pool.memset(v_st[:, :, :, DH:DH + 1], 1.0).then_inc(h_done, 1)
            stage_v(0, 0)
            stage_v(1, 1)
            for c in range(CHUNKS):
                x = h[:, c * PER:(c + 1) * PER, :]
                pool.tensor_tensor(x, x, bo_row[:, :].unsqueeze(1).to_broadcast([P, PER, P]), ALU.add).then_inc(h_done, 1)
            cut_maximum(0, 0)

            def body(i, last):
                for j in range(SETS):
                    n = i * SETS + j
                    if not (last and j == SETS - 1):
                        cut_maximum(n + 1, (j + 1) % 2)
                    if not (last and j >= SETS - 2):
                        pool.wait_ge(pv_done, (n + 1) * G)
                        stage_v(n + 2, j % 2)
            rounds(pool, body)


def project_out(nc, k, tag, attn, wo, h, banks, ident, turned_sb):
    turned, copied, made, added = k.sem(tag + "turned"), k.sem(tag + "copied"), k.sem(tag + "made"), k.sem(tag + "added")
    with nc.Block() as block:

        @block.tensor
        def _(pe):
            def turn(c):
                if c >= 2:
                    pe.wait_ge(copied, c - 1)
                for j in range(PER):
                    mm = pe.transpose(banks[:, c % 2, j * P:(j + 1) * P], attn[:, c * PER + j, :], ident[:, :])
                mm.then_inc(turned, 1)

            def mult(c):
                pe.wait_ge(copied, c + 1)
                if c >= 2:
                    pe.wait_ge(added, c - 1)
                for j in range(PER):
                    mm = pe.matmul(banks[:, 2 + c % 2, j * P:(j + 1) * P], turned_sb[:, c % 2, j * P:(j + 1) * P],
                                   wo, start=True, stop=True)
                mm.then_inc(made, 1)

            turn(0)
            for c in range(CHUNKS):
                if c + 1 < CHUNKS:
                    turn(c + 1)
                mult(c)

        @block.scalar
        def _(act):
            for c in range(CHUNKS):
                act.wait_ge(turned, c + 1)
                if c >= 2:
                    act.wait_ge(made, c - 1)
                act.activation(turned_sb[:, c % 2, :], banks[:, c % 2, :], ACT.Copy).then_inc(copied, 1)

        @block.vector
        def _(dve):
            for c in range(CHUNKS):
                dve.wait_ge(made, c + 1)
                x = h[:, c * PER:(c + 1) * PER, :]
                dve.tensor_tensor(x, banks[:, 2 + c % 2, :].rearrange("p (t d) -> p t d", t=PER), x,
                                  ALU.add).then_inc(added, 1)


def route(nc, k, tag, offset_row, all_experts, banks, weights, ident, weights_t, blank_slots=None):
    logits, shifted, ex, pick, score, sel1 = (k.route[:, i, :, :] for i in range(6))
    both = logits
    top, den = k.top[:, :], k.den[:, :]
    step, ex_ready = k.sem(tag + "step"), k.sem(tag + "ex")
    shift_ready, w_ready, turned, copied = k.sem(tag + "shift"), k.sem(tag + "w"), k.sem(tag + "turned"), k.sem(tag + "copied")

    def wide(x):
        return x.unsqueeze(2).to_broadcast([P, TILES, E])

    with nc.Block() as block:

        @block.tensor
        def _(pe):
            if weights_t is not None:
                pe.wait_ge(w_ready, 1)
            for c in range(CHUNKS if weights_t is not None else 0):
                if c >= 2:
                    pe.wait_ge(copied, c - 1)
                for j in range(PER):
                    mm = pe.transpose(banks[0:E, 1 + c % 2, j * P:(j + 1) * P], weights[:, c * PER + j, :], ident[:, :])
                mm.then_inc(turned, 1)

        @block.scalar
        def _(act):
            act.wait_ge(shift_ready, 1)
            act.activation(ex, shifted, ACT.Exp).then_inc(ex_ready, 1)
            for c in range(CHUNKS if weights_t is not None else 0):
                act.wait_ge(turned, c + 1)
                act.activation(weights_t[:, c * N:(c + 1) * N], banks[0:E, 1 + c % 2, :], ACT.Copy).then_inc(copied, 1)

        @block.vector
        def _(dve):
            n = [0]

            def then(ins):
                n[0] += 1
                ins.then_inc(step, 1)
                dve.wait_ge(step, n[0])

            then(dve.tensor_tensor(logits, banks[:, 4, 0:TILES * E].rearrange("p (t e) -> p t e", e=E),
                                   offset_row.unsqueeze(1).to_broadcast([P, TILES, E]), ALU.add))
            then(dve.tensor_reduce(top, logits, AX.X, ALU.max))
            then(dve.tensor_tensor(shifted, logits, wide(top), ALU.subtract))
            dve.tensor_scalar(pick, shifted, 0.0, None, ALU.is_ge).then_inc(shift_ready, 1)
            dve.wait_ge(shift_ready, 1)
            rank = k.rank[:, :].unsqueeze(1).to_broadcast([P, TILES, E])
            then(dve.tensor_tensor(score, pick, rank, ALU.mult))
            then(dve.tensor_reduce(top, score, AX.X, ALU.max))
            then(dve.tensor_tensor(sel1, score, wide(top), ALU.is_equal))
            then(dve.scalar_tensor_tensor(logits, sel1, -BIG, shifted, ALU.mult, ALU.add))
            then(dve.tensor_reduce(top, logits, AX.X, ALU.max))
            then(dve.tensor_tensor(pick, logits, wide(top), ALU.is_equal))
            then(dve.tensor_tensor(score, pick, rank, ALU.mult))
            then(dve.tensor_reduce(top, score, AX.X, ALU.max))
            then(dve.tensor_tensor(pick, score, wide(top), ALU.is_equal))
            then(dve.tensor_tensor(both, sel1, pick, ALU.add))
            dve.wait_ge(ex_ready, 1)
            then(dve.tensor_tensor(score, both, ex, ALU.mult))
            then(dve.tensor_reduce(den, ex if all_experts else score, AX.X, ALU.add))
            then(dve.reciprocal(top, den))
            dve.tensor_tensor(weights[:, :, :], score, wide(top), ALU.mult).then_inc(w_ready, 1)

        if blank_slots is not None:
            slots_dram, rows_sb = blank_slots
            zeroed = k.sem(tag + "zeroed")

            @block.gpsimd
            def _(pool):
                pool.memset(rows_sb[:, :, :], 0.0).then_inc(zeroed, 1)
                pool.wait_ge(zeroed, 1)
                pool.tensor_copy(rows_sb[:, :, D:D + 1], k.pad_dst.unsqueeze(2)).then_inc(zeroed, 1)

            @block.sync
            def _(sp):
                sp.wait_ge(zeroed, 2)
                sp.dma_start(slots_dram.rearrange("(p j) c -> p j c", p=P), rows_sb[:, :, :]).then_inc(k.slots_blank, 16)


def mixture_constants(k, ins, w16, expert_b, beta_w, banks, loaded):
    mean, mean_wide, mean_diag, sixteenth = k.ins_mean, k.mean_wide, k.mean_diag, k.sixteenth
    set_, mean_made, mean_out, wide_ready, made, done = (k.sem("c_" + s) for s in ("set", "mean", "mean_out", "wide", "made", "done"))

    def vector(dve):
        dve.memset(sixteenth[:, :], 1.0 / 16).then_inc(set_, 1)
        dve.memset(mean_diag[:, :, :], 0.0).then_inc(set_, 1)
        dve.memset(mean_wide[:, :], 1.0).then_inc(set_, 1)
        for e in range(E):
            dve.memset(k.rank[:, e:e + 1], float(E - e))
        dve.memset(k.ones[:, :], 1.0)
        dve.wait_ge(mean_made, 1)
        dve.tensor_copy(mean[:, :], banks[:, 4, 0:1]).then_inc(mean_out, 1)
        dve.wait_ge(mean_out, 1)
        dve.wait_ge(set_, 3)
        dve.tensor_scalar(mean_wide[:, :], mean_wide[:, :], mean[:, :], None, ALU.mult).then_inc(wide_ready, 1)
        for e in range(E):
            dve.tensor_copy(mean_diag[:, e, e:e + 1], mean[:, :]).then_inc(wide_ready, 1)
        dve.wait_ge(made, 3)
        dve.tensor_copy(k.gamma_router[:, :], banks[:, 5, 0:2 * E]).then_inc(done, 1)
        dve.tensor_copy(k.gamma_col[:, :], banks[0:E, 6, 0:1]).then_inc(done, 1)
        dve.wait_ge(done, 2)
        dve.scalar_tensor_tensor(k.offsets[:, :], expert_b, k.gamma_col[:, :], banks[0:E, 7, 0:D],
                                 ALU.mult, ALU.add).then_inc(done, 1)

    def tensor(pe):
        pe.wait_ge(set_, 1)
        pe.wait_ge(*loaded)
        pe.matmul(banks[:, 4, 0:1], ins, sixteenth[:, :], start=True, stop=True).then_inc(mean_made, 1)
        pe.wait_ge(wide_ready, 1 + E)
        pe.matmul(banks[:, 5, 0:2 * E], mean_wide[:, :], w16, start=True, stop=True).then_inc(made, 1)
        pe.matmul(banks[0:E, 6, 0:1], w16[:, 0:E], mean[:, :], start=True, stop=True).then_inc(made, 1)
        for e in range(E):
            mm = pe.matmul(banks[0:E, 7, 0:D], mean_diag[:, e, :], beta_w[:, e, :], start=e == 0, stop=e == E - 1)
        mm.then_inc(made, 1)

    return {"vector": vector, "tensor": tensor}


def mix_linear(nc, k, xT, expert_w, comb, comb_t, offsets, h, banks, scaled_sb, half_sum):
    made, offset_made, off_done, taken = k.sem("l_made"), k.sem("l_offset"), k.sem("l_offdone"), k.sem("l_taken")
    cg_ready, scaled, paired, summed, added = (k.sem("l_" + s) for s in ("cg", "scaled", "paired", "summed", "added"))
    cg = k.route[:, 0, :, :]
    EH = E // 2
    SLOT = 3
    with nc.Block() as block:

        @block.tensor
        def _(pe):
            for t in range(TILES):
                if t % PER == 0:
                    c = t // PER
                    if c >= 2:
                        pe.wait_ge(off_done, c - 1)
                    for j in range(PER):
                        mm = pe.matmul(banks[:, 6 + c % 2, j * P:(j + 1) * P], comb_t[:, (t + j) * P:(t + j + 1) * P],
                                       offsets, start=True, stop=True)
                    mm.then_inc(offset_made, 1)
                for half in range(2):
                    if t >= SLOT:
                        pe.wait_ge((taken, scaled)[half], (t - SLOT + 1) * EH)
                    pe.matmul(banks[:, 2 * (t % SLOT) + half, :], xT[:, t * P:(t + 1) * P],
                              expert_w[:, half * N:(half + 1) * N], start=True, stop=True).then_inc(made, 1)

        @block.scalar
        def _(act):
            act.wait_ge(cg_ready, 1)
            for t in range(TILES):
                act.wait_ge(made, 2 * t + 2)
                if t >= 2:
                    act.wait_ge(paired, t - 1)
                for e in range(EH):
                    act.activation(scaled_sb[:, t % 2, e, :], banks[:, 2 * (t % SLOT) + 1, e * D:(e + 1) * D], ACT.Copy,
                                   scale=cg[:, t, EH + e:EH + e + 1]).then_inc(scaled, 1)

        @block.gpsimd
        def _(pool):
            for t in range(TILES):
                pool.wait_ge(scaled, (t + 1) * EH)
                if t >= 2:
                    pool.wait_ge(added, t - 1)
                pairs = scaled_sb[:, t % 2, :, :]
                pool.tensor_tensor(half_sum[:, t % 2, :, :], pairs[:, 0:2, :], pairs[:, 2:4, :], ALU.add).then_inc(paired, 1)
                pool.wait_ge(paired, t + 1)
                pool.tensor_tensor(half_sum[:, t % 2, 0, :], half_sum[:, t % 2, 0, :], half_sum[:, t % 2, 1, :],
                                   ALU.add).then_inc(summed, 1)

        @block.vector
        def _(dve):
            def add_sum(t):
                dve.wait_ge(summed, t + 1)
                dve.wait_ge(taken, (t + 1) * EH)
                dve.tensor_tensor(h[:, t, :], h[:, t, :], half_sum[:, t % 2, 0, :], ALU.add).then_inc(added, 1)

            dve.tensor_tensor(cg, comb[:, :, :], k.gamma_router[:, 0:E].unsqueeze(1).to_broadcast([P, TILES, E]),
                              ALU.mult).then_inc(cg_ready, 1)
            dve.wait_ge(cg_ready, 1)
            for t in range(TILES):
                if t % PER == 0:
                    c = t // PER
                    dve.wait_ge(offset_made, c + 1)
                    x = h[:, t:t + PER, :]
                    dve.tensor_tensor(x, banks[:, 6 + c % 2, :].rearrange("p (t d) -> p t d", t=PER), x,
                                      ALU.add).then_inc(off_done, 1)
                    dve.wait_ge(off_done, c + 1)
                dve.wait_ge(made, 2 * t + 1)
                for e in range(EH):
                    if e:
                        dve.wait_ge(taken, t * EH + e)
                    dve.scalar_tensor_tensor(h[:, t, :], banks[:, 2 * (t % SLOT), e * D:(e + 1) * D],
                                             cg[:, t, e:e + 1], h[:, t, :], ALU.mult, ALU.add).then_inc(taken, 1)
                if t:
                    add_sum(t - 1)
            add_sum(TILES - 1)


class SortedTile:

    def __init__(self, i, first):
        self.i, self.first, self.slot = i, first, first % 4

    def index(self, add=0):
        return self.i * 4 + (self.first + add)

    def use(self, add=0):
        return self.i + (self.first // 4 + add)

    def after(self, n):
        return SortedTile(self.i, self.first + n)

    def known(self, limit):
        return not isinstance(self.i, int) or self.i * 4 + self.first < limit


def sorted_tiles(eng, body):
    for first in range(4):
        body(SortedTile(0, first))
    passes = (SORTED_TILES - 4 - 1) // 4
    with eng.Fori(0, passes) as i:
        for first in range(4, 8):
            body(SortedTile(i, first))
    for first in range(4 + 4 * passes, SORTED_TILES):
        body(SortedTile(0, first))


def mix_mlp(nc, k, rows_sb, slots_dram, y_dram, experts, b2, gain, bias, gates, gates_t, y, h, out, banks, ident, bufs):
    weight_ring, row_ring, zt_ring, hid, y_ring, best_y, second_y, chunk_hid, chunk_x = bufs
    both, second, best = (k.route[:, i, 0:SENT, :] for i in (0, 3, 5))
    ids, slot_ids, expert_rows = k.dst_ids, k.slot_ids, k.expert_rows
    step, row_sums, counts_made = k.sem("m_step"), k.sem("m_row_sums"), k.sem("m_counts")
    experts_known, slots_known, doubled, sent = (k.sem("m_" + n) for n in ("experts", "slots", "doubled", "sent"))
    turned, gates_out, off_made, off_done = (k.sem("m_" + n) for n in ("g_turned", "g_out", "offset", "off_done"))
    base, gate_ready = k.sem("m_base"), k.sem("m_gate")
    row_in, w_in, y_out = ([k.sem(f"m_{n}{s}") for s in range(4)] for n in ("row_in", "w_in", "y_out"))
    z_turned, z_copied, up, act_done, down, y_copied = (k.sem("m_" + n) for n in ("z_turned", "z_copied", "up", "gelu", "down", "y_copied"))
    best_in, second_in = ([k.sem(f"m_{n}{g}") for g in range(SENT // PER)] for n in ("best_in", "second_in"))
    settled = [k.sem(f"m_settled{i}") for i in range(2)]
    best_scaled, best_added = k.sem("m_best_scaled"), k.sem("m_best_added")
    added, stored = k.sem("m_added"), k.sem("m_stored")
    tokens = out.rearrange("b (t p) d -> p (b t) d", p=P)
    slot_rows = slots_dram.rearrange("(s f p) c -> p s f c", p=P, f=ROWS // P)
    token_rows = y_dram[0:BEST * TOKENS, :].rearrange("(w t p) d -> p w t d", p=P, w=BEST)
    chunk_w = [k.sem(f"m_chunk_w{s}") for s in range(4)]
    chunk_up, chunk_gelu, chunk_down, chunk_taken = (k.sem("m_chunk_" + n) for n in ("up", "gelu", "down", "taken"))
    FINAL = PER
    HALVES = ROWS // P

    def used(s):
        return (SORTED_TILES - s + 3) // 4

    with nc.Block() as block:

        @block.vector
        def _(dve):
            n = [0]

            def then(ins):
                n[0] += 1
                ins.then_inc(step, 1)
                dve.wait_ge(step, n[0])

            row_sum, at, tiles, end = (k.small[:, i, :] for i in range(4))
            dve.tensor_reduce(row_sum, both.rearrange("p t e -> p e t"), AX.X, ALU.add).then_inc(row_sums, 1)
            old, new, spare = both, k.route[:, 1, 0:SENT, :], k.route[:, 4, 0:SENT, :]
            reach = 1
            while reach < SENT:
                dve.tensor_copy(new[:, 0:reach, :], old[:, 0:reach, :]).then_inc(step, 1)
                n[0] += 1
                then(dve.tensor_tensor(new[:, reach:, :], old[:, reach:, :], old[:, 0:SENT - reach, :], ALU.add))
                old, new, spare = new, spare, new
                reach *= 2
            upto = old
            dve.wait_ge(counts_made, 1)
            steps = k.count_steps.unsqueeze(1).to_broadcast([P, E, COUNT_STEPS])
            then(dve.tensor_tensor(k.over[:, :, :], banks[:, 0, E:2 * E].unsqueeze(2).to_broadcast([P, E, COUNT_STEPS]),
                                   steps, ALU.is_gt))
            then(dve.tensor_reduce(tiles, k.over[:, :, :], AX.X, ALU.add))
            then(dve.tensor_copy(end[:, 0:1], tiles[:, 0:1]))
            for e in range(1, E):
                then(dve.tensor_tensor(end[:, e:e + 1], end[:, e - 1:e], tiles[:, e:e + 1], ALU.add))
            ends = end[:, 0:E - 1].unsqueeze(1).to_broadcast([P, SORTED_TILES, E - 1])
            then(dve.tensor_tensor(k.past[:, :, :], k.tile_index.unsqueeze(2).to_broadcast([P, SORTED_TILES, E - 1]),
                                   ends, ALU.is_ge))
            then(dve.tensor_reduce(k.tile_expert[:, :], k.past[:, :, :], AX.X, ALU.add))
            then(dve.tensor_scalar(k.tile_expert[:, :], k.tile_expert[:, :], float(P), k.partition, ALU.mult, ALU.add))
            dve.tensor_copy(expert_rows[:, 0:3], k.tile_expert[:, 0:3]).then_inc(experts_known, 1)
            then(dve.tensor_tensor(at, end, tiles, ALU.subtract))
            then(dve.tensor_scalar(at, at, float(ROWS), -1.0, ALU.mult, ALU.add))
            then(dve.tensor_tensor(at, at, banks[:, 0, 0:E], ALU.add))
            then(dve.tensor_tensor(upto, upto, at.unsqueeze(1).to_broadcast([P, SENT, E]), ALU.add))
            for which, mask in enumerate((best, second)):
                then(dve.tensor_tensor(new, upto, mask, ALU.mult))
                then(dve.tensor_reduce(k.slot_of[:, which, :], new, AX.X, ALU.add))
            dve.tensor_copy(slot_ids[:, :, :], k.slot_of[:, :, :]).then_inc(slots_known, 1)
            for which, mask in enumerate((best, second)):
                then(dve.tensor_tensor(new, gates[:, 0:SENT, :], mask, ALU.mult))
                then(dve.tensor_reduce(k.gate_of[:, which, :], new, AX.X, ALU.add))
            for c in range(CHUNKS):
                dve.wait_ge(off_made, c + 1)
                x = h[:, c * PER:(c + 1) * PER, :]
                dve.tensor_tensor(x, x, y[:, c * PER:(c + 1) * PER, :], ALU.add).then_inc(base, 1)
                dve.wait_ge(base, c + 1)
                dve.tensor_tensor(x, banks[:, 4 + c % 2, :].rearrange("p (t d) -> p t d", t=PER), x,
                                  ALU.add).then_inc(off_done, 1)

            dve.wait_ge(off_done, CHUNKS)
            for e in range(E):
                dve.wait_ge(chunk_down, e + 1)
                for j in range(PER):
                    if e:
                        dve.wait_ge(chunk_taken, (e - 1) * PER + j + 1)
                    dve.scalar_tensor_tensor(h[:, SENT + j, :], banks[:, 6 + e % 2, j * P:(j + 1) * P],
                                             gates[:, SENT + j, e:e + 1], h[:, SENT + j, :], ALU.mult, ALU.add).then_inc(chunk_taken, 1)

            def z_out(tile):
                dve.wait_ge(z_turned, tile.index(1))
                dve.tensor_scalar(zt_ring[:, tile.slot, :], banks[:, tile.first % 2, 0:ROWS], gain, bias, ALU.mult,
                                  ALU.add).then_inc(z_copied, 1)

            def body(tile):
                if tile.after(2).known(SORTED_TILES):
                    z_out(tile.after(2))
                ahead = tile.after(3)
                if ahead.known(SORTED_TILES):
                    if isinstance(tile.i, int):
                        rows = k.tile_expert[:, ahead.first:ahead.first + 1]
                    else:
                        rows = k.tile_expert[:, bass.ds(ahead.index(), 1)]
                    dve.tensor_copy(expert_rows[:, ahead.slot:ahead.slot + 1], rows).then_inc(experts_known, 1)
                if tile.first >= 4:
                    dve.wait_ge(y_out[tile.slot], tile.use() * (16 * HALVES))
                dve.wait_ge(down, tile.index(1))
                dve.tensor_copy(ids[:, tile.slot, :], row_ring[:, tile.slot, :, D:D + 1].rearrange("p f c -> p (f c)")).then_inc(y_copied, 1)
                dve.tensor_copy(y_ring[:, tile.slot, :], banks[:, 6 + tile.first % 2, 0:ROWS]).then_inc(y_copied, 1)

            z_out(SortedTile(0, 0))
            z_out(SortedTile(0, 1))
            sorted_tiles(dve, body)
            for g in range(SENT // FINAL):
                dve.wait_ge(second_in[g], 16)
                for t in range(g * FINAL, (g + 1) * FINAL):
                    if t % PER == 0:
                        dve.wait_ge(best_added, t // PER + 1)
                    dve.scalar_tensor_tensor(h[:, t, :], second_y[:, t, :], k.gate_of[:, 1, t:t + 1], h[:, t, :],
                                             ALU.mult, ALU.add).then_inc(added, 1)

        @block.tensor
        def _(pe):
            pe.wait_ge(row_sums, 1)
            pe.matmul(banks[:, 0, 0:E], k.lower, k.small[:, 0, :], start=True, stop=True)
            pe.matmul(banks[:, 0, E:2 * E], k.ones[:, :], k.small[:, 0, :], start=True, stop=True).then_inc(counts_made, 1)

            def offsets(c):
                pe.wait_ge(gates_out, c + 1)
                if c >= 2:
                    pe.wait_ge(off_done, c - 1)
                for j in range(PER):
                    t = c * PER + j
                    mm = pe.matmul(banks[:, 4 + c % 2, j * P:(j + 1) * P], gates_t[:, t * P:(t + 1) * P], b2,
                                   start=True, stop=True)
                mm.then_inc(off_made, 1)

            for c in range(CHUNKS):
                if c >= 2:
                    pe.wait_ge(gates_out, c - 1)
                for j in range(PER):
                    mm = pe.transpose(banks[0:E, 2 + c % 2, j * P:(j + 1) * P], gates[:, c * PER + j, :], ident[:, :])
                mm.then_inc(turned, 1)
                if c:
                    offsets(c - 1)
            offsets(CHUNKS - 1)
            pe.wait_ge(slots_known, 1)
            pe.wait_ge(off_done, CHUNKS)

            def chunk_project_up(e):
                pe.wait_ge(chunk_w[e % 4], 16 * (e // 4 + 1))
                for f in range(FC):
                    u = e * FC + f
                    if u >= 4:
                        pe.wait_ge(chunk_gelu, u - 3)
                    pe.matmul(banks[:, u % 4, :], weight_ring[e % 4][:, f * P:(f + 1) * P], chunk_x, start=True,
                              stop=True).then_inc(chunk_up, 1)

            chunk_project_up(0)
            for e in range(E):
                if e + 1 < E:
                    chunk_project_up(e + 1)
                pe.wait_ge(chunk_gelu, (e + 1) * FC)
                if e >= 2:
                    pe.wait_ge(chunk_taken, (e - 1) * PER)
                w2 = weight_ring[e % 4][:, FF:2 * FF]
                for j in range(PER):
                    for f in range(FC):
                        mm = pe.matmul(banks[:, 6 + e % 2, j * P:(j + 1) * P], chunk_hid[:, e % 2, f, j * P:(j + 1) * P],
                                       w2[:, f * D:(f + 1) * D], start=f == 0, stop=f == FC - 1)
                mm.then_inc(chunk_down, 1)
            pe.wait_ge(chunk_taken, E * PER)

            def turn(tile):
                pe.wait_ge(row_in[tile.slot], tile.use(1) * 16)
                for f in range(HALVES):
                    mm = pe.transpose(banks[:, tile.first % 2, f * P:(f + 1) * P], row_ring[:, tile.slot, f, 0:D], ident[:, :])
                mm.then_inc(z_turned, 1)

            def project_up(tile):
                pe.wait_ge(w_in[tile.slot], tile.use(1) * 16)
                pe.wait_ge(z_copied, tile.index(1))
                w1 = weight_ring[tile.slot]
                for f in range(FC):
                    mm = pe.matmul(banks[:, 2 + tile.first % 2 * 2 + f // 2, f % 2 * ROWS:(f % 2 + 1) * ROWS],
                                   w1[:, f * P:(f + 1) * P], zt_ring[:, tile.slot, :], start=True, stop=True)
                    if f % 2:
                        mm.then_inc(up, 1)

            def project_down(tile):
                pe.wait_ge(act_done, tile.index(1) * FC)
                if tile.first >= 2:
                    pe.wait_ge(y_copied, tile.index(-1) * 2)
                w2 = weight_ring[tile.slot][:, FF:2 * FF]
                for half in range(HALVES):
                    for f in range(FC):
                        mm = pe.matmul(banks[:, 6 + tile.first % 2, half * P:(half + 1) * P],
                                       hid[:, tile.first % 2, f, half * P:(half + 1) * P], w2[:, f * D:(f + 1) * D],
                                       start=f == 0, stop=f == FC - 1)
                mm.then_inc(down, 1)

            def body(tile):
                if tile.after(2).known(SORTED_TILES):
                    turn(tile.after(2))
                if tile.after(1).known(SORTED_TILES):
                    project_up(tile.after(1))
                project_down(tile)

            turn(SortedTile(0, 0))
            turn(SortedTile(0, 1))
            project_up(SortedTile(0, 0))
            sorted_tiles(pe, body)

        @block.scalar
        def _(act):
            for c in range(SENT // PER):
                s = slice(c * PER, (c + 1) * PER)
                act.activation(rows_sb[:, SENT + c * PER:SENT + (c + 1) * PER, 0:D], rows_sb[:, s, 0:D], ACT.Copy).then_inc(doubled, 1)
            for c in range(CHUNKS):
                act.wait_ge(turned, c + 1)
                act.activation(gates_t[:, c * N:(c + 1) * N], banks[0:E, 2 + c % 2, :], ACT.Copy).then_inc(gates_out, 1)
            for e in range(E):
                if e >= 2:
                    act.wait_ge(chunk_down, e - 1)
                for f in range(FC):
                    act.wait_ge(chunk_up, e * FC + f + 1)
                    act.activation(chunk_hid[:, e % 2, f, :], banks[:, (e * FC + f) % 4, :], ACT.Gelu,
                                   bias=weight_ring[e % 4][:, 2 * FF + f:2 * FF + f + 1]).then_inc(chunk_gelu, 1)

            def body(tile):
                if tile.first >= 2:
                    act.wait_ge(down, tile.index(-1))
                for f in range(FC):
                    if f % 2 == 0:
                        act.wait_ge(up, tile.index() * (FC // 2) + (f // 2 + 1))
                    act.activation(hid[:, tile.first % 2, f, :],
                                   banks[:, 2 + tile.first % 2 * 2 + f // 2, f % 2 * ROWS:(f % 2 + 1) * ROWS], ACT.Gelu,
                                   bias=weight_ring[tile.slot][:, 2 * FF + f:2 * FF + f + 1]).then_inc(act_done, 1)

            sorted_tiles(act, body)
            for t in range(SENT):
                if t % FINAL == 0:
                    act.wait_ge(best_in[t // FINAL], 16)
                act.activation(best_y[:, t, :], best_y[:, t, :], ACT.Copy, scale=k.gate_of[:, 0, t:t + 1]).then_inc(best_scaled, 1)

        @block.gpsimd
        def _(pool):
            def settle(which, tile):
                if tile.first >= 1:
                    pool.wait_ge(settled[which], tile.index())
                pool.tensor_tensor(k.held[:, which:which + 1], k.nothing[:, 0:1], k.nothing[:, 0:1], ALU.add).then_inc(settled[which], 1)

            def weights_of(tile):
                rows = expert_rows[:, tile.slot:tile.slot + 1]
                pool.indirect_dma_start(weight_ring[tile.slot], None, experts[:, :],
                                        bass.IndirectOffsetOnAxis(ap=rows, axis=0)).then_inc(w_in[tile.slot], 16)

            for which in range(BEST):
                pool.tensor_copy(rows_sb[:, which * SENT:(which + 1) * SENT, D:D + 1],
                                 k.token_dst[:, which * TILES:which * TILES + SENT].unsqueeze(2)).then_inc(doubled, 1)
            pool.wait_ge(slots_known, 1)
            pool.wait_ge(doubled, BEST + SENT // PER)
            pool.wait_ge(k.slots_blank, 16)
            for t in range(SENT):
                for which in range(BEST):
                    pool.indirect_dma_start(slots_dram[:, :], bass.IndirectOffsetOnAxis(ap=slot_ids[:, which, t:t + 1], axis=0),
                                            rows_sb[:, which * SENT + t, :], None).then_inc(sent, 16)
            pool.wait_ge(experts_known, 1)
            for first in range(3):
                pool.wait_ge(chunk_down, E - 4 + first + 1)
                weights_of(SortedTile(0, first))

            def send_back(tile):
                pool.wait_ge(y_copied, tile.index(1) * 2)
                settle(1, tile)
                for half in range(HALVES):
                    pool.indirect_dma_start(y_dram[:, :], bass.IndirectOffsetOnAxis(ap=ids[:, tile.slot, half:half + 1], axis=0),
                                            y_ring[:, tile.slot, half * P:(half + 1) * P], None).then_inc(y_out[tile.slot], 16)

            def body(tile):
                if tile.after(3).known(SORTED_TILES):
                    if tile.first >= 1:
                        pool.wait_ge(down, tile.index())
                    pool.wait_ge(experts_known, tile.index(2))
                    settle(0, tile)
                    weights_of(tile.after(3))
                if tile.first >= 1:
                    send_back(tile.after(-1))

            sorted_tiles(pool, body)
            send_back(SortedTile(0, SORTED_TILES - 1))
            pool.wait_ge(off_done, CHUNKS)
            for c in range(SENT // PER):
                pool.wait_ge(best_scaled, (c + 1) * PER)
                x = h[:, c * PER:(c + 1) * PER, :]
                pool.tensor_tensor(x, x, best_y[:, c * PER:(c + 1) * PER, :], ALU.add).then_inc(best_added, 1)

        @block.sync
        def _(sp):
            for e in range(E):
                if e >= 4:
                    sp.wait_ge(chunk_down, e - 3)
                sp.dma_start(weight_ring[e % 4], experts[e * P:(e + 1) * P, :]).then_inc(chunk_w[e % 4], 16)
            sp.wait_ge(sent, 16 * BEST * SENT)

            def body(tile):
                if tile.first >= 4:
                    sp.wait_ge(y_copied, tile.index(-3) * 2)
                if isinstance(tile.i, int):
                    rows = slot_rows[:, tile.first, :, :]
                else:
                    rows = slot_rows[:, bass.ds(tile.index(), 1), :, :].rearrange("p s f c -> p (s f) c")
                sp.dma_start(row_ring[:, tile.slot, :, :], rows).then_inc(row_in[tile.slot], 16)

            sorted_tiles(sp, body)
            sp.wait_ge(chunk_taken, E * PER)
            sp.dma_start(tokens[:, SENT:TILES, :], h[:, SENT:TILES, :]).then_inc(stored, 16)
            for s in range(4):
                sp.wait_ge(y_out[s], 16 * HALVES * used(s))
            for g in range(SENT // FINAL):
                s = slice(g * FINAL, (g + 1) * FINAL)
                sp.dma_start(best_y[:, s, :], token_rows[:, 0, s, :]).then_inc(best_in[g], 16)
                sp.dma_start(second_y[:, s, :], token_rows[:, 1, s, :]).then_inc(second_in[g], 16)
            for g in range(SENT // FINAL):
                s = slice(g * FINAL, (g + 1) * FINAL)
                sp.wait_ge(added, (g + 1) * FINAL)
                sp.dma_start(tokens[:, s, :], h[:, s, :]).then_inc(stored, 16)
            sp.wait_ge(stored, 16 * (SENT // FINAL + 1))


def program(nc, ids, table, attn_w, attn_b, bv, bo, ins, gate_w, expert_w, expert_b, gamma_rmod, beta_w,
            ln_gb, w_r, b_r, experts, b2, shape_consts, out):
    with ExitStack() as ctx:
        k = Kit(nc, ctx)
        h, y = k.sbuf("h", [P, TILES, D]), k.sbuf("y", [P, TILES, D])
        xT = k.sbuf("xT", [P, TILES * P])
        v_all, attn = k.sbuf("v_all", [P, BH * SEQ_TILES, DH]), k.sbuf("attn", [P, TILES, D])
        q_st, k_st = k.sbuf("q_st", [P, 4, SEQ], BF16), k.sbuf("k_st", [P, 4, SEQ], BF16)
        probs = k.sbuf("probs", [P, 2, 4, N])
        v_st, o_sb = k.sbuf("v_st", [P, 2, SEQ_TILES, 32]), k.sbuf("o_sb", [P, 2, N])
        ident = k.sbuf("ident", [P, P])
        k.stats, k.mv = k.sbuf("stats", [P, TILES, 6]), k.sbuf("mv", [P, TILES, 2])
        k.std, k.rstd, k.shift = (k.sbuf(name, [P, TILES]) for name in ("std", "rstd", "shift"))
        k.ids, k.ids_in, k.blank = k.sbuf("ids", [P, TILES], I32), k.lasting_sem("ids_in"), k.lasting_sem("blank")
        k.mx, k.negm, k.mrest = k.sbuf("mx", [P, 2, SEQ_TILES, 2]), k.sbuf("negm", [P, 2, SEQ_TILES]), k.sbuf("mrest", [P, 2, SEQ_TILES])
        k.mparts, k.mturn = k.sbuf("mparts", [P, 2, PARTS, 32], BF16), k.sbuf("mturn", [P, 2, PARTS * 32], BF16)
        k.held = k.sbuf("held", [P, 2])
        k.nothing = k.sbuf("nothing", [P, SEQ_TILES])
        k.rec = k.sbuf("rec", [P, 2, 4, 4])
        k.route = k.sbuf("route", [P, 6, TILES, E])
        k.top, k.den, k.rank = k.sbuf("top", [P, TILES]), k.sbuf("den", [P, TILES]), k.sbuf("rank", [P, E])
        weights = k.sbuf("weights", [P, TILES, E])
        w_sb, b_sb = k.sbuf("w_sb", [P, 2, 4, D]), k.sbuf("b_sb", [P, 2, 2])
        bv_row, bo_row = k.sbuf("bv_row", [P, 2, D]), k.sbuf("bo_row", [P, 2, D])
        ins_sb, w16 = k.sbuf("ins_sb", [16, D]), k.sbuf("w16", [P, 2 * E])
        router = k.sbuf("router", [P, 2, E])
        eb_sb, br_row, b2_sb = k.sbuf("eb_sb", [E, D]), k.sbuf("br_row", [P, E]), k.sbuf("b2_sb", [E, D])
        ln_sb = k.sbuf("ln_sb", [P, 2])
        k.ins_mean, k.mean_wide, k.mean_diag = k.sbuf("ins_mean", [P, 1]), k.sbuf("mean_wide", [P, P]), k.sbuf("mean_diag", [P, E, E])
        k.sixteenth, k.gamma_router = k.sbuf("sixteenth", [16, 1]), k.sbuf("gamma_router", [P, 2 * E])
        k.gamma_col, k.offsets = k.sbuf("gamma_col", [E, 1]), k.sbuf("offsets", [E, D])
        ew_sb = k.sbuf("ew_sb", [P, E * D])
        rows_sb = k.sbuf("rows_sb", [P, PER_PART, D + 1])
        consts = k.sbuf("consts", [P, shape_consts.shape[1]])
        widths = (P, COUNT_STEPS, SORTED_TILES, 1, BEST * TILES, PER_PART)
        starts = [sum(widths[:i]) for i in range(len(widths))]
        k.lower, k.count_steps, k.tile_index, k.partition, k.token_dst, k.pad_dst = (
            consts[:, a:a + w] for a, w in zip(starts, widths))
        k.ones, k.small, k.over = k.sbuf("ones", [P, P]), k.sbuf("small", [P, 4, E]), k.sbuf("over", [P, E, COUNT_STEPS])
        k.past, k.tile_expert = k.sbuf("past", [P, SORTED_TILES, E - 1]), k.sbuf("tile_expert", [P, SORTED_TILES])
        k.expert_rows, k.slot_ids = k.sbuf("expert_rows", [P, 4], I32), k.sbuf("slot_ids", [P, BEST, SENT], I32)
        k.slot_of, k.gate_of = k.sbuf("slot_of", [P, BEST, SENT]), k.sbuf("gate_of", [P, BEST, SENT])
        k.dst_ids, k.slots_blank = k.sbuf("dst_ids", [P, 4, ROWS // P], I32), k.lasting_sem("slots_blank")
        banks = ctx.enter_context(nc.psum_tensor("banks", [P, 8, N], F32))
        m_dram = nc.dram_tensor("m_rows", [2, P, PARTS * 32], BF16).ap()
        parts_dram = nc.dram_tensor("qk_parts", [2, PARTS, BATCH * P, SEQ], BF16).ap()
        slots_dram = nc.dram_tensor("slots", [SORTED_TILES * ROWS, D + 1], F32).ap()
        y_dram = nc.dram_tensor("expert_rows_out", [BEST * TOKENS + SORTED_TILES * ROWS, D], F32).ap()

        rows_flat = rows_sb[:, :, :].rearrange("p j c -> p (j c)")
        part_ring = rows_flat[:, 0:4 * PARTS * N // 2].bitcast(BF16).rearrange("p (r s n) -> p r s n", r=4, s=PARTS)
        load_stacks = stack_loader(k, parts_dram, q_st, k_st)
        rest_ring = probs[:, 0, :, :]
        beta_sb = probs[:, :, :, :].rearrange("p a b n -> p (a b n)")[:, 0:E * D].rearrange("p (e d) -> p e d", e=E)
        wt = attn[0:E, :, :].rearrange("p t d -> p (t d)")
        z = rows_sb[:, 0:TILES, 0:D]
        v_flat = v_all[:, :, :].rearrange("p t d -> p (t d)")
        q_f32, k_f32 = (st[:, :, :].rearrange("p s n -> p (s n)").bitcast(F32) for st in (q_st, k_st))
        early = [(ins_sb[:, :], ins), (w16[:, :], gamma_rmod), (eb_sb[:, :], expert_b), (beta_sb, beta_w),
                 (w_sb[:, :, :, :], attn_w), (b_sb[:, :, :], attn_b), (router[:, 0, :], gate_w)]
        early += [(row[:, l, :], b[l].partition_broadcast(P)) for row, b in ((bv_row, bv), (bo_row, bo)) for l in range(2)]
        late = [(router[:, 1, :], w_r), (b2_sb[:, :], b2), (br_row[:, :], b_r.partition_broadcast(P)), (ln_sb[:, :], ln_gb),
                (ew_sb[:, :], expert_w), (consts[:, :], shape_consts)]
        k.first_in = k.lasting_sem("first_in")
        k.stack_in = [k.lasting_sem(f"stack_in{s}") for s in range(4)]
        k.parts_stored = [[k.lasting_sem(f"parts_stored{b}_{s}") for s in range(4)] for b in range(BATCH)]
        early_in, late_in = k.lasting_sem("early_in"), k.lasting_sem("late_in")
        k.weights_in = (early_in, 16 * len(early))
        rows_in = [k.lasting_sem(f"rows_in{g}") for g in range(TILES // LN_GROUP)]

        def load(sp):
            for dst, src in early:
                sp.dma_start(dst, src).then_inc(early_in, 16)
            for dst, src in late:
                sp.dma_start(dst, src).then_inc(late_in, 16)
            sp.wait_ge(early_in, 16 * len(early))
            sp.wait_ge(late_in, 16 * len(late))

        start = mixture_constants(k, ins_sb[:, :], w16[:, :], eb_sb[:, :], beta_sb, banks, (early_in, 16 * len(early)))
        start["sync"] = load
        start["gpsimd"] = lambda pool: gather(pool, k, ids, table, h, ident, rows_in)
        for l in range(2):
            tag, k.layer = f"a{l}_", l
            qkv = project_qkv(k, tag + "p", xT, w_sb[:, l], b_sb[:, l], bv_row[:, l], parts_dram,
                              v_all[:, :, :].rearrange("p (b t) d -> p b t d", b=BH), banks, part_ring, rest_ring, load_stacks,
                              CHUNKS if l else CHUNKS * LN_GROUP // TILES)
            if l == 0:
                layer_norm(nc, k, tag + "n", h, y, banks, ident, xT, rows_in=rows_in, at_start=start, then=qkv)
            else:
                layer_norm(nc, k, tag + "n", h, y, banks, ident, xT)
                all_groups(nc, qkv)
            k.end_phase()
            attention(nc, k, tag, SCALES[l], parts_dram, q_st, k_st, v_all, v_st, probs, o_sb, attn, h,
                      bo_row[:, l], banks, ident, m_dram, load_stacks)
            k.end_phase()
            project_out(nc, k, tag + "o", attn, w_sb[:, l, 3, :], h, banks, ident, o_sb)
            k.end_phase()
            if l == 0:
                layer_norm(nc, k, "f0_n", h, y, banks, ident, xT, router=router[:, 0, :])
                k.end_phase()
                route(nc, k, "f0_r", k.gamma_router[:, E:2 * E], True, banks, weights, ident, wt,
                      blank_slots=(slots_dram, rows_sb))
                k.end_phase()
                mix_linear(nc, k, xT, ew_sb, weights, wt, k.offsets[:, :], h, banks, q_f32.rearrange("p (s e d) -> p s e d", e=PER, d=D),
                           k_f32.rearrange("p (s e d) -> p s e d", e=2, d=D))
                k.end_phase()
        layer_norm(nc, k, "f1_n", h, y, banks, ident)
        k.end_phase()
        layer_norm(nc, k, "f1_m", y, z, banks, ident, xT, gain=ln_sb[:, 0:1], bias=ln_sb[:, 1:2],
                   router=router[:, 1, :])
        k.end_phase()
        route(nc, k, "f1_r", br_row[:, :], False, banks, weights, ident, None)
        k.end_phase()
        W_ROW, R_ROW = experts.shape[1], ROWS // P * (D + 1)
        weight_ring = [flat[:, at:at + W_ROW] for flat in (v_flat, k_f32) for at in (0, W_ROW)]
        bufs = (weight_ring,
                v_flat[:, 2 * W_ROW:2 * W_ROW + 4 * R_ROW].rearrange("p (s f c) -> p s f c", s=4, c=D + 1),
                q_f32[:, 0:4 * ROWS].rearrange("p (s n) -> p s n", s=4),
                q_f32[:, 4 * ROWS:4 * ROWS + 2 * FC * ROWS].rearrange("p (s f n) -> p s f n", s=2, f=FC),
                q_f32[:, (4 + 2 * FC) * ROWS:(8 + 2 * FC) * ROWS].rearrange("p (s n) -> p s n", s=4),
                xT[:, :].rearrange("p (t d) -> p t d", d=D),
                probs[:, :, :, :].rearrange("p a b n -> p (a b n)").rearrange("p (t d) -> p t d", d=D),
                q_f32[:, 0:2 * FC * N].rearrange("p (s f n) -> p s f n", s=2, f=FC), xT[:, SENT * P:TILES * P])
        mix_mlp(nc, k, rows_sb, slots_dram, y_dram, experts, b2_sb[:, :], ln_sb[:, 0:1], ln_sb[:, 1:2], weights, wt, y, h, out, banks, ident, bufs)


def shape_consts(np):
    p = np.arange(P).reshape(P, 1)
    rows = lambda x: np.broadcast_to(x, (P, len(x)))
    parts = [p < np.arange(P), rows(ROWS * np.arange(COUNT_STEPS)), rows(np.arange(SORTED_TILES)), p,
             np.arange(BEST * TILES) * P + p, BEST * TOKENS + p * PER_PART + np.arange(PER_PART)]
    return np.concatenate([np.asarray(x, np.float32) for x in parts], axis=1)


def kernel(**inputs):
    import numpy as np
    import concourse.bacc as bacc
    from concourse.bass_utils import run_bass_kernel_spmd as run

    a = {name: np.asarray(x) for name, x in inputs.items()}
    qkv = a["L1_attn_qkv_w"].reshape(HEADS, 3, DH, D).transpose(1, 3, 0, 2).reshape(3, D, D)
    qkv_b = a["L1_attn_qkv_b"].reshape(HEADS, 3, DH).transpose(1, 0, 2).reshape(3, D)
    mats = [[a["L0_attn_Wq"], a["L0_attn_Wk"], a["L0_attn_Wv"], a["L0_attn_Wo"]],
            [qkv[0], qkv[1], qkv[2], a["L1_attn_out_w"].T]]
    arrays = {
        "ids": a["x"].reshape(TILES, P).T,
        "table": a["L0_tok_weight"],
        "attn_w": np.array(mats).transpose(2, 0, 1, 3),
        "attn_b": np.array([[a["L0_attn_bq"], a["L0_attn_bk"]], [qkv_b[0], qkv_b[1]]]).transpose(2, 0, 1),
        "bv": np.array([a["L0_attn_bv"], qkv_b[2]]),
        "bo": np.array([a["L0_attn_bo"], a["L1_attn_out_b"]]),
        "ins": a["L0_ffn_Ins_tk"][0],
        "gate_w": a["L0_ffn_gate_w"],
        "expert_w": a["L0_ffn_expert_w"].transpose(1, 0, 2).reshape(D, E * D),
        "expert_b": a["L0_ffn_expert_b"],
        "gamma_rmod": np.concatenate([a["L0_ffn_gamma_w"].T, a["L0_ffn_rmod_w"]], axis=1),
        "beta_w": a["L0_ffn_beta_w"].transpose(1, 0, 2),
        "ln_gb": np.array([a["L1_ffn_ln_g"], a["L1_ffn_ln_b"]]).T,
        "w_r": a["L1_ffn_w_r"].T,
        "b_r": a["L1_ffn_b_r"],
        "experts": np.concatenate([a["L1_ffn_W1"], a["L1_ffn_W2"].reshape(E, FC, P, D).transpose(0, 2, 1, 3).reshape(E, P, FF),
                                   a["L1_ffn_b1"].reshape(E, FC, P).transpose(0, 2, 1)], axis=2).reshape(E * P, 2 * FF + FC),
        "b2": a["L1_ffn_b2"],
        "shape_consts": shape_consts(np),
    }
    nc = bacc.Bacc("TRN2", target_bir_lowering=False, num_devices=1)
    feed, aps = {}, []
    for name, x in arrays.items():
        x = np.ascontiguousarray(x)
        feed[f"in_{name}"] = x
        aps.append(nc.dram_tensor(f"in_{name}", x.shape, mybir.dt.from_np(x.dtype), kind="ExternalInput").ap())
    out = nc.dram_tensor("out", (BATCH, SEQ, D), F32, kind="ExternalOutput").ap()
    program(nc, *aps, out)
    return run(nc, [feed], core_ids=[0]).results[0]["out"]
```
